# Optimizing a Trainium2 kernel written in Bass

```python
import numpy as np
import jax
import jax.numpy as jnp

def _softmax(x, axis=-1):
    return jax.nn.softmax(x, axis=axis)

def _gelu(x):
    return jax.nn.gelu(x, approximate=True)

def _silu(x):
    return jax.nn.silu(x)

def _sigmoid(x):
    return jax.nn.sigmoid(x)

def _layernorm(x, axis=-1, eps=1e-05):
    m = jnp.mean(x, axis=axis, keepdims=True)
    v = jnp.var(x, axis=axis, keepdims=True)
    return (x - m) / jnp.sqrt(v + eps)

def _scatter_add(tgt, idx, src, axis=0):
    return tgt.at[idx].add(src)

def _segment_sum(src, seg, n):
    return jax.ops.segment_sum(src, seg, n)
kernel_name = 'mk_adaln_d2_jaxref_r8_a22627'

def setup_inputs(seed: int=0):
    np.random.seed(seed)
    _w = jnp.asarray

    def _L0_attn_setup():
        import jax, jax.numpy as jnp
        import numpy as np
        import math
        CTX_LEN = 96
        N_EMBD = 128

        def _depthwise_causal_conv(z, w, T, C):
            return jax.lax.conv_general_dilated(z, w, window_strides=(1,), padding=[(T - 1, 0)], feature_group_count=C, dimension_numbers=('NCH', 'OIH', 'NCH'))
        key = jax.random.key(seed)
        ks = jax.random.split(key, 8)
        B, T, C = (8, CTX_LEN, N_EMBD)
        x = jax.random.normal(ks[0], (B, T, C), dtype=jnp.float32)
        time_decay = jax.random.normal(ks[1], (C, 1), dtype=jnp.float32) * 0.1
        time_first = jnp.full((C, 1), math.log(0.3), dtype=jnp.float32)
        time_mix = jax.random.uniform(ks[2], (1, 1, C), dtype=jnp.float32)
        s = 0.02
        Wk = jax.random.normal(ks[3], (C, C), dtype=jnp.float32) * s
        Wv = jax.random.normal(ks[4], (C, C), dtype=jnp.float32) * s
        Wr = jax.random.normal(ks[5], (C, C), dtype=jnp.float32) * s
        Wo = jax.random.normal(ks[6], (C, C), dtype=jnp.float32) * s
        return {'x': x, 'time_decay': time_decay, 'time_first': time_first, 'time_mix': time_mix, 'Wk': Wk, 'Wv': Wv, 'Wr': Wr, 'Wo': Wo}
    _L0_attn_in = _L0_attn_setup()

    def _L0_ffn_setup():
        import jax, jax.numpy as jnp
        import numpy as np
        D_EMBED = 128
        D_FF = 512
        N_EXPERTS = 8
        TOP_K = 2
        N_SHARED = 1
        B, S = (2, 256)
        key = jax.random.key(seed)
        ks = jax.random.split(key, 12)
        sd = 1.0 / np.sqrt(D_EMBED)
        sf = 1.0 / np.sqrt(D_FF)
        return {'x': jax.random.normal(ks[0], (B, S, D_EMBED), dtype=jnp.float32), 'Wg': jax.random.normal(ks[1], (D_EMBED, N_EXPERTS), dtype=jnp.float32) * sd, 'bg': jnp.zeros((N_EXPERTS,), dtype=jnp.float32), 'W1': jax.random.normal(ks[2], (N_EXPERTS, D_EMBED, D_FF), dtype=jnp.float32) * sd, 'b1': jnp.zeros((N_EXPERTS, D_FF), dtype=jnp.float32), 'W2': jax.random.normal(ks[3], (N_EXPERTS, D_FF, D_EMBED), dtype=jnp.float32) * sf, 'b2': jnp.zeros((N_EXPERTS, D_EMBED), dtype=jnp.float32), 'Ws1': jax.random.normal(ks[4], (N_SHARED, D_EMBED, D_FF), dtype=jnp.float32) * sd, 'bs1': jnp.zeros((N_SHARED, D_FF), dtype=jnp.float32), 'Ws2': jax.random.normal(ks[5], (N_SHARED, D_FF, D_EMBED), dtype=jnp.float32) * sf, 'bs2': jnp.zeros((N_SHARED, D_EMBED), dtype=jnp.float32)}
    _L0_ffn_in = _L0_ffn_setup()
    _L0_c = _w((lambda *s: np.random.randn(*s).astype(np.float32) * 0.05)(1, 128))
    _L0_wmod = _w((lambda *s: np.random.randn(*s).astype(np.float32) * 0.05)(128, 6 * 128) * 128 ** (-0.5))

    def _L1_attn_setup():
        import jax, jax.numpy as jnp
        import numpy as np
        B, S, D, H = (2, 256, 128, 16)
        DK = D // H
        key = jax.random.key(seed)
        ks = jax.random.split(key, 7)
        s = 1.0 / np.sqrt(D)
        return {'x': jax.random.normal(ks[0], (B, S, D), dtype=jnp.float32), 'Wq': jax.random.uniform(ks[1], (D, D), jnp.float32, -s, s), 'bq': jax.random.uniform(ks[2], (D,), jnp.float32, -s, s), 'Wk': jax.random.uniform(ks[3], (D, D), jnp.float32, -s, s), 'bk': jax.random.uniform(ks[4], (D,), jnp.float32, -s, s), 'Wv': jax.random.uniform(ks[5], (D, D), jnp.float32, -s, s), 'bv': jax.random.uniform(ks[6], (D,), jnp.float32, -s, s)}
    _L1_attn_in = _L1_attn_setup()

    def _L1_ffn_setup():
        import jax, jax.numpy as jnp
        import numpy as np
        E = 8
        K = 2
        CF = 1.25
        key = jax.random.key(seed)
        kx, kr, kg, ku, kd = jax.random.split(key, 5)
        D, F = (128, 512)
        x = jax.random.normal(kx, (4, 256, D), dtype=jnp.float32)
        router_w = 0.02 * jax.random.normal(kr, (E, D), dtype=jnp.float32)
        wg = jax.random.normal(kg, (E, D, F), dtype=jnp.float32) / np.sqrt(D)
        wu = jax.random.normal(ku, (E, D, F), dtype=jnp.float32) / np.sqrt(D)
        wd = jax.random.normal(kd, (E, F, D), dtype=jnp.float32) / np.sqrt(F)
        return {'x': x, 'router_w': router_w, 'wg': wg, 'wu': wu, 'wd': wd}
    _L1_ffn_in = _L1_ffn_setup()
    _L1_c = _w((lambda *s: np.random.randn(*s).astype(np.float32) * 0.05)(1, 128))
    _L1_wmod = _w((lambda *s: np.random.randn(*s).astype(np.float32) * 0.05)(128, 6 * 128) * 128 ** (-0.5))
    _d = {'L0_attn_x': _L0_attn_in['x'], 'L0_attn_time_decay': _L0_attn_in['time_decay'], 'L0_attn_time_first': _L0_attn_in['time_first'], 'L0_attn_time_mix': _L0_attn_in['time_mix'], 'L0_attn_Wk': _L0_attn_in['Wk'], 'L0_attn_Wv': _L0_attn_in['Wv'], 'L0_attn_Wr': _L0_attn_in['Wr'], 'L0_attn_Wo': _L0_attn_in['Wo'], 'L0_ffn_Wg': _L0_ffn_in['Wg'], 'L0_ffn_bg': _L0_ffn_in['bg'], 'L0_ffn_W1': _L0_ffn_in['W1'], 'L0_ffn_b1': _L0_ffn_in['b1'], 'L0_ffn_W2': _L0_ffn_in['W2'], 'L0_ffn_b2': _L0_ffn_in['b2'], 'L0_ffn_Ws1': _L0_ffn_in['Ws1'], 'L0_ffn_bs1': _L0_ffn_in['bs1'], 'L0_ffn_Ws2': _L0_ffn_in['Ws2'], 'L0_ffn_bs2': _L0_ffn_in['bs2'], 'L0_c': _L0_c, 'L0_wmod': _L0_wmod, 'L1_attn_Wq': _L1_attn_in['Wq'], 'L1_attn_bq': _L1_attn_in['bq'], 'L1_attn_Wk': _L1_attn_in['Wk'], 'L1_attn_bk': _L1_attn_in['bk'], 'L1_attn_Wv': _L1_attn_in['Wv'], 'L1_attn_bv': _L1_attn_in['bv'], 'L1_ffn_router_w': _L1_ffn_in['router_w'], 'L1_ffn_wg': _L1_ffn_in['wg'], 'L1_ffn_wu': _L1_ffn_in['wu'], 'L1_ffn_wd': _L1_ffn_in['wd'], 'L1_c': _L1_c, 'L1_wmod': _L1_wmod}
    _x0 = _d['L0_attn_x']
    _d['L0_attn_x'] = jax.random.normal(jax.random.fold_in(jax.random.key(seed), 1), (1, 2048, 128), dtype=_x0.dtype)
    del _x0
    return _d

def reference(L0_attn_x, L0_attn_time_decay, L0_attn_time_first, L0_attn_time_mix, L0_attn_Wk, L0_attn_Wv, L0_attn_Wr, L0_attn_Wo, L0_ffn_Wg, L0_ffn_bg, L0_ffn_W1, L0_ffn_b1, L0_ffn_W2, L0_ffn_b2, L0_ffn_Ws1, L0_ffn_bs1, L0_ffn_Ws2, L0_ffn_bs2, L0_c, L0_wmod, L1_attn_Wq, L1_attn_bq, L1_attn_Wk, L1_attn_bk, L1_attn_Wv, L1_attn_bv, L1_ffn_router_w, L1_ffn_wg, L1_ffn_wu, L1_ffn_wd, L1_c, L1_wmod):

    def _L0_attn_ref(x, time_decay, time_first, time_mix, Wk, Wv, Wr, Wo):
        import jax, jax.numpy as jnp
        import numpy as np
        import math
        CTX_LEN = 96
        N_EMBD = 128

        def _depthwise_causal_conv(z, w, T, C):
            return jax.lax.conv_general_dilated(z, w, window_strides=(1,), padding=[(T - 1, 0)], feature_group_count=C, dimension_numbers=('NCH', 'OIH', 'NCH'))
        B, T, C = x.shape
        xs = jnp.pad(x, ((0, 0), (1, 0), (0, 0)))[:, :-1]
        xm = x * time_mix + xs * (1.0 - time_mix)
        k = jnp.einsum('btc,dc->bdt', xm, Wk)
        v = jnp.einsum('btc,dc->bdt', xm, Wv)
        r = jnp.einsum('btc,dc->btd', xm, Wr)
        k = jnp.exp(jnp.minimum(k, 60.0))
        kv = k * v
        time_curve = (jnp.arange(T - 1, dtype=jnp.float32) - (T - 2))[None, :]
        time_w = jnp.concatenate([jnp.exp(time_decay) * time_curve, time_first], axis=-1)
        w = jnp.exp(time_w)[:, None, :]
        wkv = _depthwise_causal_conv(kv, w, T, C)
        wk = _depthwise_causal_conv(k, w, T, C) + 1e-09
        rwkv = jax.nn.sigmoid(r) * jnp.swapaxes(wkv / wk, 1, 2)
        return jnp.einsum('btc,dc->btd', rwkv, Wo)

    def _L0_ffn_ref(x, Wg, bg, W1, b1, W2, b2, Ws1, bs1, Ws2, bs2):
        import jax, jax.numpy as jnp
        import numpy as np
        D_EMBED = 128
        D_FF = 512
        N_EXPERTS = 8
        TOP_K = 2
        N_SHARED = 1
        B, S = (2, 256)
        Bsz, Ssz, D = x.shape
        T = Bsz * Ssz
        xf = x.reshape(T, D)
        logits = xf @ Wg + bg
        probs = jax.nn.softmax(logits, axis=-1)
        scores, indices = jax.lax.top_k(probs, TOP_K)
        E = W1.shape[0]
        gate = jnp.zeros((T, E), dtype=x.dtype).at[jnp.arange(T)[:, None], indices].add(scores)
        y = jnp.zeros_like(xf)
        for e in range(E):
            h = jax.nn.gelu(xf @ W1[e] + b1[e], approximate=False)
            out = h @ W2[e] + b2[e]
            y = y + out * gate[:, e:e + 1]
        ns = Ws1.shape[0]
        shared = jnp.zeros_like(xf)
        for s in range(ns):
            shared = shared + (jax.nn.gelu(xf @ Ws1[s] + bs1[s], approximate=False) @ Ws2[s] + bs2[s])
        y = y + shared / ns
        return y.reshape(Bsz, Ssz, D)

    def _L1_attn_ref(x, Wq, bq, Wk, bk, Wv, bv):
        import jax, jax.numpy as jnp
        import numpy as np
        B, S, D, H = (2, 256, 128, 16)
        DK = D // H
        b, s, d = x.shape

        def proj(W, bias):
            return (jnp.einsum('bsd,ed->bse', x, W) + bias).reshape(b, s, H, DK).transpose(0, 2, 1, 3)
        q, k, v = (proj(Wq, bq), proj(Wk, bk), proj(Wv, bv))
        scores = jnp.einsum('bhqd,bhkd->bhqk', q, k) / np.sqrt(DK).astype(np.float32)
        causal = jnp.tril(jnp.ones((s, s), dtype=bool))
        scores = jnp.where(causal[None, None], scores, jnp.float32(-1000000000.0))
        attn = jax.nn.softmax(scores, axis=-1)
        out = jnp.einsum('bhqk,bhkd->bhqd', attn, v)
        return out.transpose(0, 2, 1, 3).reshape(b, s, d)

    def _L1_ffn_ref(x, router_w, wg, wu, wd):
        import jax, jax.numpy as jnp
        import numpy as np
        E = 8
        K = 2
        CF = 1.25
        B, L, D = x.shape
        xf = x.reshape(-1, D)
        N = xf.shape[0]
        capacity = max(1, int(CF * N / E))
        logits = xf @ router_w.T
        probs = jax.nn.softmax(logits, axis=-1)
        topw, topi = jax.lax.top_k(probs, K)
        topw = topw / (topw.sum(-1, keepdims=True) + 1e-06)
        fe = topi.reshape(-1)
        fw = topw.reshape(-1)
        ft = jnp.repeat(jnp.arange(N), K)
        order = jnp.lexsort((-fw, fe))
        se, sw, st = (fe[order], fw[order], ft[order])
        counts = jax.ops.segment_sum(jnp.ones_like(se), se, num_segments=E)
        starts = jnp.cumsum(counts) - counts
        rank = jnp.arange(N * K) - starts[se]
        keep = rank < capacity
        pos = jnp.where(keep, rank, capacity)
        disp = jnp.zeros((E, capacity + 1, D), x.dtype).at[se, pos].set(xf[st])
        disp = disp[:, :capacity]
        g = jnp.einsum('ecd,edf->ecf', disp, wg)
        u = jnp.einsum('ecd,edf->ecf', disp, wu)
        eo = jnp.einsum('ecf,efd->ecd', jax.nn.silu(g) * u, wd)
        gathered = eo[se, jnp.minimum(pos, capacity - 1)]
        contrib = gathered * (sw * keep.astype(x.dtype))[:, None]
        out = jnp.zeros_like(xf).at[st].add(contrib)
        return out.reshape(B, L, D)
    x = L0_attn_x
    mod = (_silu(L0_c) @ L0_wmod).reshape(L0_c.shape[0], 6, 1, -1)
    sa, ca, ga, sb, cb, gb = (mod[:, 0], mod[:, 1], mod[:, 2], mod[:, 3], mod[:, 4], mod[:, 5])
    ga = (2 * (ga >= 0) - 1) * jnp.maximum(jnp.abs(ga), 0.25)
    gb = (2 * (gb >= 0) - 1) * jnp.maximum(jnp.abs(gb), 0.25)
    h = _layernorm(x, axis=-1) * (1 + ca) + sa
    x = x + ga * _L0_attn_ref(h, L0_attn_time_decay, L0_attn_time_first, L0_attn_time_mix, L0_attn_Wk, L0_attn_Wv, L0_attn_Wr, L0_attn_Wo)
    h = _layernorm(x, axis=-1) * (1 + cb) + sb
    x = x + gb * _L0_ffn_ref(h, L0_ffn_Wg, L0_ffn_bg, L0_ffn_W1, L0_ffn_b1, L0_ffn_W2, L0_ffn_b2, L0_ffn_Ws1, L0_ffn_bs1, L0_ffn_Ws2, L0_ffn_bs2)
    mod = (_silu(L1_c) @ L1_wmod).reshape(L1_c.shape[0], 6, 1, -1)
    sa, ca, ga, sb, cb, gb = (mod[:, 0], mod[:, 1], mod[:, 2], mod[:, 3], mod[:, 4], mod[:, 5])
    ga = (2 * (ga >= 0) - 1) * jnp.maximum(jnp.abs(ga), 0.25)
    gb = (2 * (gb >= 0) - 1) * jnp.maximum(jnp.abs(gb), 0.25)
    h = _layernorm(x, axis=-1) * (1 + ca) + sa
    x = x + ga * _L1_attn_ref(h, L1_attn_Wq, L1_attn_bq, L1_attn_Wk, L1_attn_bk, L1_attn_Wv, L1_attn_bv)
    h = _layernorm(x, axis=-1) * (1 + cb) + sb
    x = x + gb * _L1_ffn_ref(h, L1_ffn_router_w, L1_ffn_wg, L1_ffn_wu, L1_ffn_wd)
    return x

_drawn_inputs = setup_inputs


def setup_inputs(seed=0):
    import zlib

    import numpy as np

    out = dict(_drawn_inputs(seed))
    spreads = {'L0_attn_time_first': (-1.2039728164672852, 0.6),
     'L0_ffn_bg': (0.0, 2.0),
     'L0_ffn_b1': (0.0, 2.0),
     'L0_ffn_b2': (0.0, 2.0),
     'L0_ffn_bs1': (0.0, 1.52),
     'L0_ffn_bs2': (0.0, 1.034)}
    factors = {'L0_attn_time_decay': 8.0,
     'L0_attn_time_mix': 8.0,
     'L0_attn_Wk': 8.0,
     'L0_attn_Wv': 8.0,
     'L0_attn_Wr': 8.0,
     'L0_attn_Wo': 8.0,
     'L1_attn_Wq': 6.384,
     'L1_attn_bq': 8.0,
     'L1_attn_Wk': 7.167,
     'L1_attn_bk': 64.0,
     'L1_attn_Wv': 3.282,
     'L1_attn_bv': 14.387}
    for name, (base, spread) in spreads.items():
        noise = np.random.default_rng([zlib.crc32(name.encode()), seed]).standard_normal(out[name].shape)
        drawn = base * np.exp(spread * noise) if base else spread * noise
        out[name] = jnp.asarray(drawn.astype(out[name].dtype))
    for name, factor in factors.items():
        out[name] = (out[name] * factor).astype(out[name].dtype)
    return out
```

```python
from contextlib import ExitStack, contextmanager

import concourse.bass as bass
from concourse import mybir

F32 = mybir.dt.float32
BF16 = mybir.dt.bfloat16
I32 = mybir.dt.int32
ALU = mybir.AluOpType
ACT = mybir.ActivationFunctionType
AX = mybir.AxisListType

D = 128
NT = 2048
TB = 512
NB = NT // TB
NTILE = NT // 128
E = 8
F = 512
FC = F // 128
H = 16
DK = D // H
CAP = int(1.25 * NT / E)
LN_EPS = 1e-5
BIG = 3.0e38
STAGE = 6
NBITS = 30

TD, TF, TM, C0, C1, BQ, BK = range(7)
SA, CA, GA, SB, CB, GB = range(6)


class Shared:
    pass


def blk(b, n=TB):
    return slice(b * n, (b + 1) * n)



def ln_tensor(pe, S, k, mean_ps, var_ps):
    def mean(b):
        pe.wait_ge(S.x_ready, 4 * k + b + 1)
        if b >= 2:
            pe.wait_ge(S.ln_centered, 4 * k + b - 1)
        pe.matmul(mean_ps[b % 2][:, :], S.mean_w[:, :], S.xT[:, blk(b)], start=True, stop=True).then_inc(S.ln_mean, 1)

    mean(0)
    for b in range(NB):
        if b + 1 < NB:
            mean(b + 1)
        pe.wait_ge(S.ln_squared, 4 * k + b + 1)
        pe.matmul(var_ps[b % 2][:, :], S.mean_w[:, :], S.sq[:, b % 2, :], start=True, stop=True).then_inc(S.ln_var, 1)


def ln_scalar(act, S, k, var_ps):
    for b in range(NB):
        act.wait_ge(S.ln_centered, 4 * k + b + 1)
        if b >= 2:
            act.wait_ge(S.ln_var, 4 * k + b - 1)
        act.activation(S.sq[:, b % 2, :], S.xc[:, blk(b)], ACT.Square).then_inc(S.ln_squared, 1)
        if b >= 1:
            ln_spread(act, S, k, var_ps, b - 1)
    ln_spread(act, S, k, var_ps, NB - 1)


def ln_spread(act, S, k, var_ps, b):
    act.wait_ge(S.ln_var, 4 * k + b + 1)
    act.activation(S.sd[:, blk(b)], var_ps[b % 2][:, :], ACT.Sqrt, bias=S.eps_col[:, :]).then_inc(S.ln_sd, 1)


def ln_vector(dve, S, link, k, mean_ps, scale, shift):
    def center(b):
        dve.wait_ge(S.ln_mean, 4 * k + b + 1)
        dve.tensor_tensor(S.xc[:, blk(b)], S.xT[:, blk(b)], mean_ps[b % 2][:, :], ALU.subtract).then_inc(S.ln_centered, 1)

    center(0)
    center(1)
    for b in range(NB):
        dve.wait_ge(S.ln_sd, 4 * k + b + 1)
        link(dve.reciprocal(S.sd[:, blk(b)], S.sd[:, blk(b)]))
        link(dve.scalar_tensor_tensor(S.sd[:, blk(b)], S.xc[:, blk(b)], scale, S.sd[:, blk(b)], ALU.mult, ALU.mult))
        dve.tensor_scalar(S.hT[:, 1 + b * TB:1 + (b + 1) * TB], S.sd[:, blk(b)], shift, None, ALU.add).then_inc(S.h_ready, 1)
        if b + 2 < NB:
            center(b + 2)


def h_block(S, b):
    return S.hT[:, 1 + b * TB:1 + (b + 1) * TB]


def h_tile(S, t):
    return S.hT[:, 1 + t * 128:1 + (t + 1) * 128]


def make_link(eng, sem):
    done = [0]

    def link(ins):
        done[0] += 1
        ins.then_inc(sem, 1)
        eng.wait_ge(sem, done[0])

    return link



def stage_mix(nc, S, A):
    with ExitStack() as ctx:
        sb = lambda n, s, d=F32: ctx.enter_context(nc.sbuf_tensor(n, s, d))
        ps = lambda n: ctx.enter_context(nc.psum_tensor(n, [128, TB], F32))
        wmod = sb("wmod", [128, 2, 6 * D])
        wmix = sb("wmix", [128, 4, D])
        small = sb("small", [128, 16])
        kf = sb("kf", [128, TB])
        k_exp = sb("k_exp", [128, 2, TB])
        r_exp = sb("r_exp", [128, 2, TB])
        kv = sb("kv", [128, TB])
        xm = sb("xm", [128, 2, TB])
        mix_t = sb("mix_t", [128, TB])
        sum_kv = sb("sum_kv", [128, NT + 1])
        sum_k = sb("sum_k", [128, NT + 1])
        decay_row = sb("decay_row", [128, TB])
        wkv = sb("wkv", [128, TB])
        wk = sb("wk", [128, TB])
        rwkv = sb("rwkv", [128, 2, TB])
        mean_ps = [ps("mean0"), ps("mean1")]
        var_ps = [ps("var0"), ps("var1")]
        k_ps, v_ps, r_ps, o_ps = ps("k_ps"), ps("v_ps"), ps("r_ps"), ps("o_ps")
        decay, first, one_m_tm = small[:, 0:1], small[:, 1:2], small[:, 2:3]
        silu_c, c_exp = small[:, 4:6], small[:, 6:8]

        sem = S.sem
        w_in, c_exped, silu_done, mod_mm = sem("w_in"), sem("c_exped"), sem("silu_done"), sem("mod_mm")
        coef, xm_ready, kvr_ready, kmin_done = sem("coef"), sem("xm_ready"), sem("kvr_ready"), sem("kmin_done")
        kr_exped, kvr_read, rwkv_ready, o_ready = sem("kr_exped"), sem("kvr_read"), sem("rwkv_ready"), sem("o_ready")
        tdone = sem("tdone")
        block = ctx.enter_context(nc.Block())

        @block.sync
        def _(sp):
            sp.dma_start(S.cols[:, :], A["cols"]).then_inc(S.cols_in, 16)
            for b in range(NB):
                sp.dma_start(S.xT[:, blk(b)], A["xT"][:, blk(b)]).then_inc(S.x_in[b], 16)
            sp.dma_start(wmod[:, :, :], A["wmod"]).then_inc(w_in, 16)
            sp.dma_start(wmix[:, :, :], A["wmix"]).then_inc(w_in, 16)
            sp.dma_start(S.consts[:, :], A["consts"]).then_inc(S.const_in, 16)
            sp.dma_start(S.bits[:, :], A["bits"]).then_inc(S.const_in, 16)

        @block.tensor
        def _(pe):
            pe.wait_ge(w_in, 32)
            pe.wait_ge(silu_done, 1)
            for layer in range(2):
                for j in range(6):
                    last = pe.matmul(o_ps[:, 6 * layer + j:6 * layer + j + 1], wmod[:, layer, blk(j, 128)],
                                     silu_c[:, layer:layer + 1], start=True, stop=True)
            last.then_inc(mod_mm, 1)
            ln_tensor(pe, S, 0, mean_ps, var_ps)
            for b in range(NB + 1):
                if b < NB:
                    pe.wait_ge(xm_ready, b + 1)
                    if b >= 1:
                        pe.wait_ge(kvr_read, 3 * b)
                    for j, bank in enumerate((k_ps, v_ps, r_ps)):
                        pe.matmul(bank[:, :], wmix[:, j, :], xm[:, b % 2, :], start=True, stop=True).then_inc(kvr_ready, 1)
                if b >= 1:
                    pe.wait_ge(rwkv_ready, b)
                    if b >= 2:
                        pe.wait_ge(S.x_ready, NB + b - 1)
                    pe.matmul(o_ps[:, :], wmix[:, 3, :], rwkv[:, (b - 1) % 2, :], start=True, stop=True).then_inc(o_ready, 1)

        @block.scalar
        def _(act):
            act.wait_ge(S.cols_in, 16)
            act.activation(c_exp, S.cols[:, C0:C1 + 1], ACT.Exp, scale=-1.0).then_inc(c_exped, 1)
            act.activation(first, S.cols[:, TF:TF + 1], ACT.Exp).then_inc(coef, 1)
            act.activation(decay, S.cols[:, TD:TD + 1], ACT.Exp).then_inc(coef, 1)
            act.wait_ge(coef, 2)
            act.activation(decay, decay, ACT.Exp, scale=-1.0).then_inc(coef, 1)
            act.wait_ge(S.eps_set, 1)
            ln_scalar(act, S, 0, var_ps)
            for b in range(NB):
                if b >= 2:
                    act.wait_ge(rwkv_ready, b - 1)
                act.wait_ge(kmin_done, b + 1)
                act.activation(k_exp[:, b % 2, :], kf[:, :], ACT.Exp).then_inc(kr_exped, 1)
                act.wait_ge(kvr_ready, 3 * b + 3)
                act.activation(r_exp[:, b % 2, :], r_ps[:, :], ACT.Exp, scale=-1.0).then_inc(kvr_read, 1)

        @block.vector
        def _(dve):
            link = make_link(dve, tdone)
            link(dve.memset(S.mean_w[:, :], 1.0 / D))
            dve.memset(S.eps_col[:, :], LN_EPS).then_inc(S.eps_set, 1)
            link(dve.memset(S.hT[:, 0:1], 0.0))
            link(dve.memset(sum_kv[:, 0:1], 0.0))
            link(dve.memset(sum_k[:, 0:1], 0.0))
            link(dve.memset(decay_row[:, :], 0.0))
            for b in range(NB):
                dve.wait_ge(S.x_in[b], 16)
            dve.wait_ge(c_exped, 1)
            link(dve.tensor_scalar(c_exp, c_exp, 1.0, None, ALU.add))
            link(dve.reciprocal(c_exp, c_exp))
            dve.tensor_tensor(silu_c, S.cols[:, C0:C1 + 1], c_exp, ALU.mult).then_inc(silu_done, 1)
            dve.tensor_scalar(one_m_tm, S.cols[:, TM:TM + 1], -1.0, 1.0, ALU.mult, ALU.add).then_inc(S.x_ready, NB)
            dve.wait_ge(S.x_ready, NB)
            dve.wait_ge(coef, 3)
            link(dve.tensor_scalar(decay_row[:, :], decay_row[:, :], decay, None, ALU.add))
            dve.wait_ge(mod_mm, 1)
            link(dve.tensor_copy(S.mod[:, :], o_ps[:, 0:12]))
            mods = S.mod[:, :].rearrange("p (l m) -> p l m", l=2)
            for c in (CA, CB):
                link(dve.tensor_scalar(mods[:, :, c], mods[:, :, c], 1.0, None, ALU.add))
            for g in (GA, GB):
                sign, size = small[:, 8:10], small[:, 10:12]
                link(dve.tensor_scalar(sign, mods[:, :, g], 0.0, 2.0, ALU.is_ge, ALU.mult))
                link(dve.tensor_scalar(sign, sign, -1.0, None, ALU.add))
                link(dve.scalar_tensor_tensor(size, mods[:, :, g], -1.0, mods[:, :, g], ALU.mult, ALU.max))
                link(dve.tensor_scalar(size, size, 0.25, None, ALU.max))
                link(dve.tensor_tensor(mods[:, :, g], sign, size, ALU.mult))
            ln_vector(dve, S, link, 0, mean_ps, S.mod[:, CA:CA + 1], S.mod[:, SA:SA + 1])
            dve.wait_ge(S.h_ready, NB)

            def add_to_x(b):
                dve.wait_ge(o_ready, b + 1)
                dve.scalar_tensor_tensor(S.xT[:, blk(b)], o_ps[:, :], S.mod[:, GA:GA + 1], S.xT[:, blk(b)],
                                         ALU.mult, ALU.add).then_inc(S.x_ready, 1)

            for b in range(NB):
                link(dve.tensor_scalar(mix_t[:, :], S.hT[:, blk(b)], one_m_tm, None, ALU.mult))
                if b >= 2:
                    dve.wait_ge(kvr_ready, 3 * b - 3)
                dve.scalar_tensor_tensor(xm[:, b % 2, :], h_block(S, b), S.cols[:, TM:TM + 1], mix_t[:, :],
                                         ALU.mult, ALU.add).then_inc(xm_ready, 1)
                if b >= 1:
                    add_to_x(b - 1)
                dve.wait_ge(kvr_ready, 3 * b + 1)
                dve.tensor_scalar(kf[:, :], k_ps[:, :], 60.0, None, ALU.min).then_inc(kmin_done, 1)
                dve.wait_ge(kr_exped, b + 1)
                dve.wait_ge(kvr_ready, 3 * b + 2)
                ke = k_exp[:, b % 2, :]
                dve.tensor_tensor(kv[:, :], ke, v_ps[:, :], ALU.mult).then_inc(kvr_read, 2)
                dve.wait_ge(kvr_read, 3 * b + 3)
                new = slice(1 + b * TB, 1 + (b + 1) * TB)
                old = slice(b * TB, (b + 1) * TB)
                link(dve.tensor_tensor_scan(sum_k[:, new], decay_row[:, :], ke, sum_k[:, b * TB:b * TB + 1],
                                            ALU.mult, ALU.add))
                link(dve.tensor_tensor_scan(sum_kv[:, new], decay_row[:, :], kv[:, :], sum_kv[:, b * TB:b * TB + 1],
                                            ALU.mult, ALU.add))
                link(dve.scalar_tensor_tensor(wk[:, :], ke, first, sum_k[:, old], ALU.mult, ALU.add))
                link(dve.scalar_tensor_tensor(wkv[:, :], kv[:, :], first, sum_kv[:, old], ALU.mult, ALU.add))
                link(dve.tensor_scalar(wk[:, :], wk[:, :], 1e-9, None, ALU.add))
                link(dve.scalar_tensor_tensor(wk[:, :], r_exp[:, b % 2, :], 1.0, wk[:, :], ALU.add, ALU.mult))
                link(dve.reciprocal(wk[:, :], wk[:, :]))
                if b >= 2:
                    dve.wait_ge(o_ready, b - 1)
                dve.tensor_tensor(rwkv[:, b % 2, :], wkv[:, :], wk[:, :], ALU.mult).then_inc(rwkv_ready, 1)
            add_to_x(NB - 1)
            dve.wait_ge(S.x_ready, 2 * NB)



def router_tensor(pe, S, logits_ps, router_w, h_done, done):
    for t in range(NTILE):
        pe.wait_ge(S.h_ready, h_done + t // (NTILE // NB) + 1)
        last = pe.matmul(logits_ps[:, blk(t, E)], h_tile(S, t), router_w, start=True, stop=True)
    last.then_inc(done, 1)


def top2_vector(dve, S, link, R, to_exp, exped):
    wide = lambda a: a.unsqueeze(2).to_broadcast([128, NTILE, E])
    rev = S.rev.unsqueeze(1).to_broadcast([128, NTILE, E])
    link(dve.tensor_reduce(R.m[:, :], R.p[:, :, :], AX.X, ALU.max))
    dve.tensor_tensor(R.p[:, :, :], R.p[:, :, :], wide(R.m[:, :]), ALU.subtract).then_inc(to_exp, 1)
    dve.wait_ge(exped, 1)
    link(dve.tensor_reduce(R.m[:, :], R.p[:, :, :], AX.X, ALU.add))
    link(dve.reciprocal(R.m[:, :], R.m[:, :]))
    link(dve.tensor_tensor(R.p[:, :, :], R.p[:, :, :], wide(R.m[:, :]), ALU.mult))

    def pick(src, top, hot):
        link(dve.tensor_reduce(top, src, AX.X, ALU.max))
        link(dve.tensor_tensor(hot, src, wide(top), ALU.is_equal))
        link(dve.tensor_tensor(hot, hot, rev, ALU.mult))
        link(dve.tensor_reduce(R.m[:, :], hot, AX.X, ALU.max))
        link(dve.tensor_tensor(hot, hot, wide(R.m[:, :]), ALU.is_equal))

    pick(R.p[:, :, :], R.top1[:, :], R.sel[:, :, :])
    link(dve.scalar_tensor_tensor(R.rest[:, :, :], R.sel[:, :, :], -2.0, R.p[:, :, :], ALU.mult, ALU.add))
    pick(R.rest[:, :, :], R.top2[:, :], R.hot[:, :, :])
    link(dve.tensor_tensor(R.sel[:, :, :], R.sel[:, :, :], R.hot[:, :, :], ALU.add))


class Routing:
    def __init__(self, sb, k):
        self.p = sb(f"rt{k}_p", [128, NTILE, E])
        self.sel = sb(f"rt{k}_sel", [128, NTILE, E])
        self.hot = sb(f"rt{k}_hot", [128, NTILE, E])
        self.rest = sb(f"rt{k}_rest", [128, NTILE, E])
        self.gate = sb(f"rt{k}_gate", [128, E, NTILE])
        self.m = sb(f"rt{k}_m", [128, NTILE])
        self.top1 = sb(f"rt{k}_top1", [128, NTILE])
        self.top2 = sb(f"rt{k}_top2", [128, NTILE])



def stage_gelu_moe(nc, S, A):
    NE = E + 1
    gates_d = A["gates0"]
    with ExitStack() as ctx:
        sb = lambda n, s, d=F32: ctx.enter_context(nc.sbuf_tensor(n, s, d))
        ps = lambda n: ctx.enter_context(nc.psum_tensor(n, [128, TB], F32))
        R = Routing(sb, 0)
        wg = sb("wg0", [128, E])
        bgB = sb("bgB", [128, E])
        gate_rows = sb("gate_rows", [128, 128])
        ones_rows = sb("ones_rows", [NTILE, 128])
        gT = sb("gT", [NE, NT])
        b2 = sb("b2", [NE, D])
        w1 = [sb(f"w1_{p}", [128, F]) for p in range(2)]
        w2 = [sb(f"w2_{p}", [128, FC, D]) for p in range(2)]
        b1 = [sb(f"b1_{p}", [128, FC]) for p in range(2)]
        gB = [sb(f"gB_{p}", [128, NT]) for p in range(2)]
        hid = sb("hid", [128, 4, TB])
        gated = sb("gated", [128, 2 * FC, TB])
        y_ps = [ps(f"y{b}") for b in range(NB)]
        hid_ps = [ps(f"hid{n}") for n in range(4)]
        mean_ps, var_ps = hid_ps[0:2], hid_ps[2:4]
        logits_ps = y_ps[0][:, 0:NTILE * E]
        gate_ps = y_ps[1][:, 0:128]

        sem = S.sem
        rw_in, logits_done, to_exp, exped = sem("rw_in"), sem("logits0"), sem("to_exp0"), sem("exped0")
        gate_ready, gate_turned, rows_ready, rows_out, gT_in = (
            sem("gate0"), sem("gturn0"), sem("grow0"), sem("grow_out0"), sem("gT_in0"))
        w_in = [sem(f"w_in0_{p}") for p in range(2)]
        hid_ready, tdone = sem("hid_ready0"), sem("tdone2")
        gelu_done = sem("gelu0")
        gate_done = sem("gated0")
        gated_used = sem("used0")
        block = ctx.enter_context(nc.Block())

        @block.sync
        def _(sp):
            sp.dma_start(wg[:, :], A["wg0"]).then_inc(rw_in, 16)
            sp.dma_start(bgB[:, :], A["bg0"].to_broadcast([128, E])).then_inc(rw_in, 16)
            sp.dma_start(b2[:, :], A["b2_0"]).then_inc(rw_in, 16)

            def load_weights(e, p):
                sp.dma_start(w1[p][:, :], A["w1_0"][bass.ds(e, 1), :, :].rearrange("e p f -> (e p) f")).then_inc(w_in[p], 16)
                sp.dma_start(w2[p][:, :, :], A["w2_0"][bass.ds(e, 1), :, :].rearrange("e p (c d) -> (e p) c d", c=FC)).then_inc(w_in[p], 16)
                sp.dma_start(b1[p][:, :], A["b1_0"][bass.ds(e, 1), :, :].rearrange("e p f -> (e p) f")).then_inc(w_in[p], 16)

            def load_gate(e, p):
                sp.dma_start(gB[p][:, :], gates_d[bass.ds(e, 1), :].to_broadcast([128, NT])).then_inc(w_in[p], 16)

            load_weights(0, 0)
            load_weights(1, 1)
            sp.wait_ge(rows_ready, 1)
            sp.dma_start(gates_d[0:E, :].rearrange("e (c j) -> (e c) j", j=128), gate_rows[:, :]).then_inc(rows_out, 16)
            sp.dma_start(gates_d[E:NE, :].rearrange("e (c j) -> (e c) j", j=128), ones_rows[:, :]).then_inc(rows_out, 16)
            sp.wait_ge(rows_out, 32)
            sp.dma_start(gT[:, :], gates_d[:, :]).then_inc(gT_in, 16)
            load_gate(0, 0)
            load_gate(1, 1)

            def load(e, p):
                sp.wait_ge(gated_used, 16 * e - 8)
                load_weights(e, p)
                load_gate(e, p)

            with sp.Fori(2, E, 2) as e:
                load(e, 0)
                load(e + 1, 1)
            load(E, 0)

        @block.tensor
        def _(pe):
            ln_tensor(pe, S, 1, mean_ps, var_ps)
            pe.wait_ge(rw_in, 48)
            router_tensor(pe, S, logits_ps, wg[:, :], NB, logits_done)
            pe.wait_ge(gate_ready, 1)
            pe.transpose(gate_ps, R.gate[:, :, :].rearrange("p e c -> p (e c)"), S.ident).then_inc(gate_turned, 1)
            pe.wait_ge(rows_ready, 1)
            pe.wait_ge(gT_in, 16)
            for b in range(NB):
                pe.matmul(y_ps[b][:, :], b2[:, :], gT[:, blk(b)], start=True, stop=False, skip_group_check=True)

            def hidden(e, p, b):
                for f in range(FC):
                    n = FC * b + f
                    pe.wait_ge(gelu_done, 16 * e + n + 1)
                    pe.matmul(hid_ps[n % 4][:, :], w1[p][:, blk(f, 128)], h_block(S, b), start=True, stop=True).then_inc(hid_ready, 1)

            def back(e, p, b):
                for f in range(FC):
                    n = FC * b + f
                    pe.wait_ge(gate_done, 16 * e + n + 5)
                    pe.matmul(y_ps[b][:, :], w2[p][:, f, :], gated[:, n % (2 * FC), :], start=False,
                              stop=False, skip_group_check=True).then_inc(gated_used, 1)

            def expert(e, p, uses):
                pe.wait_ge(w_in[p], 64 * uses)
                hidden(e, p, 0)
                for b in range(NB):
                    if b + 1 < NB:
                        hidden(e, p, b + 1)
                    back(e, p, b)

            with pe.Fori(0, E // 2) as i:
                expert(2 * i, 0, i + 1)
                expert(2 * i + 1, 1, i + 1)
            expert(E, 0, E // 2 + 1)

        @block.scalar
        def _(act):
            ln_scalar(act, S, 1, var_ps)
            act.wait_ge(to_exp, 1)
            act.activation(R.p[:, :, :], R.p[:, :, :], ACT.Exp).then_inc(exped, 1)

            def expert(e, p, uses):
                act.wait_ge(w_in[p], 64 * uses)
                for n in range(4 * FC):
                    act.wait_ge(hid_ready, 16 * e + n + 1)
                    act.wait_ge(gate_done, 16 * e + n + 1)
                    act.activation(hid[:, n % 4, :], hid_ps[n % 4][:, :], ACT.Gelu,
                                   bias=b1[p][:, n % FC:n % FC + 1]).then_inc(gelu_done, 1)

            with act.Fori(0, E // 2) as i:
                expert(2 * i, 0, i + 1)
                expert(2 * i + 1, 1, i + 1)
            expert(E, 0, E // 2 + 1)

        @block.vector
        def _(dve):
            link = make_link(dve, tdone)
            link(dve.memset(ones_rows[:, :], 1.0))
            dve.memset(R.m[:, 0:1], 0.0).then_inc(gelu_done, 4)
            dve.memset(R.m[:, 1:2], 0.0).then_inc(gate_done, 4)
            dve.memset(R.m[:, 2:3], 0.0).then_inc(gated_used, 8)
            dve.wait_ge(gated_used, 8)
            ln_vector(dve, S, link, 1, mean_ps, S.mod[:, CB:CB + 1], S.mod[:, SB:SB + 1])
            dve.wait_ge(rw_in, 48)
            dve.wait_ge(logits_done, 1)
            link(dve.tensor_tensor(R.p[:, :, :], logits_ps.rearrange("p (t e) -> p t e", e=E),
                                   bgB[:, :].unsqueeze(1).to_broadcast([128, NTILE, E]), ALU.add))
            top2_vector(dve, S, link, R, to_exp, exped)
            dve.tensor_tensor(R.gate[:, :, :].rearrange("p e c -> p c e"), R.sel[:, :, :], R.p[:, :, :],
                              ALU.mult).then_inc(gate_ready, 1)
            dve.wait_ge(gate_turned, 1)
            dve.tensor_copy(gate_rows[:, :], gate_ps).then_inc(rows_ready, 1)

            def expert(e, p, uses):
                dve.wait_ge(w_in[p], 64 * uses)
                for n in range(4 * FC):
                    dve.wait_ge(gelu_done, 16 * e + n + 5)
                    dve.wait_ge(gated_used, 16 * e + n + 1)
                    dve.tensor_tensor(gated[:, n % (2 * FC), :], hid[:, n % 4, :], gB[p][:, blk(n // FC)],
                                      ALU.mult).then_inc(gate_done, 1)

            with dve.Fori(0, E // 2) as i:
                expert(2 * i, 0, i + 1)
                expert(2 * i + 1, 1, i + 1)
            expert(E, 0, E // 2 + 1)
            dve.wait_ge(gated_used, 8 + 16 * NE)
            for b in range(NB):
                dve.scalar_tensor_tensor(S.xT[:, blk(b)], y_ps[b][:, :], S.mod[:, GB:GB + 1], S.xT[:, blk(b)],
                                         ALU.mult, ALU.add).then_inc(S.x_ready, 1)
            dve.wait_ge(S.x_ready, 3 * NB)



Q_PARTS = (0, 0, 1, 1, 0, 2)
K_PARTS = (0, 1, 0, 1, 2, 0)
KP = DK * len(Q_PARTS)
KM = KP + 3
VW = DK + 1


def stage_qkv(nc, S, A):
    with ExitStack() as ctx:
        sb = lambda n, s, d=F32: ctx.enter_context(nc.sbuf_tensor(n, s, d))
        ps = lambda n: ctx.enter_context(nc.psum_tensor(n, [128, TB], F32))
        wqkv = sb("wqkv", [128, 3, D])
        bvB = sb("bvB", [128, D])
        full = sb("qk_full", [128, 2, TB])
        parts = sb("parts_sb", [128, 2, 3, TB], BF16)
        mean_ps = [ps("mean3a"), ps("mean3b")]
        var_ps = [ps("var3a"), ps("var3b")]
        qk_ps = [ps("qk0"), ps("qk1")]
        v_ps = [ps("v0"), ps("v1")]

        sem = S.sem
        w_in, qk_mm, full_done, part1, rest_done, part2, part3 = (
            sem("w_in3"), sem("qk_mm"), sem("full_done"), sem("part1"), sem("rest_done"), sem("part2"), sem("part3"))
        parts_out = [sem("q_parts_out"), sem("k_parts_out")]
        v_mm, v_done, tdone = sem("v_mm"), sem("v_done"), sem("tdone3")
        block = ctx.enter_context(nc.Block())

        @block.sync
        def _(sp):
            sp.dma_start(wqkv[:, :, :], A["wqkv"]).then_inc(w_in, 16)
            sp.dma_start(bvB[:, :], A["bv"].to_broadcast([128, D])).then_inc(w_in, 16)
            sp.dma_start(S.kop[KP:KM, :, :], A["one_rows"]).then_inc(S.ones_in, 16)
            for n in range(2 * NB):
                sp.wait_ge(part3, n + 1)
                sp.dma_start(A["qk_parts"][n % 2].rearrange("s p t -> p s t")[:, :, blk(n // 2)],
                             parts[:, n % 2, :, :]).then_inc(parts_out[n % 2], 16)
            for q_or_k in parts_out:
                sp.wait_ge(q_or_k, 16 * NB)
            for rest, heads in enumerate((slice(0, QUAD), slice(QUAD, H))):
                for j, (op, which) in enumerate(((S.qop, Q_PARTS), (S.kop, K_PARTS))):
                    for r, s in enumerate(which):
                        sp.dma_start(op[DK * r:DK * (r + 1), heads, :],
                                     A["qk_parts"][j, s].rearrange("(h d) t -> d h t", d=DK)[:, heads, :]).then_inc(S.ops_in[rest], 16)

        @block.tensor
        def _(pe):
            ln_tensor(pe, S, 2, mean_ps, var_ps)
            pe.wait_ge(w_in, 32)
            for b in range(NB):
                pe.wait_ge(S.h_ready, 2 * NB + b + 1)
                for j in range(2):
                    n = 2 * b + j
                    if n >= 2:
                        pe.wait_ge(full_done, n - 1)
                    pe.matmul(qk_ps[j][:, :], wqkv[:, j, :], h_block(S, b), start=True, stop=True).then_inc(qk_mm, 1)
                if b >= 2:
                    pe.wait_ge(v_done, b - 1)
                for u in range(TB // 128):
                    last = pe.matmul(v_ps[b % 2][:, blk(u, 128)], h_tile(S, 4 * b + u), wqkv[:, 2, :], start=True, stop=True)
                last.then_inc(v_mm, 1)

        @block.scalar
        def _(act):
            ln_scalar(act, S, 2, var_ps)
            for n in range(2 * NB):
                act.wait_ge(full_done, n + 1)
                if n >= 2:
                    act.wait_ge(parts_out[n % 2], 16 * (n // 2))
                act.activation(parts[:, n % 2, 0, :], full[:, n % 2, :], ACT.Copy).then_inc(part1, 1)
                act.wait_ge(rest_done, n + 1)
                act.activation(parts[:, n % 2, 1, :], full[:, n % 2, :], ACT.Copy).then_inc(part2, 1)

        @block.vector
        def _(dve):
            link = make_link(dve, tdone)
            link(dve.memset(S.v_all[:, :, :, DK:VW], 1.0))
            ln_vector(dve, S, link, 2, mean_ps, S.mod[:, 6 + CA:7 + CA], S.mod[:, 6 + SA:7 + SA])
            dve.wait_ge(w_in, 32)
            for b in range(NB):
                for j in range(2):
                    n = 2 * b + j
                    dve.wait_ge(qk_mm, n + 1)
                    if n >= 2:
                        dve.wait_ge(part3, n - 1)
                    x = full[:, n % 2, :]
                    dve.tensor_scalar(x, qk_ps[j][:, :], S.cols[:, BQ + j:BQ + j + 1], None, ALU.add).then_inc(full_done, 1)
                dve.wait_ge(v_mm, b + 1)
                dve.tensor_tensor(S.v_all[:, 4 * b:4 * b + 4, :, 0:DK],
                                  v_ps[b % 2][:, :].rearrange("p (t h d) -> p t h d", t=4, d=DK),
                                  bvB[:, :].rearrange("p (h d) -> p h d", d=DK).unsqueeze(1).to_broadcast([128, 4, H, DK]),
                                  ALU.add).then_inc(v_done, 1)
                for j in range(2):
                    n = 2 * b + j
                    x = full[:, n % 2, :]
                    dve.wait_ge(part1, n + 1)
                    dve.tensor_tensor(x, x, parts[:, n % 2, 0, :], ALU.subtract).then_inc(rest_done, 1)
                for j in range(2):
                    n = 2 * b + j
                    dve.wait_ge(part2, n + 1)
                    dve.tensor_tensor(parts[:, n % 2, 2, :], full[:, n % 2, :], parts[:, n % 2, 1, :],
                                      ALU.subtract).then_inc(part3, 1)



QUAD = 4
NQ = H // QUAD
MW = 2 * TB
STEPS = [(g, kt, max(0, kt - 4 * g) * 128) for g in range(NB) for kt in range(4 * g + 4)]
CHUNKS = []
for _g in range(NB):
    for _t in range(4 * _g, 4 * _g + 4):
        for _j in range(QUAD):
            for _c in range(_t * 128 // MW + 1):
                CHUNKS.append((_t, _j, _c, min(MW, 128 * (_t + 1) - MW * _c)))
    CHUNKS.append(None)
NS, NCH = len(STEPS), len(CHUNKS)


def chunks_by_step():
    step_cost = [TB - off for _, _, off in STEPS]
    chunk_cost = [c[3] if c else 16 for c in CHUNKS]
    done, at, spent, out = 0, 0, 0, []
    for cost in step_cost:
        done += cost
        while at < NCH and spent * sum(step_cost) <= done * sum(chunk_cost):
            spent += chunk_cost[at]
            at += 1
        out.append(at)
    out[-1] = NCH
    return out


def early(eng, value):
    if not isinstance(value, int):
        eng.compute_val(value)


def stage_attention(nc, S, A):
    with ExitStack() as ctx:
        sb = lambda n, s, d=F32: ctx.enter_context(nc.sbuf_tensor(n, s, d))
        ps = lambda n, w=TB: ctx.enter_context(nc.psum_tensor(n, [128, w], F32))
        mask, masked = S.sd[:, 0:MW], (S.sd[:, MW:2 * MW], S.xc[:, MW:2 * MW])
        o_sb = S.xc[:, 0:2 * TB].rearrange("p (a t) -> p a t", a=2)
        chunk_max = sb("chunk_max", [128, QUAD, NTILE, 2])
        causal_t = sb("causal_t", [128, 2, 128], BF16)
        neg_max = sb("neg_max", [128, QUAD, 4])
        max_rest = sb("max_rest", [QUAD * 4, 128])
        max_parts = sb("max_parts", [QUAD * 4, 2, 3, 128], BF16)
        probs = sb("probs", [128, 2, QUAD, TB])
        v_quad = sb("v_quad", [128, NTILE, QUAD, VW])
        max_ps = [ps("max0", MW), ps("max1", MW)]
        st_ps = [ps(f"st{n}") for n in range(3)]
        o_ps = ps("o_acc")
        qop = S.qop[:, :, :].rearrange("p h t -> p (h t)")
        kop = S.kop[:, :, :].rearrange("p h t -> p (h t)")

        sem = S.sem
        mask_in, causal_in = sem("mask_in"), sem("causal_in")
        scores_ready = sem("scores_ready")
        max_bank_free = sem("max_bank_free")
        max_stored, neg_max_ready, max_parts_ready = sem("max_stored"), sem("neg_max"), sem("max_parts")
        max_rows_in = [sem("max_rows_in0"), sem("max_rows_in1")]
        st_ready = sem("st_ready")
        st_free = sem("st_free")
        probs_free = sem("probs_free")
        v_ready, o_out = sem("v_ready"), [sem("o_out0"), sem("o_out1")]
        o_free = sem("o_free")
        block = ctx.enter_context(nc.Block())

        last_step = [max(s for s, x in enumerate(STEPS) if x[0] == g) for g in range(NB)]
        plan = chunks_by_step()

        @block.sync
        def _(sp):
            sp.dma_start(mask, A["causal"]).then_inc(mask_in, 16)
            sp.dma_start(causal_t[:, :, :], A["causal_t"]).then_inc(causal_in, 16)

            def max_rows(i, g):
                sp.wait_ge(max_parts_ready, NB * i + g + 1)
                rows = A["max_rows"][g, :, bass.ds(QUAD * i, QUAD), :]
                sp.dma_start(rows.rearrange("s j (t q) -> (j t) s q", q=128),
                             max_parts[:, g % 2, :, :]).then_inc(max_stored, 16)
                sp.wait_ge(max_stored, i * (16 * NB) + 16 * (g + 1))
                sp.dma_start(S.qop[KP:KM, bass.ds(QUAD * i, QUAD), blk(g)], rows).then_inc(max_rows_in[g % 2], 16)

            def store(i, g):
                sp.wait_ge(o_free, NB * i + g + 2)
                for j in range(QUAD):
                    sp.dma_start(A["attn_sums"][bass.ds(QUAD * i + j, 1), :, blk(g)].rearrange("o v t -> (o v) t"),
                                 o_sb[32 * j:32 * j + VW, g % 2, :]).then_inc(o_out[g % 2], 16)

            for g in range(NB):
                max_rows(0, g)
            with sp.Fori(0, NQ - 1) as i:
                for g in range(NB):
                    max_rows(i + 1, g)
                    store(i, g)
            for g in range(NB):
                store(NQ - 1, g)
            for half in o_out:
                sp.wait_ge(half, 8 * QUAD * NB * NQ)

        @block.tensor
        def _(pe):
            pe.wait_ge(S.ones_in, 16)
            pe.wait_ge(causal_in, 16)
            pe.wait_ge(S.const_in, 32)

            @contextmanager
            def quad_offset(i, s):
                if isinstance(i, int):
                    yield i * (QUAD * NT)
                    return
                reg = pe.alloc_register(f"quad_offset{s}")
                pe.reg_mov(reg, i * (QUAD * NT))
                yield pe.snap(reg, min_val=0, max_val=(NQ - 2) * QUAD * NT)
                pe.free_register(reg)

            def chunk(at, i, ahead, n):
                pe.wait_ge(max_bank_free, i * NCH + (ahead * NCH + n + 1))
                bank = max_ps[n % 2]
                if CHUNKS[n] is None:
                    g = sum(c is None for c in CHUNKS[:n])
                    pe.wait_ge(neg_max_ready, i * NB + (ahead * NB + g + 1))
                    pe.transpose(bank[0:4 * QUAD, 0:128], neg_max[:, :, :].rearrange("p j t -> p (j t)"),
                                 S.ident).then_inc(scores_ready, 1)
                    return
                t, j, c, width = CHUNKS[n]
                head = (ahead * QUAD + j) * NT
                for u in range(0, width, TB):
                    w = min(TB, width - u)
                    last = pe.matmul(bank[:, u:u + w], qop[0:KP, bass.ds(at + (head + 128 * t), 128)],
                                     kop[0:KP, bass.ds(at + (head + MW * c + u), w)], start=True, stop=True)
                last.then_inc(scores_ready, 1)

            def scores(at, i, s):
                g, kt, off = STEPS[s]
                if kt == 0:
                    pe.wait_ge(max_rows_in[g % 2], i * (8 * NB) + 16 * (g // 2 + 1))
                for j in range(QUAD):
                    n = QUAD * s + j
                    pe.wait_ge(st_free, i * (QUAD * NS) + max(n + 1, 3))
                    own = kt >= 4 * g
                    last = pe.matmul(st_ps[n % 3][:, off:TB], kop[0:KM, bass.ds(at + (j * NT + 128 * kt), 128)],
                                     qop[0:KM, bass.ds(at + (j * NT + TB * g + off), TB - off)],
                                     start=True, stop=not own)
                    if own:
                        last = pe.matmul(st_ps[n % 3][:, off:off + 128], causal_t[:, 0, :], causal_t[:, 1, :],
                                         start=False, stop=True)
                    last.then_inc(st_ready, 1)

            def products(i, s):
                g, kt, off = STEPS[s]
                if s == 0:
                    pe.wait_ge(v_ready, i + 1)
                if kt == 0:
                    pe.wait_ge(o_free, NB * i + g + 1)
                pe.wait_ge(st_free, i * (QUAD * NS) + QUAD * (s + 1) + 3)
                for j in range(QUAD):
                    last = pe.matmul(o_ps[32 * j:32 * j + VW, off:TB], v_quad[:, kt, j, :], probs[:, s % 2, j, off:TB],
                                     start=(kt == 0), stop=(kt == 4 * g + 3))
                last.then_inc(probs_free, 1)

            pe.wait_ge(S.ops_in[0], 12 * 16)
            for n in range(NCH):
                chunk(0, 0, 0, n)
            pe.wait_ge(S.ops_in[1], 12 * 16)

            def quad(i, beside):
                for s in range(NS):
                    with quad_offset(i, s) as at:
                        scores(at, i, s)
                        if beside:
                            for n in range(plan[s - 1] if s else 0, plan[s]):
                                chunk(at, i, 1, n)
                    if s:
                        products(i, s - 1)
                products(i, NS - 1)

            with pe.Fori(0, NQ - 1) as i:
                quad(i, True)
            quad(NQ - 1, False)

        @block.vector
        def _(dve):
            dve.memset(chunk_max[:, :, :, :], -BIG).then_inc(max_bank_free, 2)
            dve.memset(v_quad[:, 0, 0, 0:1], 0.0).then_inc(st_free, 3)
            dve.memset(o_ps[:, :], 0.0).then_inc(o_free, 1)
            dve.memset(v_quad[:, 0, 0, 1:2], 0.0).then_inc(probs_free, 2)
            dve.wait_ge(max_bank_free, 2)

            def maxima(i, first):
                for n, c in enumerate(CHUNKS):
                    if c:
                        early(dve, NCH * i + n + 1)
                        dve.wait_ge(mask_in, 16)
                        dve.wait_ge(scores_ready, NCH * i + n + 1)
                    bank = max_ps[n % 2]
                    if c:
                        t, j, k, width = c
                        out = chunk_max[:, j, t, k:k + 1]
                        if MW * k + width == 128 * (t + 1):
                            dve.tensor_tensor_reduce(masked[n % 2][:, 0:width], bank[:, 0:width], mask[:, MW - width:MW], 1.0,
                                                     -BIG, ALU.add, ALU.max, out).then_inc(max_bank_free, 1)
                        else:
                            dve.tensor_reduce(out, bank[:, 0:width], AX.X, ALU.max).then_inc(max_bank_free, 1)
                        continue
                    g = sum(x is None for x in CHUNKS[:n])
                    dve.wait_ge(max_bank_free, NCH * i + n + 2)
                    dve.tensor_reduce(neg_max[:, :, :], chunk_max[:, :, 4 * g:4 * g + 4, :], AX.X, ALU.max,
                                      negate=True).then_inc(neg_max_ready, 1)
                    dve.wait_ge(scores_ready, NCH * i + n + 1)
                    if not (first and g < 2):
                        dve.wait_ge(max_rows_in[g % 2], i * (8 * NB) + 16 * (g // 2))
                    parts = max_parts[:, g % 2, :, :]
                    turned = bank[0:4 * QUAD, 0:128]
                    dve.tensor_copy(parts[:, 0, :], turned).then_inc(S.split, 1)
                    dve.wait_ge(S.split, i * (2 * NB) + 2 * g + 1)
                    dve.tensor_tensor(max_rest[:, :], turned, parts[:, 0, :], ALU.subtract).then_inc(max_bank_free, 1)
                    dve.wait_ge(max_bank_free, NCH * i + n + 3)
                    dve.tensor_copy(parts[:, 1, :], max_rest[:, :]).then_inc(S.split, 1)
                    dve.wait_ge(S.split, i * (2 * NB) + 2 * g + 2)
                    dve.tensor_tensor(parts[:, 2, :], max_rest[:, :], parts[:, 1, :], ALU.subtract).then_inc(max_parts_ready, 1)
                    early(dve, NB * i + g + 1)
                    dve.wait_ge(mask_in, 16)
                    dve.wait_ge(max_parts_ready, NB * i + g + 1)

            maxima(0, True)
            with dve.Fori(1, NQ) as i:
                maxima(i, False)

        @block.scalar
        def _(act):
            def quad(i, first):
                for s, (g, kt, off) in enumerate(STEPS):
                    act.wait_ge(probs_free, NS * i + s + 1)
                    for j in range(QUAD):
                        n = QUAD * s + j
                        act.wait_ge(st_ready, i * (QUAD * NS) + n + 1)
                        act.activation(probs[:, s % 2, j, off:TB], st_ps[n % 3][:, off:TB], ACT.Exp,
                                       scale=DK ** -0.5).then_inc(st_free, 1)
                    if kt == 0 and g:
                        copy_sums(i, g - 1, first)
                copy_sums(i, NB - 1, first)

            def copy_sums(i, g, first):
                act.wait_ge(probs_free, NS * i + last_step[g] + 3)
                if not (first and g < 2):
                    act.wait_ge(o_out[g % 2], i * (32 * NB) + 64 * (g // 2))
                act.activation(o_sb[:, g % 2, :], o_ps[:, :], ACT.Copy).then_inc(o_free, 1)

            quad(0, True)
            with act.Fori(1, NQ) as i:
                quad(i, False)

        @block.gpsimd
        def _(pool):
            def quad(i):
                pool.wait_ge(probs_free, NS * i + 2)
                pool.tensor_copy(v_quad[:, :, :, :], S.v_all[:, :, bass.ds(QUAD * i, QUAD), :]).then_inc(v_ready, 1)

            with pool.Fori(0, NQ) as i:
                quad(i)



def stage_attention_out(nc, S, A):
    with ExitStack() as ctx:
        sb = lambda n, s, d=F32: ctx.enter_context(nc.sbuf_tensor(n, s, d))
        num = sb("num", [128, NT])
        den = sb("den", [128, NT])
        sums_in = [S.sem(f"sums_in{b}") for b in range(NB)]
        tdone = S.sem("tdone5a")
        block = ctx.enter_context(nc.Block())

        @block.sync
        def _(sp):
            for b in range(NB):
                sp.dma_start(num[:, blk(b)], A["attn_sums"][:, 0:DK, blk(b)]).then_inc(sums_in[b], 16)
                sp.dma_start(den[:, blk(b)], A["attn_sums"][:, DK:VW, blk(b)].to_broadcast([H, DK, TB])).then_inc(sums_in[b], 16)

        @block.vector
        def _(dve):
            link = make_link(dve, tdone)
            for b in range(NB):
                dve.wait_ge(sums_in[b], 32)
                link(dve.reciprocal(den[:, blk(b)], den[:, blk(b)]))
                link(dve.scalar_tensor_tensor(num[:, blk(b)], num[:, blk(b)], S.mod[:, 6 + GA:7 + GA], den[:, blk(b)],
                                              ALU.mult, ALU.mult))
                dve.tensor_tensor(S.xT[:, blk(b)], S.xT[:, blk(b)], num[:, blk(b)], ALU.add).then_inc(S.x_ready, 1)
            dve.wait_ge(S.x_ready, 4 * NB)



def stage_swiglu_moe(nc, S, A):
    gates_d = A["gates1"]
    with ExitStack() as ctx:
        sb = lambda n, s, d=F32: ctx.enter_context(nc.sbuf_tensor(n, s, d))
        ps = lambda n: ctx.enter_context(nc.psum_tensor(n, [128, TB], F32))
        R = Routing(sb, 1)
        wr = sb("wr1", [128, E])
        w_t = sb("w_t", [128, 128])
        hit = sb("hit", [128, 128])
        tie = sb("tie", [128, 128])
        rank = sb("rank", [128, 128])
        count = sb("count", [128, 1])
        need = sb("need", [128, 1])
        bit = sb("bit", [128, 1], I32)
        thr = sb("thr", [128, 1], I32)
        cand = sb("cand", [128, 1], I32)
        gate_rows = sb("gate_rows1", [128, 128])
        wg = [sb(f"wgt_{p}", [128, F]) for p in range(2)]
        wu = [sb(f"wup_{p}", [128, F]) for p in range(2)]
        wd = [sb(f"wdn_{p}", [128, FC, D]) for p in range(2)]
        gB = [sb(f"gB1_{p}", [128, NT]) for p in range(2)]
        act_g = sb("act_g", [128, 2, TB])
        mul_u = sb("mul_u", [128, 2, TB])
        gated = sb("gated1", [128, 2 * FC, TB])
        y_ps = [ps(f"y1_{b}") for b in range(NB)]
        g_ps = [ps("g_ps0"), ps("g_ps1")]
        u_ps = [ps("u_ps0"), ps("u_ps1")]
        mean_ps, var_ps = g_ps, u_ps
        logits_ps = y_ps[0][:, 0:NTILE * E]
        turn_ps = y_ps[1][:, 0:128]
        total_ps = y_ps[2]

        sem = S.sem
        rw_in, logits_done, to_exp, exped = sem("rw_in1"), sem("logits1"), sem("to_exp1"), sem("exped1")
        weights_ready, turned, rows_ready, rows_out = sem("weights1"), sem("turned1"), sem("grow1"), sem("grow_out1")
        counted, totalled = sem("counted"), sem("totalled")
        w_in = [sem(f"w_in1_{p}") for p in range(2)]
        up_ready, silu_done = sem("up_ready"), sem("silu_done1")
        up_free = sem("up_free")
        gate_done = sem("gated1_done")
        gated_used = sem("used1")
        tdone, tloop, y_zero = sem("tdone6"), sem("bit_steps"), sem("y_zero")
        stored = sem("stored")
        block = ctx.enter_context(nc.Block())

        @block.sync
        def _(sp):
            sp.dma_start(wr[:, :], A["wr1"]).then_inc(rw_in, 16)

            def load_weights(e, p):
                sp.dma_start(wg[p][:, :], A["wg_1"][bass.ds(e, 1), :, :].rearrange("e p f -> (e p) f")).then_inc(w_in[p], 16)
                sp.dma_start(wu[p][:, :], A["wu_1"][bass.ds(e, 1), :, :].rearrange("e p f -> (e p) f")).then_inc(w_in[p], 16)
                sp.dma_start(wd[p][:, :, :], A["wd_1"][bass.ds(e, 1), :, :].rearrange("e p (c d) -> (e p) c d", c=FC)).then_inc(w_in[p], 16)

            def load_gate(e, p):
                sp.dma_start(gB[p][:, :], gates_d[bass.ds(e, 1), :].to_broadcast([128, NT])).then_inc(w_in[p], 16)

            load_weights(0, 0)
            load_weights(1, 1)
            sp.wait_ge(rows_ready, 1)
            sp.dma_start(gates_d.rearrange("e (c j) -> (e c) j", j=128), gate_rows[:, :]).then_inc(rows_out, 16)
            sp.wait_ge(rows_out, 16)
            load_gate(0, 0)
            load_gate(1, 1)
            with sp.Fori(1, E // 2) as i:
                for p in range(2):
                    sp.wait_ge(gated_used, i * 32 + (16 * p - 8))
                    load_weights(2 * i + p, p)
                    load_gate(2 * i + p, p)
            for b in range(NB):
                sp.wait_ge(S.x_ready, 4 * NB + b + 1)
                sp.dma_start(A["out"][:, blk(b)], S.xT[:, blk(b)]).then_inc(stored, 16)
            sp.wait_ge(stored, 16 * NB)

        @block.tensor
        def _(pe):
            ln_tensor(pe, S, 3, mean_ps, var_ps)
            pe.wait_ge(rw_in, 16)
            router_tensor(pe, S, logits_ps, wr[:, :], 3 * NB, logits_done)
            pe.wait_ge(weights_ready, 1)
            pe.transpose(turn_ps, R.gate[:, :, :].rearrange("p e c -> p (e c)"), S.ident).then_inc(turned, 1)

            def total(n, weights=None):
                pe.wait_ge(counted, n)
                pe.matmul(total_ps[:, 0:1], S.same_expert if weights is None else weights, count[:, :],
                          start=True, stop=True).then_inc(totalled, 1)

            total(1)
            with pe.Fori(2, NBITS + 1) as n:
                total(n)
            total(NBITS + 1)
            total(NBITS + 2, S.earlier_tile)
            pe.wait_ge(y_zero, 1)
            for b in range(NB):
                pe.matmul(y_ps[b][:, :], hit[:, :], S.hT[:, blk(b)], start=True, stop=False, skip_group_check=True)

            def hidden(i, p, b):
                for f in range(FC):
                    n = FC * b + f
                    pe.wait_ge(up_free, i * 32 + (16 * p + n + 1))
                    pe.matmul(g_ps[n % 2][:, :], wg[p][:, blk(f, 128)], h_block(S, b), start=True, stop=True)
                    pe.matmul(u_ps[n % 2][:, :], wu[p][:, blk(f, 128)], h_block(S, b), start=True, stop=True).then_inc(up_ready, 1)

            def back(i, p, b):
                for f in range(FC):
                    n = FC * b + f
                    pe.wait_ge(gate_done, i * 32 + (16 * p + n + 1))
                    pe.matmul(y_ps[b][:, :], wd[p][:, f, :], gated[:, n % (2 * FC), :], start=False,
                              stop=False, skip_group_check=True).then_inc(gated_used, 1)

            with pe.Fori(0, E // 2) as i:
                for p in range(2):
                    pe.wait_ge(w_in[p], i * 64 + 64)
                    hidden(i, p, 0)
                    for b in range(NB):
                        if b + 1 < NB:
                            hidden(i, p, b + 1)
                        back(i, p, b)

        @block.scalar
        def _(act):
            ln_scalar(act, S, 3, var_ps)
            act.wait_ge(to_exp, 1)
            act.activation(R.p[:, :, :], R.p[:, :, :], ACT.Exp).then_inc(exped, 1)
            with act.Fori(0, E) as e:
                for n in range(4 * FC):
                    act.wait_ge(up_free, e * 16 + (n + 1))
                    act.wait_ge(up_ready, e * 16 + (n + 1))
                    act.activation(act_g[:, n % 2, :], g_ps[n % 2][:, :], ACT.Silu).then_inc(silu_done, 1)

        @block.vector
        def _(dve):
            link = make_link(dve, tdone)
            dve.memset(R.m[:, 0:1], 0.0).then_inc(up_free, 2)
            dve.memset(R.m[:, 1:2], 0.0).then_inc(gated_used, 8)
            dve.wait_ge(gated_used, 8)
            ln_vector(dve, S, link, 3, mean_ps, S.mod[:, 6 + CB:7 + CB], S.mod[:, 6 + SB:7 + SB])
            dve.wait_ge(logits_done, 1)
            link(dve.tensor_copy(R.p[:, :, :], logits_ps.rearrange("p (t e) -> p t e", e=E)))
            top2_vector(dve, S, link, R, to_exp, exped)
            link(dve.tensor_tensor(R.m[:, :], R.top1[:, :], R.top2[:, :], ALU.add))
            link(dve.tensor_scalar(R.m[:, :], R.m[:, :], 1e-6, None, ALU.add))
            link(dve.reciprocal(R.m[:, :], R.m[:, :]))
            link(dve.tensor_tensor(R.p[:, :, :], R.p[:, :, :], R.m[:, :].unsqueeze(2).to_broadcast([128, NTILE, E]), ALU.mult))
            link(dve.tensor_tensor(R.p[:, :, :], R.p[:, :, :], R.sel[:, :, :], ALU.mult))
            link(dve.tensor_scalar(R.sel[:, :, :], R.sel[:, :, :], -1.0, None, ALU.add))
            dve.tensor_tensor(R.gate[:, :, :].rearrange("p e c -> p c e"), R.p[:, :, :], R.sel[:, :, :],
                              ALU.add).then_inc(weights_ready, 1)
            dve.wait_ge(turned, 1)
            link(dve.tensor_copy(w_t[:, :], turn_ps))
            link(dve.memset(thr[:, :], 0))
            link(dve.memset(cand[:, :], 1 << (NBITS - 1)))

            def count_from(n):
                dve.tensor_scalar(hit[:, :], w_t[:, :], cand[:, :].bitcast(F32), None, ALU.is_ge, ALU.add,
                                  accum_out=count[:, :]).then_inc(counted, 1)
                dve.wait_ge(totalled, n)

            def settle(step, value, next_value):
                dve.tensor_scalar(bit[:, :], total_ps[:, 0:1], float(CAP), value, ALU.is_ge, ALU.mult).then_inc(tloop, 1)
                dve.wait_ge(tloop, step + 1)
                dve.tensor_tensor(thr[:, :], thr[:, :], bit[:, :], ALU.bitwise_or).then_inc(tloop, 1)
                dve.wait_ge(tloop, step + 2)
                dve.tensor_tensor(cand[:, :], thr[:, :], next_value, ALU.bitwise_or).then_inc(tloop, 1)
                dve.wait_ge(tloop, step + 3)

            with dve.Fori(0, NBITS) as k:
                count_from(k + 1)
                settle(k * 3, S.consts[:, bass.ds(k + 392, 1)], S.bits[:, bass.ds(k + 1, 1)])
            link(dve.tensor_scalar(hit[:, :], w_t[:, :], thr[:, :].bitcast(F32), None, ALU.is_gt))
            dve.tensor_scalar(tie[:, :], hit[:, :], 1.0, None, ALU.mult, ALU.add, accum_out=count[:, :]).then_inc(counted, 1)
            dve.wait_ge(totalled, NBITS + 1)
            link(dve.tensor_scalar(need[:, :], total_ps[:, 0:1], -1.0, float(CAP), ALU.mult, ALU.add))
            link(dve.tensor_scalar(tie[:, :], w_t[:, :], thr[:, :].bitcast(F32), None, ALU.is_equal))
            link(dve.tensor_tensor_scan(rank[:, :], tie[:, :], tie[:, :], 0.0, ALU.add, ALU.max))
            dve.tensor_copy(count[:, :], rank[:, 127:128]).then_inc(counted, 1)
            dve.wait_ge(totalled, NBITS + 2)
            link(dve.tensor_tensor(need[:, :], need[:, :], total_ps[:, 0:1], ALU.subtract))
            link(dve.tensor_scalar(rank[:, :], rank[:, :], need[:, :], None, ALU.is_le))
            link(dve.tensor_tensor(tie[:, :], tie[:, :], rank[:, :], ALU.mult))
            link(dve.tensor_tensor(hit[:, :], hit[:, :], tie[:, :], ALU.add))
            dve.tensor_tensor(gate_rows[:, :], w_t[:, :], hit[:, :], ALU.mult).then_inc(rows_ready, 1)
            dve.wait_ge(rows_ready, 1)
            dve.memset(hit[:, :], 0.0).then_inc(y_zero, 1)

            with dve.Fori(0, E // 2) as i:
                for p in range(2):
                    dve.wait_ge(w_in[p], i * 64 + 64)
                    for n in range(4 * FC):
                        at = 16 * p + n
                        dve.wait_ge(silu_done, i * 32 + (at + 1))
                        dve.tensor_tensor(mul_u[:, n % 2, :], act_g[:, n % 2, :], u_ps[n % 2][:, :], ALU.mult).then_inc(up_free, 1)
                        dve.wait_ge(up_free, i * 32 + (at + 3))
                        dve.wait_ge(gated_used, i * 32 + (at + 1))
                        dve.tensor_tensor(gated[:, n % (2 * FC), :], mul_u[:, n % 2, :], gB[p][:, blk(n // FC)],
                                          ALU.mult).then_inc(gate_done, 1)
            dve.wait_ge(gated_used, 8 + 16 * E)
            for b in range(NB):
                dve.scalar_tensor_tensor(S.xT[:, blk(b)], y_ps[b][:, :], S.mod[:, 6 + GB:7 + GB], S.xT[:, blk(b)],
                                         ALU.mult, ALU.add).then_inc(S.x_ready, 1)



def stage_store(nc, S, A):
    with ExitStack() as ctx:
        stored = S.sem("stored")
        block = ctx.enter_context(nc.Block())

        @block.sync
        def _(sp):
            sp.wait_ge(S.const_in, 32)
            sp.dma_start(A["out"], S.xT[:, :]).then_inc(stored, 16)
            sp.wait_ge(stored, 16)



def build(nc, A):
    with ExitStack() as ctx:
        S = Shared()
        sb = lambda n, s, d=F32: ctx.enter_context(nc.sbuf_tensor(n, s, d))
        S.sem = lambda n: ctx.enter_context(nc.semaphore(n))
        S.xT = sb("xT_s", [128, NT])
        S.hT = sb("hT_s", [128, NT + 1])
        S.xc = sb("xc_s", [128, NT])
        S.sd = sb("sd_s", [128, NT])
        S.sq = sb("sq_s", [128, 2, TB])
        S.cols = sb("cols_s", [128, 7])
        S.mod = sb("mod_s", [128, 12])
        S.eps_col = sb("eps_col", [128, 1])
        S.mean_w = sb("mean_w", [128, 128])
        S.consts = sb("consts_s", [128, A["consts"].shape[1]])
        S.ident = S.consts[:, 0:128]
        S.same_expert = S.consts[:, 128:256]
        S.earlier_tile = S.consts[:, 256:384]
        S.rev = S.consts[:, 384:392]
        S.bits = sb("bits", [128, NBITS + 1], I32)
        S.cols_in, S.const_in, S.ones_in, S.eps_set = S.sem("cols_in"), S.sem("const_in"), S.sem("ones_in"), S.sem("eps_set")
        S.x_ready, S.h_ready = S.sem("x_ready"), S.sem("h_ready")
        S.ln_mean, S.ln_centered, S.ln_squared = S.sem("ln_mean"), S.sem("ln_centered"), S.sem("ln_squared")
        S.ln_var, S.ln_sd = S.sem("ln_var"), S.sem("ln_sd")
        S.x_in = [S.sem(f"x_in{b}") for b in range(NB)]
        stage_mix(nc, S, A)
        if STAGE >= 2:
            stage_gelu_moe(nc, S, A)
        if STAGE >= 4:
            with ExitStack() as ctx34:
                sb34 = lambda n, s, d=F32: ctx34.enter_context(nc.sbuf_tensor(n, s, d))
                S.qop = sb34("qop", [KM, H, NT], BF16)
                S.kop = sb34("kop", [KM, H, NT], BF16)
                S.v_all = sb34("v_all", [128, NTILE, H, VW])
                S.ops_in, S.split = [S.sem("ops_in0"), S.sem("ops_in1")], S.sem("max_split")
                stage_qkv(nc, S, A)
                stage_attention(nc, S, A)
            stage_attention_out(nc, S, A)
        if STAGE >= 6:
            stage_swiglu_moe(nc, S, A)
            return
        stage_store(nc, S, A)


def kernel(**inputs):
    import numpy as np
    import ml_dtypes
    import concourse.bacc as _bacc
    from concourse.bass_utils import run_bass_kernel_spmd as _run

    g = {k: np.asarray(v) for k, v in inputs.items()}
    f32 = np.float32
    col = lambda n: g[n].reshape(D)
    cc = np.ascontiguousarray
    part = np.arange(128)
    causal = np.zeros((128, 1024), f32)
    causal[:, 896:] = np.where(part[None, :] > part[:, None], -BIG, 0.0)
    consts = np.concatenate([
        np.eye(128, dtype=f32),
        (part[:, None] // 16 == part[None, :] // 16).astype(f32),
        ((part[:, None] // 16 == part[None, :] // 16) & (part[:, None] % 16 < part[None, :] % 16)).astype(f32),
        np.broadcast_to(np.arange(E, 0, -1).astype(f32), (128, E)),
        np.broadcast_to(2.0 ** np.arange(NBITS - 1, -1, -1, dtype=f32), (128, NBITS)),
    ], axis=1)
    arrays = {
        "xT": cc(g["L0_attn_x"][0].T),
        "cols": cc(np.stack([col("L0_attn_time_decay"), col("L0_attn_time_first"), col("L0_attn_time_mix"),
                             col("L0_c"), col("L1_c"), col("L1_attn_bq"), col("L1_attn_bk")], axis=1)),
        "wmod": cc(np.stack([g["L0_wmod"], g["L1_wmod"]], axis=1)),
        "wmix": cc(np.stack([g[f"L0_attn_W{n}"].T for n in "kvro"], axis=1)),
        "consts": consts,
        "causal": causal,
        "wqkv": cc(np.stack([g[f"L1_attn_W{n}"].T for n in "qkv"], axis=1)),
        "bv": g["L1_attn_bv"].reshape(1, D),
        "wg0": g["L0_ffn_Wg"],
        "bg0": g["L0_ffn_bg"].reshape(1, E),
        "w1_0": np.concatenate([g["L0_ffn_W1"], g["L0_ffn_Ws1"]], axis=0),
        "w2_0": cc(np.concatenate([g["L0_ffn_W2"], g["L0_ffn_Ws2"]], axis=0).reshape(E + 1, FC, 128, D)
                   .transpose(0, 2, 1, 3).reshape(E + 1, 128, FC * D)),
        "b1_0": cc(np.concatenate([g["L0_ffn_b1"], g["L0_ffn_bs1"]], axis=0).reshape(E + 1, FC, 128).transpose(0, 2, 1)),
        "wr1": cc(g["L1_ffn_router_w"].T),
        "wg_1": g["L1_ffn_wg"],
        "wu_1": g["L1_ffn_wu"],
        "wd_1": cc(g["L1_ffn_wd"].reshape(E, FC, 128, D).transpose(0, 2, 1, 3).reshape(E, 128, FC * D)),
        "b2_0": np.concatenate([g["L0_ffn_b2"], g["L0_ffn_bs2"]], axis=0),
    }
    nc = _bacc.Bacc("TRN2", target_bir_lowering=False, num_devices=1)
    A = {n: nc.dram_tensor(f"in_{n}", a.shape, F32, kind="ExternalInput").ap() for n, a in arrays.items()}
    one_rows = np.ones((3, H, NT), ml_dtypes.bfloat16)
    arrays["one_rows"] = one_rows
    arrays["bits"] = cc(np.broadcast_to(np.append(1 << np.arange(NBITS - 1, -1, -1), 0).astype(np.int32), (128, NBITS + 1)))
    A["bits"] = nc.dram_tensor("in_bits", (128, NBITS + 1), I32, kind="ExternalInput").ap()
    arrays["causal_t"] = cc(np.stack([np.eye(128), np.where(part[None, :] < part[:, None], -BIG, 0.0)], axis=1)
                            .astype(ml_dtypes.bfloat16))
    A["causal_t"] = nc.dram_tensor("in_causal_t", (128, 2, 128), BF16, kind="ExternalInput").ap()
    A["one_rows"] = nc.dram_tensor("in_one_rows", one_rows.shape, BF16, kind="ExternalInput").ap()
    A["gates0"] = nc.dram_tensor("gates0", (E + 1, NT), F32, kind="Internal").ap()
    A["qk_parts"] = nc.dram_tensor("qk_parts", (2, 3, D, NT), BF16, kind="Internal").ap()
    A["max_rows"] = nc.dram_tensor("max_rows", (NB, 3, H, TB), BF16, kind="Internal").ap()
    A["attn_sums"] = nc.dram_tensor("attn_sums", (H, VW, NT), F32, kind="Internal").ap()
    A["gates1"] = nc.dram_tensor("gates1", (E, NT), F32, kind="Internal").ap()
    A["out"] = nc.dram_tensor("out", (D, NT), F32, kind="ExternalOutput").ap()
    build(nc, A)
    r = _run(nc, [{f"in_{n}": a for n, a in arrays.items()}], core_ids=[0])
    return cc(r.results[0]["out"].T).reshape(1, NT, D)
```

```python
from contextlib import ExitStack, contextmanager

import concourse.bass as bass
from concourse import mybir

F32 = mybir.dt.float32
BF16 = mybir.dt.bfloat16
I32 = mybir.dt.int32
ALU = mybir.AluOpType
ACT = mybir.ActivationFunctionType
AX = mybir.AxisListType

D = 128
NT = 2048
TB = 512
NB = NT // TB
NTILE = NT // 128
E = 8
F = 512
FC = F // 128
H = 16
DK = D // H
CAP = int(1.25 * NT / E)
LN_EPS = 1e-5
BIG = 3.0e38
STAGE = 6
NBITS = 30
ROUND_BITS = 3
ROUNDS = NBITS // ROUND_BITS
NCAND = 2 ** ROUND_BITS - 1
ST = -(-CAP // 128)
NO_SLOT = 2 * E * ST * 128
ROW = D + 2

TD, TF, TM, C0, C1, BQ, BK = range(7)
SA, CA, GA, SB, CB, GB = range(6)


class Shared:
    pass


def blk(b, n=TB):
    return slice(b * n, (b + 1) * n)



def ln_tensor(pe, S, k, mean_ps, var_ps):
    def mean(b):
        pe.wait_ge(S.x_ready, 4 * k + b + 1)
        if b >= 2:
            pe.wait_ge(S.ln_centered, 4 * k + b - 1)
        pe.matmul(mean_ps[b % 2][:, :], S.mean_w[:, :], S.xT[:, blk(b)], start=True, stop=True).then_inc(S.ln_mean, 1)

    mean(0)
    for b in range(NB):
        if b + 1 < NB:
            mean(b + 1)
        pe.wait_ge(S.ln_squared, 4 * k + b + 1)
        pe.matmul(var_ps[b % 2][:, :], S.mean_w[:, :], S.sq[:, b % 2, :], start=True, stop=True).then_inc(S.ln_var, 1)


def ln_scalar(act, S, k, var_ps):
    for b in range(NB):
        act.wait_ge(S.ln_centered, 4 * k + b + 1)
        if b >= 2:
            act.wait_ge(S.ln_var, 4 * k + b - 1)
        act.activation(S.sq[:, b % 2, :], S.xc[:, blk(b)], ACT.Square).then_inc(S.ln_squared, 1)
        if b >= 1:
            ln_spread(act, S, k, var_ps, b - 1)
    ln_spread(act, S, k, var_ps, NB - 1)


def ln_spread(act, S, k, var_ps, b):
    act.wait_ge(S.ln_var, 4 * k + b + 1)
    act.activation(S.sd[:, blk(b)], var_ps[b % 2][:, :], ACT.Sqrt, bias=S.eps_col[:, :]).then_inc(S.ln_sd, 1)


def ln_vector(dve, S, link, k, mean_ps, scale, shift):
    def center(b):
        dve.wait_ge(S.ln_mean, 4 * k + b + 1)
        dve.tensor_tensor(S.xc[:, blk(b)], S.xT[:, blk(b)], mean_ps[b % 2][:, :], ALU.subtract).then_inc(S.ln_centered, 1)

    center(0)
    center(1)
    for b in range(NB):
        dve.wait_ge(S.ln_sd, 4 * k + b + 1)
        link(dve.reciprocal(S.sd[:, blk(b)], S.sd[:, blk(b)]))
        link(dve.scalar_tensor_tensor(S.sd[:, blk(b)], S.xc[:, blk(b)], scale, S.sd[:, blk(b)], ALU.mult, ALU.mult))
        dve.tensor_scalar(S.hT[:, 1 + b * TB:1 + (b + 1) * TB], S.sd[:, blk(b)], shift, None, ALU.add).then_inc(S.h_ready, 1)
        if b + 2 < NB:
            center(b + 2)


def h_block(S, b):
    return S.hT[:, 1 + b * TB:1 + (b + 1) * TB]


def h_tile(S, t):
    return S.hT[:, 1 + t * 128:1 + (t + 1) * 128]


def make_link(eng, sem):
    done = [0]

    def link(ins):
        done[0] += 1
        ins.then_inc(sem, 1)
        eng.wait_ge(sem, done[0])

    return link



def stage_mix(nc, S, A):
    with ExitStack() as ctx:
        sb = lambda n, s, d=F32: ctx.enter_context(nc.sbuf_tensor(n, s, d))
        ps = lambda n: ctx.enter_context(nc.psum_tensor(n, [128, TB], F32))
        wmod = sb("wmod", [128, 2, 6 * D])
        wmix = sb("wmix", [128, 4, D])
        small = sb("small", [128, 16])
        kf = sb("kf", [128, TB])
        k_exp = sb("k_exp", [128, 2, TB])
        r_exp = sb("r_exp", [128, 2, TB])
        kv = sb("kv", [128, TB])
        xm = sb("xm", [128, 2, TB])
        mix_t = sb("mix_t", [128, TB])
        sum_kv = sb("sum_kv", [128, NT + 1])
        sum_k = sb("sum_k", [128, NT + 1])
        decay_row = sb("decay_row", [128, TB])
        wkv = sb("wkv", [128, TB])
        wk = sb("wk", [128, TB])
        rwkv = sb("rwkv", [128, 2, TB])
        mean_ps = [ps("mean0"), ps("mean1")]
        var_ps = [ps("var0"), ps("var1")]
        k_ps, v_ps, r_ps, o_ps = ps("k_ps"), ps("v_ps"), ps("r_ps"), ps("o_ps")
        decay, first, one_m_tm = small[:, 0:1], small[:, 1:2], small[:, 2:3]
        silu_c, c_exp = small[:, 4:6], small[:, 6:8]

        sem = S.sem
        w_in, c_exped, silu_done, mod_mm = sem("w_in"), sem("c_exped"), sem("silu_done"), sem("mod_mm")
        coef, xm_ready, kvr_ready, kmin_done = sem("coef"), sem("xm_ready"), sem("kvr_ready"), sem("kmin_done")
        kr_exped, kvr_read, rwkv_ready, o_ready = sem("kr_exped"), sem("kvr_read"), sem("rwkv_ready"), sem("o_ready")
        tdone = sem("tdone")
        block = ctx.enter_context(nc.Block())

        @block.sync
        def _(sp):
            sp.dma_start(S.cols[:, :], A["cols"]).then_inc(S.cols_in, 16)
            for b in range(NB):
                sp.dma_start(S.xT[:, blk(b)], A["xT"][:, blk(b)]).then_inc(S.x_in[b], 16)
            sp.dma_start(wmod[:, :, :], A["wmod"]).then_inc(w_in, 16)
            sp.dma_start(wmix[:, :, :], A["wmix"]).then_inc(w_in, 16)
            sp.dma_start(S.consts[:, :], A["consts"]).then_inc(S.const_in, 16)
            sp.dma_start(S.bits[:, :], A["bits"]).then_inc(S.const_in, 16)
            sp.dma_start(A["slots"].bitcast(I32).rearrange("(c p) w -> p c w", p=128),
                         A["empty_slot"].unsqueeze(1).to_broadcast([128, E * ST, ROW])).then_inc(S.dram_init, 16)
            sp.dma_start(A["y_sum"].bitcast(I32).rearrange("(c p) w -> p c w", p=128),
                         A["empty_slot"][:, 0:D].unsqueeze(1).to_broadcast([128, NTILE + 1, D])).then_inc(S.dram_init, 16)

        @block.tensor
        def _(pe):
            pe.wait_ge(w_in, 32)
            pe.wait_ge(silu_done, 1)
            for layer in range(2):
                for j in range(6):
                    last = pe.matmul(o_ps[:, 6 * layer + j:6 * layer + j + 1], wmod[:, layer, blk(j, 128)],
                                     silu_c[:, layer:layer + 1], start=True, stop=True)
            last.then_inc(mod_mm, 1)
            ln_tensor(pe, S, 0, mean_ps, var_ps)
            for b in range(NB + 1):
                if b < NB:
                    pe.wait_ge(xm_ready, b + 1)
                    if b >= 1:
                        pe.wait_ge(kvr_read, 3 * b)
                    for j, bank in enumerate((k_ps, v_ps, r_ps)):
                        pe.matmul(bank[:, :], wmix[:, j, :], xm[:, b % 2, :], start=True, stop=True).then_inc(kvr_ready, 1)
                if b >= 1:
                    pe.wait_ge(rwkv_ready, b)
                    if b >= 2:
                        pe.wait_ge(S.x_ready, NB + b - 1)
                    pe.matmul(o_ps[:, :], wmix[:, 3, :], rwkv[:, (b - 1) % 2, :], start=True, stop=True).then_inc(o_ready, 1)

        @block.scalar
        def _(act):
            act.wait_ge(S.cols_in, 16)
            act.activation(c_exp, S.cols[:, C0:C1 + 1], ACT.Exp, scale=-1.0).then_inc(c_exped, 1)
            act.activation(first, S.cols[:, TF:TF + 1], ACT.Exp).then_inc(coef, 1)
            act.activation(decay, S.cols[:, TD:TD + 1], ACT.Exp).then_inc(coef, 1)
            act.wait_ge(coef, 2)
            act.activation(decay, decay, ACT.Exp, scale=-1.0).then_inc(coef, 1)
            act.wait_ge(S.eps_set, 1)
            ln_scalar(act, S, 0, var_ps)
            for b in range(NB):
                if b >= 2:
                    act.wait_ge(rwkv_ready, b - 1)
                act.wait_ge(kmin_done, b + 1)
                act.activation(k_exp[:, b % 2, :], kf[:, :], ACT.Exp).then_inc(kr_exped, 1)
                act.wait_ge(kvr_ready, 3 * b + 3)
                act.activation(r_exp[:, b % 2, :], r_ps[:, :], ACT.Exp, scale=-1.0).then_inc(kvr_read, 1)

        @block.vector
        def _(dve):
            link = make_link(dve, tdone)
            link(dve.memset(S.mean_w[:, :], 1.0 / D))
            dve.memset(S.eps_col[:, :], LN_EPS).then_inc(S.eps_set, 1)
            link(dve.memset(S.hT[:, 0:1], 0.0))
            link(dve.memset(sum_kv[:, 0:1], 0.0))
            link(dve.memset(sum_k[:, 0:1], 0.0))
            link(dve.memset(decay_row[:, :], 0.0))
            for b in range(NB):
                dve.wait_ge(S.x_in[b], 16)
            dve.wait_ge(c_exped, 1)
            link(dve.tensor_scalar(c_exp, c_exp, 1.0, None, ALU.add))
            link(dve.reciprocal(c_exp, c_exp))
            dve.tensor_tensor(silu_c, S.cols[:, C0:C1 + 1], c_exp, ALU.mult).then_inc(silu_done, 1)
            dve.tensor_scalar(one_m_tm, S.cols[:, TM:TM + 1], -1.0, 1.0, ALU.mult, ALU.add).then_inc(S.x_ready, NB)
            dve.wait_ge(S.x_ready, NB)
            dve.wait_ge(coef, 3)
            link(dve.tensor_scalar(decay_row[:, :], decay_row[:, :], decay, None, ALU.add))
            dve.wait_ge(mod_mm, 1)
            link(dve.tensor_copy(S.mod[:, :], o_ps[:, 0:12]))
            mods = S.mod[:, :].rearrange("p (l m) -> p l m", l=2)
            for c in (CA, CB):
                link(dve.tensor_scalar(mods[:, :, c], mods[:, :, c], 1.0, None, ALU.add))
            for g in (GA, GB):
                sign, size = small[:, 8:10], small[:, 10:12]
                link(dve.tensor_scalar(sign, mods[:, :, g], 0.0, 2.0, ALU.is_ge, ALU.mult))
                link(dve.tensor_scalar(sign, sign, -1.0, None, ALU.add))
                link(dve.scalar_tensor_tensor(size, mods[:, :, g], -1.0, mods[:, :, g], ALU.mult, ALU.max))
                link(dve.tensor_scalar(size, size, 0.25, None, ALU.max))
                link(dve.tensor_tensor(mods[:, :, g], sign, size, ALU.mult))
            ln_vector(dve, S, link, 0, mean_ps, S.mod[:, CA:CA + 1], S.mod[:, SA:SA + 1])
            dve.wait_ge(S.h_ready, NB)

            def add_to_x(b):
                dve.wait_ge(o_ready, b + 1)
                dve.scalar_tensor_tensor(S.xT[:, blk(b)], o_ps[:, :], S.mod[:, GA:GA + 1], S.xT[:, blk(b)],
                                         ALU.mult, ALU.add).then_inc(S.x_ready, 1)

            for b in range(NB):
                link(dve.tensor_scalar(mix_t[:, :], S.hT[:, blk(b)], one_m_tm, None, ALU.mult))
                if b >= 2:
                    dve.wait_ge(kvr_ready, 3 * b - 3)
                dve.scalar_tensor_tensor(xm[:, b % 2, :], h_block(S, b), S.cols[:, TM:TM + 1], mix_t[:, :],
                                         ALU.mult, ALU.add).then_inc(xm_ready, 1)
                if b >= 1:
                    add_to_x(b - 1)
                dve.wait_ge(kvr_ready, 3 * b + 1)
                dve.tensor_scalar(kf[:, :], k_ps[:, :], 60.0, None, ALU.min).then_inc(kmin_done, 1)
                dve.wait_ge(kr_exped, b + 1)
                dve.wait_ge(kvr_ready, 3 * b + 2)
                ke = k_exp[:, b % 2, :]
                dve.tensor_tensor(kv[:, :], ke, v_ps[:, :], ALU.mult).then_inc(kvr_read, 2)
                dve.wait_ge(kvr_read, 3 * b + 3)
                new = slice(1 + b * TB, 1 + (b + 1) * TB)
                old = slice(b * TB, (b + 1) * TB)
                link(dve.tensor_tensor_scan(sum_k[:, new], decay_row[:, :], ke, sum_k[:, b * TB:b * TB + 1],
                                            ALU.mult, ALU.add))
                link(dve.tensor_tensor_scan(sum_kv[:, new], decay_row[:, :], kv[:, :], sum_kv[:, b * TB:b * TB + 1],
                                            ALU.mult, ALU.add))
                link(dve.scalar_tensor_tensor(wk[:, :], ke, first, sum_k[:, old], ALU.mult, ALU.add))
                link(dve.scalar_tensor_tensor(wkv[:, :], kv[:, :], first, sum_kv[:, old], ALU.mult, ALU.add))
                link(dve.tensor_scalar(wk[:, :], wk[:, :], 1e-9, None, ALU.add))
                link(dve.scalar_tensor_tensor(wk[:, :], r_exp[:, b % 2, :], 1.0, wk[:, :], ALU.add, ALU.mult))
                link(dve.reciprocal(wk[:, :], wk[:, :]))
                if b >= 2:
                    dve.wait_ge(o_ready, b - 1)
                dve.tensor_tensor(rwkv[:, b % 2, :], wkv[:, :], wk[:, :], ALU.mult).then_inc(rwkv_ready, 1)
            add_to_x(NB - 1)
            dve.wait_ge(S.x_ready, 2 * NB)



def router_tensor(pe, S, logits_ps, router_w, h_done, done):
    for t in range(NTILE):
        pe.wait_ge(S.h_ready, h_done + t // (NTILE // NB) + 1)
        last = pe.matmul(logits_ps[:, blk(t, E)], h_tile(S, t), router_w, start=True, stop=True)
    last.then_inc(done, 1)


def top2_vector(dve, S, link, R, to_exp, exped):
    wide = lambda a: a.unsqueeze(2).to_broadcast([128, NTILE, E])
    rev = S.rev.unsqueeze(1).to_broadcast([128, NTILE, E])
    link(dve.tensor_reduce(R.m[:, :], R.p[:, :, :], AX.X, ALU.max))
    dve.tensor_tensor(R.p[:, :, :], R.p[:, :, :], wide(R.m[:, :]), ALU.subtract).then_inc(to_exp, 1)
    dve.wait_ge(exped, 1)
    link(dve.tensor_reduce(R.m[:, :], R.p[:, :, :], AX.X, ALU.add))
    link(dve.reciprocal(R.m[:, :], R.m[:, :]))
    link(dve.tensor_tensor(R.p[:, :, :], R.p[:, :, :], wide(R.m[:, :]), ALU.mult))

    def pick(src, top, hot):
        link(dve.tensor_reduce(top, src, AX.X, ALU.max))
        link(dve.tensor_tensor(hot, src, wide(top), ALU.is_equal))
        link(dve.tensor_tensor(hot, hot, rev, ALU.mult))
        link(dve.tensor_reduce(R.m[:, :], hot, AX.X, ALU.max))
        link(dve.tensor_tensor(hot, hot, wide(R.m[:, :]), ALU.is_equal))

    pick(R.p[:, :, :], R.top1[:, :], R.sel[:, :, :])
    link(dve.scalar_tensor_tensor(R.rest[:, :, :], R.sel[:, :, :], -2.0, R.p[:, :, :], ALU.mult, ALU.add))
    pick(R.rest[:, :, :], R.top2[:, :], R.hot[:, :, :])
    link(dve.tensor_tensor(R.sel[:, :, :], R.sel[:, :, :], R.hot[:, :, :], ALU.add))


class Routing:
    def __init__(self, sb, k):
        self.p = sb(f"rt{k}_p", [128, NTILE, E])
        self.sel = sb(f"rt{k}_sel", [128, NTILE, E])
        self.hot = sb(f"rt{k}_hot", [128, NTILE, E])
        self.rest = sb(f"rt{k}_rest", [128, NTILE, E])
        self.gate = sb(f"rt{k}_gate", [128, E, NTILE])
        self.m = sb(f"rt{k}_m", [128, NTILE])
        self.top1 = sb(f"rt{k}_top1", [128, NTILE])
        self.top2 = sb(f"rt{k}_top2", [128, NTILE])



def stage_gelu_moe(nc, S, A):
    NE = E + 1
    gates_d = A["gates0"]
    with ExitStack() as ctx:
        sb = lambda n, s, d=F32: ctx.enter_context(nc.sbuf_tensor(n, s, d))
        ps = lambda n: ctx.enter_context(nc.psum_tensor(n, [128, TB], F32))
        R = Routing(sb, 0)
        wg = sb("wg0", [128, E])
        bgB = sb("bgB", [128, E])
        gate_rows = sb("gate_rows", [128, 128])
        ones_rows = sb("ones_rows", [NTILE, 128])
        gT = sb("gT", [NE, NT])
        b2 = sb("b2", [NE, D])
        w1 = [sb(f"w1_{p}", [128, F]) for p in range(2)]
        w2 = [sb(f"w2_{p}", [128, FC, D]) for p in range(2)]
        b1 = [sb(f"b1_{p}", [128, FC]) for p in range(2)]
        gB = [sb(f"gB_{p}", [128, NT]) for p in range(2)]
        hid = sb("hid", [128, 4, TB])
        gated = sb("gated", [128, 2 * FC, TB])
        y_ps = [ps(f"y{b}") for b in range(NB)]
        hid_ps = [ps(f"hid{n}") for n in range(4)]
        mean_ps, var_ps = hid_ps[0:2], hid_ps[2:4]
        logits_ps = y_ps[0][:, 0:NTILE * E]
        gate_ps = y_ps[1][:, 0:128]

        sem = S.sem
        rw_in, logits_done, to_exp, exped = sem("rw_in"), sem("logits0"), sem("to_exp0"), sem("exped0")
        gate_ready, gate_turned, rows_ready, rows_out, gT_in = (
            sem("gate0"), sem("gturn0"), sem("grow0"), sem("grow_out0"), sem("gT_in0"))
        w_in = [sem(f"w_in0_{p}") for p in range(2)]
        hid_ready, tdone = sem("hid_ready0"), sem("tdone2")
        gelu_done = sem("gelu0")
        gate_done = sem("gated0")
        gated_used = sem("used0")
        block = ctx.enter_context(nc.Block())

        @block.sync
        def _(sp):
            sp.dma_start(wg[:, :], A["wg0"]).then_inc(rw_in, 16)
            sp.dma_start(bgB[:, :], A["bg0"].to_broadcast([128, E])).then_inc(rw_in, 16)
            sp.dma_start(b2[:, :], A["b2_0"]).then_inc(rw_in, 16)

            def load_weights(e, p):
                sp.dma_start(w1[p][:, :], A["w1_0"][bass.ds(e, 1), :, :].rearrange("e p f -> (e p) f")).then_inc(w_in[p], 16)
                sp.dma_start(w2[p][:, :, :], A["w2_0"][bass.ds(e, 1), :, :].rearrange("e p (c d) -> (e p) c d", c=FC)).then_inc(w_in[p], 16)
                sp.dma_start(b1[p][:, :], A["b1_0"][bass.ds(e, 1), :, :].rearrange("e p f -> (e p) f")).then_inc(w_in[p], 16)

            def load_gate(e, p):
                sp.dma_start(gB[p][:, :], gates_d[bass.ds(e, 1), :].to_broadcast([128, NT])).then_inc(w_in[p], 16)

            load_weights(0, 0)
            load_weights(1, 1)
            sp.wait_ge(rows_ready, 1)
            sp.dma_start(gates_d[0:E, :].rearrange("e (c j) -> (e c) j", j=128), gate_rows[:, :]).then_inc(rows_out, 16)
            sp.dma_start(gates_d[E:NE, :].rearrange("e (c j) -> (e c) j", j=128), ones_rows[:, :]).then_inc(rows_out, 16)
            sp.wait_ge(rows_out, 32)
            sp.dma_start(gT[:, :], gates_d[:, :]).then_inc(gT_in, 16)
            load_gate(0, 0)
            load_gate(1, 1)

            def load(e, p):
                sp.wait_ge(gated_used, 16 * e - 8)
                load_weights(e, p)
                load_gate(e, p)

            with sp.Fori(2, E, 2) as e:
                load(e, 0)
                load(e + 1, 1)
            load(E, 0)

        @block.tensor
        def _(pe):
            ln_tensor(pe, S, 1, mean_ps, var_ps)
            pe.wait_ge(rw_in, 48)
            router_tensor(pe, S, logits_ps, wg[:, :], NB, logits_done)
            pe.wait_ge(gate_ready, 1)
            pe.transpose(gate_ps, R.gate[:, :, :].rearrange("p e c -> p (e c)"), S.ident).then_inc(gate_turned, 1)
            pe.wait_ge(rows_ready, 1)
            pe.wait_ge(gT_in, 16)
            for b in range(NB):
                pe.matmul(y_ps[b][:, :], b2[:, :], gT[:, blk(b)], start=True, stop=False, skip_group_check=True)

            def hidden(e, p, b):
                for f in range(FC):
                    n = FC * b + f
                    pe.wait_ge(gelu_done, 16 * e + n + 1)
                    pe.matmul(hid_ps[n % 4][:, :], w1[p][:, blk(f, 128)], h_block(S, b), start=True, stop=True).then_inc(hid_ready, 1)

            def back(e, p, b):
                for f in range(FC):
                    n = FC * b + f
                    pe.wait_ge(gate_done, 16 * e + n + 5)
                    pe.matmul(y_ps[b][:, :], w2[p][:, f, :], gated[:, n % (2 * FC), :], start=False,
                              stop=False, skip_group_check=True).then_inc(gated_used, 1)

            def expert(e, p, uses):
                pe.wait_ge(w_in[p], 64 * uses)
                hidden(e, p, 0)
                for b in range(NB):
                    if b + 1 < NB:
                        hidden(e, p, b + 1)
                    back(e, p, b)

            with pe.Fori(0, E // 2) as i:
                expert(2 * i, 0, i + 1)
                expert(2 * i + 1, 1, i + 1)
            expert(E, 0, E // 2 + 1)

        @block.scalar
        def _(act):
            ln_scalar(act, S, 1, var_ps)
            act.wait_ge(to_exp, 1)
            act.activation(R.p[:, :, :], R.p[:, :, :], ACT.Exp).then_inc(exped, 1)

            def expert(e, p, uses):
                act.wait_ge(w_in[p], 64 * uses)
                for n in range(4 * FC):
                    act.wait_ge(hid_ready, 16 * e + n + 1)
                    act.wait_ge(gate_done, 16 * e + n + 1)
                    act.activation(hid[:, n % 4, :], hid_ps[n % 4][:, :], ACT.Gelu,
                                   bias=b1[p][:, n % FC:n % FC + 1]).then_inc(gelu_done, 1)

            with act.Fori(0, E // 2) as i:
                expert(2 * i, 0, i + 1)
                expert(2 * i + 1, 1, i + 1)
            expert(E, 0, E // 2 + 1)

        @block.vector
        def _(dve):
            link = make_link(dve, tdone)
            link(dve.memset(ones_rows[:, :], 1.0))
            dve.memset(R.m[:, 0:1], 0.0).then_inc(gelu_done, 4)
            dve.memset(R.m[:, 1:2], 0.0).then_inc(gate_done, 4)
            dve.memset(R.m[:, 2:3], 0.0).then_inc(gated_used, 8)
            dve.wait_ge(gated_used, 8)
            ln_vector(dve, S, link, 1, mean_ps, S.mod[:, CB:CB + 1], S.mod[:, SB:SB + 1])
            dve.wait_ge(rw_in, 48)
            dve.wait_ge(logits_done, 1)
            link(dve.tensor_tensor(R.p[:, :, :], logits_ps.rearrange("p (t e) -> p t e", e=E),
                                   bgB[:, :].unsqueeze(1).to_broadcast([128, NTILE, E]), ALU.add))
            top2_vector(dve, S, link, R, to_exp, exped)
            dve.tensor_tensor(R.gate[:, :, :].rearrange("p e c -> p c e"), R.sel[:, :, :], R.p[:, :, :],
                              ALU.mult).then_inc(gate_ready, 1)
            dve.wait_ge(gate_turned, 1)
            dve.tensor_copy(gate_rows[:, :], gate_ps).then_inc(rows_ready, 1)

            def expert(e, p, uses):
                dve.wait_ge(w_in[p], 64 * uses)
                for n in range(4 * FC):
                    dve.wait_ge(gelu_done, 16 * e + n + 5)
                    dve.wait_ge(gated_used, 16 * e + n + 1)
                    dve.tensor_tensor(gated[:, n % (2 * FC), :], hid[:, n % 4, :], gB[p][:, blk(n // FC)],
                                      ALU.mult).then_inc(gate_done, 1)

            with dve.Fori(0, E // 2) as i:
                expert(2 * i, 0, i + 1)
                expert(2 * i + 1, 1, i + 1)
            expert(E, 0, E // 2 + 1)
            dve.wait_ge(gated_used, 8 + 16 * NE)
            for b in range(NB):
                dve.scalar_tensor_tensor(S.xT[:, blk(b)], y_ps[b][:, :], S.mod[:, GB:GB + 1], S.xT[:, blk(b)],
                                         ALU.mult, ALU.add).then_inc(S.x_ready, 1)
            dve.wait_ge(S.x_ready, 3 * NB)



Q_PARTS = (0, 0, 1, 1, 0, 2)
K_PARTS = (0, 1, 0, 1, 2, 0)
KP = DK * len(Q_PARTS)
KM = KP + 3
VW = DK + 1


def stage_qkv(nc, S, A):
    with ExitStack() as ctx:
        sb = lambda n, s, d=F32: ctx.enter_context(nc.sbuf_tensor(n, s, d))
        ps = lambda n: ctx.enter_context(nc.psum_tensor(n, [128, TB], F32))
        wqkv = sb("wqkv", [128, 3, D])
        bvB = sb("bvB", [128, D])
        full = sb("qk_full", [128, 2, TB])
        parts = sb("parts_sb", [128, 2, 3, TB], BF16)
        mean_ps = [ps("mean3a"), ps("mean3b")]
        var_ps = [ps("var3a"), ps("var3b")]
        qk_ps = [ps("qk0"), ps("qk1")]
        v_ps = [ps("v0"), ps("v1")]

        sem = S.sem
        w_in, qk_mm, full_done, part1, rest_done, part2, part3 = (
            sem("w_in3"), sem("qk_mm"), sem("full_done"), sem("part1"), sem("rest_done"), sem("part2"), sem("part3"))
        parts_out = [sem("q_parts_out"), sem("k_parts_out")]
        v_mm, v_done, tdone = sem("v_mm"), sem("v_done"), sem("tdone3")
        zeroed = sem("zeroed")
        block = ctx.enter_context(nc.Block())

        @block.gpsimd
        def _(pool):
            for i in range(NQ):
                for op in (S.qop, S.kop):
                    pool.memset(op[:, QUAD * i:QUAD * (i + 1), :].bitcast(I32), 0).then_inc(zeroed, 1)

        @block.sync
        def _(sp):
            sp.dma_start(wqkv[:, :, :], A["wqkv"]).then_inc(w_in, 16)
            sp.dma_start(bvB[:, :], A["bv"].to_broadcast([128, D])).then_inc(w_in, 16)
            sp.wait_ge(zeroed, 2 * NQ)
            sp.dma_start(S.kop[KP:KM, :, :], A["one_rows"]).then_inc(S.ones_in, 16)
            for n in range(2 * NB):
                sp.wait_ge(part3, n + 1)
                sp.dma_start(A["qk_parts"][n % 2].rearrange("s p t -> p s t")[:, :, blk(n // 2)],
                             parts[:, n % 2, :, :]).then_inc(parts_out[n % 2], 16)
            for q_or_k in parts_out:
                sp.wait_ge(q_or_k, 16 * NB)
            for rest, heads in enumerate((slice(0, QUAD), slice(QUAD, H))):
                for j, (op, which) in enumerate(((S.qop, Q_PARTS), (S.kop, K_PARTS))):
                    for r, s in enumerate(which):
                        sp.dma_start(op[DK * r:DK * (r + 1), heads, :],
                                     A["qk_parts"][j, s].rearrange("(h d) t -> d h t", d=DK)[:, heads, :]).then_inc(S.ops_in[rest], 16)

        @block.tensor
        def _(pe):
            ln_tensor(pe, S, 2, mean_ps, var_ps)
            pe.wait_ge(w_in, 32)
            for b in range(NB):
                pe.wait_ge(S.h_ready, 2 * NB + b + 1)
                for j in range(2):
                    n = 2 * b + j
                    if n >= 2:
                        pe.wait_ge(full_done, n - 1)
                    pe.matmul(qk_ps[j][:, :], wqkv[:, j, :], h_block(S, b), start=True, stop=True).then_inc(qk_mm, 1)
                if b >= 2:
                    pe.wait_ge(v_done, b - 1)
                for u in range(TB // 128):
                    last = pe.matmul(v_ps[b % 2][:, blk(u, 128)], h_tile(S, 4 * b + u), wqkv[:, 2, :], start=True, stop=True)
                last.then_inc(v_mm, 1)

        @block.scalar
        def _(act):
            ln_scalar(act, S, 2, var_ps)
            for n in range(2 * NB):
                act.wait_ge(full_done, n + 1)
                if n >= 2:
                    act.wait_ge(parts_out[n % 2], 16 * (n // 2))
                act.activation(parts[:, n % 2, 0, :], full[:, n % 2, :], ACT.Copy).then_inc(part1, 1)
                act.wait_ge(rest_done, n + 1)
                act.activation(parts[:, n % 2, 1, :], full[:, n % 2, :], ACT.Copy).then_inc(part2, 1)

        @block.vector
        def _(dve):
            link = make_link(dve, tdone)
            link(dve.memset(S.v_all[:, :, :, DK:VW], 1.0))
            ln_vector(dve, S, link, 2, mean_ps, S.mod[:, 6 + CA:7 + CA], S.mod[:, 6 + SA:7 + SA])
            dve.wait_ge(w_in, 32)
            for b in range(NB):
                for j in range(2):
                    n = 2 * b + j
                    dve.wait_ge(qk_mm, n + 1)
                    if n >= 2:
                        dve.wait_ge(part3, n - 1)
                    x = full[:, n % 2, :]
                    dve.tensor_scalar(x, qk_ps[j][:, :], S.cols[:, BQ + j:BQ + j + 1], None, ALU.add).then_inc(full_done, 1)
                dve.wait_ge(v_mm, b + 1)
                dve.tensor_tensor(S.v_all[:, 4 * b:4 * b + 4, :, 0:DK],
                                  v_ps[b % 2][:, :].rearrange("p (t h d) -> p t h d", t=4, d=DK),
                                  bvB[:, :].rearrange("p (h d) -> p h d", d=DK).unsqueeze(1).to_broadcast([128, 4, H, DK]),
                                  ALU.add).then_inc(v_done, 1)
                for j in range(2):
                    n = 2 * b + j
                    x = full[:, n % 2, :]
                    dve.wait_ge(part1, n + 1)
                    dve.tensor_tensor(x, x, parts[:, n % 2, 0, :], ALU.subtract).then_inc(rest_done, 1)
                for j in range(2):
                    n = 2 * b + j
                    dve.wait_ge(part2, n + 1)
                    dve.tensor_tensor(parts[:, n % 2, 2, :], full[:, n % 2, :], parts[:, n % 2, 1, :],
                                      ALU.subtract).then_inc(part3, 1)



QUAD = 4
LEAD_16THS = 8.5
NQ = H // QUAD
RING = 4
STEPS = [(g, kt, max(0, kt - 4 * g) * 128) for g in range(NB) for kt in range(4 * g + 4)]
TURN_DELAY = 3
CHUNKS = []
for _g in range(NB):
    _block = [("chunk", _t, _j, _c, 128 * (_c * (_t + 1) // (_g + 1)), 128 * ((_c + 1) * (_t + 1) // (_g + 1)))
              for _t in range(4 * _g, 4 * _g + 4) for _j in range(QUAD) for _c in range(_g + 1)]
    CHUNKS += _block if _g == 0 else _block[:TURN_DELAY] + [("turn", _g - 1)] + _block[TURN_DELAY:]
CHUNKS.append(("turn", NB - 1))
BLOCK_LAST = [max(n for n, c in enumerate(CHUNKS) if c[0] == "chunk" and c[1] // 4 == g) for g in range(NB)]
NS, NCH = len(STEPS), len(CHUNKS)
CHUNK_COST = [c[5] - c[4] + 64 if c[0] == "chunk" else 64 for c in CHUNKS]
CHUNK_COST[-1] = 2048
LEAD = next(n for n in range(NCH) if 16 * sum(CHUNK_COST[:n]) >= LEAD_16THS * sum(CHUNK_COST))


def chunks_by_step():
    order = [(n, 0) for n in range(LEAD, NCH)] + [(n, 1) for n in range(LEAD)]
    step_cost = [TB - off for _, _, off in STEPS]
    total = sum(CHUNK_COST)
    done, at, spent, out = 0, 0, 0, []
    for cost in step_cost:
        done += cost
        first = at
        while at < NCH and (spent + CHUNK_COST[order[at][0]] // 2) * sum(step_cost) <= done * total:
            spent += CHUNK_COST[order[at][0]]
            at += 1
        out.append(order[first:at])
    out[-1] += order[at:]
    return out


V_FIRST = 12


def early(eng, value):
    if not isinstance(value, int):
        eng.compute_val(value)


def stage_attention(nc, S, A):
    with ExitStack() as ctx:
        sb = lambda n, s, d=F32: ctx.enter_context(nc.sbuf_tensor(n, s, d))
        ps = lambda n, w=TB: ctx.enter_context(nc.psum_tensor(n, [128, w], F32))
        mask, masked = S.sd[:, blk(0)], (S.sd[:, blk(1)], S.sd[:, blk(2)], S.sd[:, blk(3)], S.xc[:, blk(2)])
        o_sb = S.xc[:, 0:2 * TB].rearrange("p (a t) -> p a t", a=2)
        chunk_max = sb("chunk_max", [128, QUAD, NTILE, NB])
        causal_t = sb("causal_t", [128, 2, 128], BF16)
        neg_max = sb("neg_max", [128, QUAD, 4])
        max_rest = sb("max_rest", [QUAD * 4, 128])
        max_parts = sb("max_parts", [QUAD * 4, 2, 3, 128], BF16)
        probs = sb("probs", [128, 2, QUAD, TB])
        v_quad = sb("v_quad", [128, NTILE, QUAD, VW])
        max_ps = [ps(f"max{n}") for n in range(RING)]
        st_ps = [ps(f"st{n}") for n in range(3)]
        o_ps = ps("o_acc")
        qop = S.qop[:, :, :].rearrange("p h t -> p (h t)")
        kop = S.kop[:, :, :].rearrange("p h t -> p (h t)")

        sem = S.sem
        mask_in, causal_in = sem("mask_in"), sem("causal_in")
        scores_ready = sem("scores_ready")
        max_bank_free = sem("max_bank_free")
        max_stored, neg_max_ready, max_parts_ready = sem("max_stored"), sem("neg_max"), sem("max_parts")
        max_rows_in = [sem("max_rows_in0"), sem("max_rows_in1")]
        st_ready = sem("st_ready")
        st_free = sem("st_free")
        probs_free = sem("probs_free")
        v_ready, o_out = sem("v_ready"), [sem("o_out0"), sem("o_out1")]
        o_free = sem("o_free")
        block = ctx.enter_context(nc.Block())

        last_step = [max(s for s, x in enumerate(STEPS) if x[0] == g) for g in range(NB)]
        plan = chunks_by_step()

        @block.sync
        def _(sp):
            sp.dma_start(mask, A["causal"]).then_inc(mask_in, 16)
            sp.dma_start(causal_t[:, :, :], A["causal_t"]).then_inc(causal_in, 16)

            def max_rows(i, g):
                sp.wait_ge(max_parts_ready, NB * i + g + 1)
                rows = A["max_rows"][g, :, bass.ds(QUAD * i, QUAD), :]
                sp.dma_start(rows.rearrange("s j (t q) -> (j t) s q", q=128),
                             max_parts[:, g % 2, :, :]).then_inc(max_stored, 16)
                sp.wait_ge(max_stored, i * (16 * NB) + 16 * (g + 1))
                sp.dma_start(S.qop[KP:KM, bass.ds(QUAD * i, QUAD), blk(g)], rows).then_inc(max_rows_in[g % 2], 16)

            def store(i, g):
                sp.wait_ge(o_free, NB * i + g + 2)
                for j in range(QUAD):
                    sp.dma_start(A["attn_sums"][bass.ds(QUAD * i + j, 1), :, blk(g)].rearrange("o v t -> (o v) t"),
                                 o_sb[32 * j:32 * j + VW, g % 2, :]).then_inc(o_out[g % 2], 16)

            max_rows(0, 0)
            max_rows(0, 1)
            with sp.Fori(0, NQ - 1) as i:
                max_rows(i, 2)
                store(i, 0)
                store(i, 1)
                max_rows(i, 3)
                max_rows(i + 1, 0)
                store(i, 2)
                max_rows(i + 1, 1)
                store(i, 3)
            max_rows(NQ - 1, 2)
            store(NQ - 1, 0)
            store(NQ - 1, 1)
            max_rows(NQ - 1, 3)
            store(NQ - 1, 2)
            store(NQ - 1, 3)
            for half in o_out:
                sp.wait_ge(half, 8 * QUAD * NB * NQ)

        @block.tensor
        def _(pe):
            pe.wait_ge(S.ones_in, 16)
            pe.wait_ge(causal_in, 16)
            pe.wait_ge(S.const_in, 32)

            @contextmanager
            def quad_offset(i, s):
                if isinstance(i, int):
                    yield i * (QUAD * NT)
                    return
                reg = pe.alloc_register(f"quad_offset{s}")
                pe.reg_mov(reg, i * (QUAD * NT))
                yield pe.snap(reg, min_val=0, max_val=(NQ - 2) * QUAD * NT)
                pe.free_register(reg)

            def chunk(at, i, ahead, n):
                pe.wait_ge(max_bank_free, i * NCH + (ahead * NCH + n + 1))
                bank = max_ps[n % RING]
                if CHUNKS[n][0] == "turn":
                    g = CHUNKS[n][1]
                    pe.wait_ge(neg_max_ready, i * NB + (ahead * NB + g + 1))
                    pe.transpose(bank[0:4 * QUAD, 0:128], neg_max[:, :, :].rearrange("p j t -> p (j t)"),
                                 S.ident).then_inc(scores_ready, 1)
                    return
                _, t, j, _, key, end = CHUNKS[n]
                head = (ahead * QUAD + j) * NT
                pe.matmul(bank[:, 0:end - key], qop[:, bass.ds(at + (head + 128 * t), 128)],
                          kop[:, bass.ds(at + (head + key), end - key)], start=True, stop=True).then_inc(scores_ready, 1)

            def scores(at, i, s, j):
                g, kt, off = STEPS[s]
                if kt == 0 and j == 0:
                    pe.wait_ge(max_rows_in[g % 2], i * (8 * NB) + 16 * (g // 2 + 1))
                n = QUAD * s + j
                pe.wait_ge(st_free, i * (QUAD * NS) + max(n + 1, 3))
                own = kt >= 4 * g
                last = pe.matmul(st_ps[n % 3][:, off:TB], kop[:, bass.ds(at + (j * NT + 128 * kt), 128)],
                                 qop[:, bass.ds(at + (j * NT + TB * g + off), TB - off)],
                                 start=True, stop=not own)
                if own:
                    last = pe.matmul(st_ps[n % 3][:, off:off + 128], causal_t[:, 0, :], causal_t[:, 1, :],
                                     start=False, stop=True)
                last.then_inc(st_ready, 1)

            def products(i, s):
                g, kt, off = STEPS[s]
                if s == 0:
                    pe.wait_ge(v_ready, 2 * i + 1)
                if kt == V_FIRST and g == NB - 1:
                    pe.wait_ge(v_ready, 2 * i + 2)
                if kt == 0:
                    pe.wait_ge(o_free, NB * i + g + 1)
                pe.wait_ge(st_free, i * (QUAD * NS) + QUAD * (s + 1) + 3)
                for j in range(QUAD):
                    last = pe.matmul(o_ps[32 * j:32 * j + VW, off:TB], v_quad[:, kt, j, :], probs[:, s % 2, j, off:TB],
                                     start=(kt == 0), stop=(kt == 4 * g + 3))
                last.then_inc(probs_free, 1)

            pe.wait_ge(S.ops_in[0], 12 * 16)
            for n in range(LEAD):
                chunk(0, 0, 0, n)
            pe.wait_ge(S.ops_in[1], 12 * 16)

            def quad(i, next_too):
                for s in range(NS):
                    beside = [c for c in plan[s] if next_too or not c[1]]
                    with quad_offset(i, s) as at:
                        for j in range(QUAD):
                            scores(at, i, s, j)
                            for n, ahead in beside[j * len(beside) // QUAD:(j + 1) * len(beside) // QUAD]:
                                chunk(at, i, ahead, n)
                            if j == 2 and s:
                                products(i, s - 1)
                products(i, NS - 1)

            with pe.Fori(0, NQ - 1) as i:
                quad(i, True)
            quad(NQ - 1, False)

        @block.vector
        def _(dve):
            dve.memset(chunk_max[:, :, :, :], -BIG).then_inc(max_bank_free, RING)
            dve.memset(neg_max[:, 0, 0:1], 0.0).then_inc(st_free, 3)
            dve.memset(o_ps[:, :], 0.0).then_inc(o_free, 1)
            dve.memset(neg_max[:, 0, 1:2], 0.0).then_inc(probs_free, 2)
            dve.wait_ge(max_bank_free, RING)

            def maxima(i, first):
                for n, c in enumerate(CHUNKS):
                    if c[0] == "turn":
                        split_maxima(i, first, n, c[1])
                        continue
                    early(dve, NCH * i + n + 1)
                    dve.wait_ge(mask_in, 16)
                    dve.wait_ge(scores_ready, NCH * i + n + 1)
                    bank = max_ps[n % RING]
                    _, t, j, k, key, end = c
                    width = end - key
                    out = chunk_max[:, j, t, k:k + 1]
                    if end == 128 * (t + 1):
                        dve.tensor_tensor_reduce(masked[n % RING][:, 0:width], bank[:, 0:width], mask[:, TB - width:TB], 1.0,
                                                 -BIG, ALU.add, ALU.max, out).then_inc(max_bank_free, 1)
                    else:
                        dve.tensor_reduce(out, bank[:, 0:width], AX.X, ALU.max).then_inc(max_bank_free, 1)
                    if n in BLOCK_LAST:
                        g = BLOCK_LAST.index(n)
                        dve.wait_ge(max_bank_free, NCH * i + n + 1 + RING)
                        dve.tensor_reduce(neg_max[:, :, :], chunk_max[:, :, 4 * g:4 * g + 4, :], AX.X, ALU.max,
                                          negate=True).then_inc(neg_max_ready, 1)

            def split_maxima(i, first, n, g):
                dve.wait_ge(scores_ready, NCH * i + n + 1)
                if not (first and g < 2):
                    dve.wait_ge(max_rows_in[g % 2], i * (8 * NB) + 16 * (g // 2))
                parts = max_parts[:, g % 2, :, :]
                turned = max_ps[n % RING][0:4 * QUAD, 0:128]
                dve.tensor_copy(parts[:, 0, :], turned).then_inc(S.split, 1)
                dve.wait_ge(S.split, i * (2 * NB) + 2 * g + 1)
                dve.tensor_tensor(max_rest[:, :], turned, parts[:, 0, :], ALU.subtract).then_inc(max_bank_free, 1)
                dve.wait_ge(max_bank_free, NCH * i + n + 1 + RING)
                dve.tensor_copy(parts[:, 1, :], max_rest[:, :]).then_inc(S.split, 1)
                dve.wait_ge(S.split, i * (2 * NB) + 2 * g + 2)
                dve.tensor_tensor(parts[:, 2, :], max_rest[:, :], parts[:, 1, :], ALU.subtract).then_inc(max_parts_ready, 1)
                early(dve, NB * i + g + 1)
                dve.wait_ge(mask_in, 16)
                dve.wait_ge(max_parts_ready, NB * i + g + 1)

            maxima(0, True)
            with dve.Fori(1, NQ) as i:
                maxima(i, False)

        @block.scalar
        def _(act):
            def quad(i, first):
                for s, (g, kt, off) in enumerate(STEPS):
                    act.wait_ge(probs_free, NS * i + s + 1)
                    for j in range(QUAD):
                        n = QUAD * s + j
                        act.wait_ge(st_ready, i * (QUAD * NS) + n + 1)
                        act.activation(probs[:, s % 2, j, off:TB], st_ps[n % 3][:, off:TB], ACT.Exp,
                                       scale=DK ** -0.5).then_inc(st_free, 1)
                    if kt == 0 and g:
                        copy_sums(i, g - 1, first)
                copy_sums(i, NB - 1, first)

            def copy_sums(i, g, first):
                act.wait_ge(probs_free, NS * i + last_step[g] + 3)
                if not (first and g < 2):
                    act.wait_ge(o_out[g % 2], i * (32 * NB) + 64 * (g // 2))
                act.activation(o_sb[:, g % 2, :], o_ps[:, :], ACT.Copy).then_inc(o_free, 1)

            quad(0, True)
            with act.Fori(1, NQ) as i:
                quad(i, False)

        @block.gpsimd
        def _(pool):
            def gather(i, tiles):
                pool.tensor_copy(v_quad[:, tiles, :, :], S.v_all[:, tiles, bass.ds(QUAD * i, QUAD), :]).then_inc(v_ready, 1)

            first, rest = slice(0, V_FIRST), slice(V_FIRST, NTILE)
            gather(0, first)
            gather(0, rest)
            with pool.Fori(1, NQ) as i:
                pool.wait_ge(probs_free, NS * i + (V_FIRST - NTILE + 2))
                gather(i, first)
                pool.wait_ge(probs_free, NS * i + 2)
                gather(i, rest)



def stage_attention_out(nc, S, A):
    with ExitStack() as ctx:
        sb = lambda n, s, d=F32: ctx.enter_context(nc.sbuf_tensor(n, s, d))
        num = sb("num", [128, NT])
        den = sb("den", [128, NT])
        sums_in = [S.sem(f"sums_in{b}") for b in range(NB)]
        tdone = S.sem("tdone5a")
        block = ctx.enter_context(nc.Block())

        @block.sync
        def _(sp):
            for b in range(NB):
                sp.dma_start(num[:, blk(b)], A["attn_sums"][:, 0:DK, blk(b)]).then_inc(sums_in[b], 16)
                sp.dma_start(den[:, blk(b)], A["attn_sums"][:, DK:VW, blk(b)].to_broadcast([H, DK, TB])).then_inc(sums_in[b], 16)

        @block.vector
        def _(dve):
            link = make_link(dve, tdone)
            for b in range(NB):
                dve.wait_ge(sums_in[b], 32)
                link(dve.reciprocal(den[:, blk(b)], den[:, blk(b)]))
                link(dve.scalar_tensor_tensor(num[:, blk(b)], num[:, blk(b)], S.mod[:, 6 + GA:7 + GA], den[:, blk(b)],
                                              ALU.mult, ALU.mult))
                dve.tensor_tensor(S.xT[:, blk(b)], S.xT[:, blk(b)], num[:, blk(b)], ALU.add).then_inc(S.x_ready, 1)
            dve.wait_ge(S.x_ready, 4 * NB)



def stage_swiglu_moe(nc, S, A):
    with ExitStack() as ctx:
        sb = lambda n, s, d=F32: ctx.enter_context(nc.sbuf_tensor(n, s, d))
        ps = lambda n: ctx.enter_context(nc.psum_tensor(n, [128, TB], F32))
        R = Routing(sb, 1)
        wr = sb("wr1", [128, E])
        token_id = sb("token_id", [128, NTILE], I32)
        w_t = sb("w_t", [128, 128])
        reach = sb("reach", [128, NCAND, 128])
        reached = sb("reached", [128, NCAND])
        hit = sb("hit", [128, 128])
        tie = sb("tie", [128, 128])
        rank = sb("rank", [128, 128])
        count = sb("count", [128, NCAND])
        need = sb("need", [128, 1])
        step = sb("step", [128, 1])
        bits = sb("found_bits", [128, 1], I32)
        thr = sb("thr", [128, 1], I32)
        cand = sb("cand", [128, NCAND], I32)
        slot_f = sb("slot_f", [128, 2, NTILE])
        slot = sb("slot", [128, 2, NTILE], I32)
        token_rows = sb("token_rows", [128, NTILE, 2, ROW])
        slot_rows = sb("slot_rows", [128, E * ST, ROW])
        x_slots = sb("x_slots", [128, E, ST * 128])
        ids = [sb(f"ids_{p}", [128, ST], I32) for p in range(2)]
        y_rows = [sb(f"y_rows_{p}", [128, ST, D]) for p in range(2)]
        y_tok = sb("y_tok", [128, NTILE, D])
        wg = [sb(f"wgt_{p}", [128, F]) for p in range(2)]
        wu = [sb(f"wup_{p}", [128, F]) for p in range(2)]
        wd = [sb(f"wdn_{p}", [128, FC, D]) for p in range(2)]
        act_g = sb("act_g", [128, 2, CAP])
        gated = sb("gated1", [128, 2 * FC, CAP])
        g_ps = [ps("g_ps0"), ps("g_ps1")]
        u_ps = [ps("u_ps0"), ps("u_ps1")]
        y_ps = [ps("y_ps0"), ps("y_ps1")]
        t_ps = [ps("t_ps0"), ps("t_ps1")]
        mean_ps, var_ps = g_ps, u_ps
        four_ps = g_ps + u_ps
        logits_ps = y_ps[0][:, 0:NTILE * E]
        turn_ps = y_ps[1][:, 0:128]
        total_ps = t_ps[0]
        slot_ps = t_ps[1][:, 0:128]
        slot_base = S.consts[:, 392 + ROUNDS:393 + ROUNDS]

        sem = S.sem
        rw_in, logits_done, to_exp, exped = sem("rw_in1"), sem("logits1"), sem("to_exp1"), sem("exped1")
        h_turned, h_first, h_rows = sem("h_turned"), sem("h_first"), sem("h_rows")
        weights_ready, turned, slots_ready, slots_turned = sem("weights1"), sem("turned1"), sem("slots1"), sem("slots_turned")
        tags_ready, slot_ready, scattered = sem("tags_ready"), sem("slot_ready"), sem("scattered")
        counted, totalled = sem("counted"), sem("totalled")
        rows_in = [sem(f"slot_rows_in{i}") for i in range(E // 2)]
        x_turned, x_copied = sem("x_turned"), sem("x_copied")
        gu_in = [sem(f"gu_in{p}") for p in range(2)]
        d_in = [sem(f"d_in{p}") for p in range(2)]
        up_ready, silu_done = sem("up_ready"), sem("silu_done1")
        gate_done = sem("gated1_done")
        y_ready = sem("y_ready")
        y_scaled = sem("y_scaled")
        scaled, added = sem("scaled"), sem("added")
        y_in = [sem(f"y_in{b}") for b in range(NB)]
        y_turned = sem("y_turned")
        tdone, tloop = sem("tdone6"), sem("bit_steps")
        stored = sem("stored")
        block = ctx.enter_context(nc.Block())

        @block.sync
        def _(sp):
            sp.dma_start(wr[:, :], A["wr1"]).then_inc(rw_in, 16)
            sp.dma_start(token_id[:, :], A["token_id"]).then_inc(rw_in, 16)

            def load_gu(e, p):
                sp.dma_start(wg[p][:, :], A["wg_1"][bass.ds(e, 1), :, :].rearrange("e p f -> (e p) f")).then_inc(gu_in[p], 16)
                sp.dma_start(wu[p][:, :], A["wu_1"][bass.ds(e, 1), :, :].rearrange("e p f -> (e p) f")).then_inc(gu_in[p], 16)

            def load_d(e, p):
                sp.dma_start(wd[p][:, :, :], A["wd_1"][bass.ds(e, 1), :, :].rearrange("e p (c d) -> (e p) c d", c=FC)).then_inc(d_in[p], 16)

            for p in range(2):
                load_gu(p, p)
                load_d(p, p)
            sp.wait_ge(scattered, 2 * NTILE * 16)
            for i in range(E // 2):
                sp.dma_start(slot_rows[:, blk(i, 2 * ST), :],
                             A["slots"][blk(i, 2 * ST * 128), :].rearrange("(c p) w -> p c w", p=128)).then_inc(rows_in[i], 16)
            with sp.Fori(0, E // 2 - 1) as i:
                for p in range(2):
                    sp.wait_ge(up_ready, i * (2 * FC) + FC * (p + 1))
                    load_gu(2 * i + (2 + p), p)
                    sp.wait_ge(y_ready, i * 2 + (p + 1))
                    load_d(2 * i + (2 + p), p)
            sp.wait_ge(added, ST * 16 * E)
            for b in range(NB):
                sp.dma_start(y_tok[:, blk(b, NTILE // NB), :],
                             A["y_sum"][blk(b), :].rearrange("(c p) d -> p c d", p=128)).then_inc(y_in[b], 16)
            for b in range(NB):
                sp.wait_ge(S.x_ready, 4 * NB + b + 1)
                sp.dma_start(A["out"][:, blk(b)], S.xT[:, blk(b)]).then_inc(stored, 16)
            sp.wait_ge(stored, 16 * NB)

        @block.tensor
        def _(pe):
            ln_tensor(pe, S, 3, mean_ps, var_ps)
            pe.wait_ge(rw_in, 32)
            router_tensor(pe, S, logits_ps, wr[:, :], 3 * NB, logits_done)
            for b in range(NB):
                for u in range(4):
                    last = pe.transpose(four_ps[b][:, blk(u, 128)], h_tile(S, 4 * b + u), S.ident)
                last.then_inc(h_turned, 1)
            pe.wait_ge(weights_ready, 1)
            pe.transpose(turn_ps, R.gate[:, :, :].rearrange("p e c -> p (e c)"), S.ident).then_inc(turned, 1)

            def total(n, weights, width):
                pe.wait_ge(counted, n)
                pe.matmul(total_ps[:, 0:width], weights, count[:, 0:width], start=True, stop=True).then_inc(totalled, 1)

            total(NCAND, S.same_expert, NCAND)
            with pe.Fori(1, ROUNDS) as r:
                total(r * NCAND + NCAND, S.same_expert, NCAND)
            total(ROUNDS * NCAND + 1, S.same_expert, 1)
            total(ROUNDS * NCAND + 2, S.earlier_tile, 1)
            total(ROUNDS * NCAND + 3, S.earlier_tile, 1)
            pe.wait_ge(slots_ready, 1)
            pe.transpose(slot_ps, rank[:, :], S.ident).then_inc(slots_turned, 1)
            pe.wait_ge(slot_ready, 2)

            for e in range(E):
                if e % 2 == 0:
                    pe.wait_ge(rows_in[e // 2], 16)
                if e >= 2:
                    pe.wait_ge(x_copied, e - 1)
                for c in range(ST):
                    last = pe.transpose(t_ps[e % 2][:, blk(c, 128)], slot_rows[:, ST * e + c, 0:D], S.ident)
                last.then_inc(x_turned, 1)
            pe.wait_ge(x_copied, E)
            pe.wait_ge(h_rows, NB)

            def hidden(i, k):
                p = k % 2
                x = x_slots[:, :, :].rearrange("p e s -> p (e s)")[:, bass.ds(i * (2 * ST * 128) + k * (ST * 128), CAP)]
                pe.wait_ge(gu_in[p], i * 32 + 32 * (k // 2 + 1))
                for f in range(FC):
                    pe.wait_ge(gate_done, i * (2 * FC) + (FC * k + f + 1))
                    pe.matmul(g_ps[f % 2][:, 0:CAP], wg[p][:, blk(f, 128)], x, start=True, stop=True)
                    pe.matmul(u_ps[f % 2][:, 0:CAP], wu[p][:, blk(f, 128)], x, start=True, stop=True).then_inc(up_ready, 1)

            def back(i, p):
                pe.wait_ge(d_in[p], i * 16 + 16)
                pe.wait_ge(y_scaled, i * 2 + (p + 1))
                pe.wait_ge(gate_done, i * (2 * FC) + (FC * p + FC + 2))
                for c in range(ST):
                    n = min(128, CAP - 128 * c)
                    for f in range(FC):
                        last = pe.matmul(y_ps[p][0:n, blk(c, D)], gated[:, FC * p + f, 128 * c:128 * c + n], wd[p][:, f, :],
                                         start=(f == 0), stop=(f == FC - 1))
                last.then_inc(y_ready, 1)

            hidden(0, 0)
            with pe.Fori(0, E // 2 - 1) as i:
                hidden(i, 1)
                back(i, 0)
                hidden(i, 2)
                back(i, 1)
            last_pair = E // 2 - 1
            hidden(last_pair, 1)
            back(last_pair, 0)
            back(last_pair, 1)

            for b in range(NB):
                pe.wait_ge(y_in[b], 16)
                for u in range(4):
                    last = pe.transpose(four_ps[b][:, blk(u, 128)], y_tok[:, 4 * b + u, :], S.ident)
                last.then_inc(y_turned, 1)

        @block.scalar
        def _(act):
            ln_scalar(act, S, 3, var_ps)
            act.wait_ge(to_exp, 1)
            act.activation(R.p[:, :, :], R.p[:, :, :], ACT.Exp).then_inc(exped, 1)
            for b in range(NB):
                act.wait_ge(h_turned, b + 1)
                for k in range(2):
                    ins = act.activation(token_rows[:, blk(b, 4), k, 0:D],
                                         four_ps[b][:, :].rearrange("p (c d) -> p c d", d=D), ACT.Copy)
                    if k == 0:
                        ins.then_inc(h_first, 1)
                    else:
                        ins.then_inc(h_rows, 1)
            for e in range(E):
                act.wait_ge(x_turned, e + 1)
                act.activation(x_slots[:, e, :], t_ps[e % 2][:, 0:ST * 128], ACT.Copy).then_inc(x_copied, 1)
            with act.Fori(0, E // 2) as i:
                for n in range(2 * FC):
                    act.wait_ge(gate_done, i * (2 * FC) + (n + 1))
                    act.wait_ge(up_ready, i * (2 * FC) + (n + 1))
                    act.activation(act_g[:, n % 2, :], g_ps[n % 2][:, 0:CAP], ACT.Silu).then_inc(silu_done, 1)

        @block.vector
        def _(dve):
            link = make_link(dve, tdone)
            dve.memset(R.m[:, 0:1], 0.0).then_inc(gate_done, 2)
            dve.memset(R.m[:, 1:2], 0.0).then_inc(y_scaled, 2)
            dve.wait_ge(gate_done, 2)
            dve.wait_ge(y_scaled, 2)
            ln_vector(dve, S, link, 3, mean_ps, S.mod[:, 6 + CB:7 + CB], S.mod[:, 6 + SB:7 + SB])
            dve.wait_ge(logits_done, 1)
            link(dve.tensor_copy(R.p[:, :, :], logits_ps.rearrange("p (t e) -> p t e", e=E)))
            top2_vector(dve, S, link, R, to_exp, exped)
            link(dve.tensor_tensor(R.rest[:, :, :], R.sel[:, :, :], R.hot[:, :, :], ALU.subtract))
            link(dve.tensor_tensor(R.m[:, :], R.top1[:, :], R.top2[:, :], ALU.add))
            link(dve.tensor_scalar(R.m[:, :], R.m[:, :], 1e-6, None, ALU.add))
            link(dve.reciprocal(R.m[:, :], R.m[:, :]))
            link(dve.tensor_tensor(R.p[:, :, :], R.p[:, :, :], R.m[:, :].unsqueeze(2).to_broadcast([128, NTILE, E]), ALU.mult))
            link(dve.tensor_tensor(R.p[:, :, :], R.p[:, :, :], R.sel[:, :, :], ALU.mult))
            link(dve.tensor_scalar(R.sel[:, :, :], R.sel[:, :, :], -1.0, None, ALU.add))
            dve.tensor_tensor(R.gate[:, :, :].rearrange("p e c -> p c e"), R.p[:, :, :], R.sel[:, :, :],
                              ALU.add).then_inc(weights_ready, 1)
            for k, top in enumerate((R.top1, R.top2)):
                dve.tensor_tensor(token_rows[:, :, k, D], top[:, :], R.m[:, :], ALU.mult).then_inc(tags_ready, 1)
                dve.wait_ge(rw_in, 32)
                dve.tensor_copy(token_rows[:, :, k, D + 1].bitcast(I32), token_id[:, :]).then_inc(tags_ready, 1)
            dve.wait_ge(turned, 1)
            link(dve.tensor_copy(w_t[:, :], turn_ps))
            link(dve.memset(thr[:, :], 0))
            link(dve.tensor_copy(cand[:, :], S.bits[:, 0:NCAND]))

            with dve.Fori(0, ROUNDS) as r:
                for j in range(NCAND):
                    dve.tensor_scalar(reach[:, j, :], w_t[:, :], cand[:, j:j + 1].bitcast(F32), None, ALU.is_ge, ALU.add,
                                      accum_out=count[:, j:j + 1]).then_inc(counted, 1)
                dve.wait_ge(totalled, r + 1)
                dve.tensor_scalar(reached[:, :], total_ps[:, 0:NCAND], float(CAP), None, ALU.is_ge, ALU.add,
                                  accum_out=step[:, :]).then_inc(tloop, 1)
                dve.wait_ge(tloop, r * 4 + 1)
                dve.tensor_scalar(bits[:, :], step[:, :], S.consts[:, bass.ds(r + 392, 1)], None, ALU.mult).then_inc(tloop, 1)
                dve.wait_ge(tloop, r * 4 + 2)
                dve.tensor_tensor(thr[:, :], thr[:, :], bits[:, :], ALU.bitwise_or).then_inc(tloop, 1)
                dve.wait_ge(tloop, r * 4 + 3)
                dve.tensor_tensor(cand[:, :], S.bits[:, bass.ds(r * NCAND + NCAND, NCAND)],
                                  thr[:, :].to_broadcast([128, NCAND]), ALU.bitwise_or).then_inc(tloop, 1)
                dve.wait_ge(tloop, r * 4 + 4)
            link(dve.tensor_scalar(hit[:, :], w_t[:, :], thr[:, :].bitcast(F32), None, ALU.is_gt))
            dve.tensor_scalar(tie[:, :], hit[:, :], 1.0, None, ALU.mult, ALU.add, accum_out=count[:, 0:1]).then_inc(counted, 1)
            dve.wait_ge(totalled, ROUNDS + 1)
            link(dve.tensor_scalar(need[:, :], total_ps[:, 0:1], -1.0, float(CAP), ALU.mult, ALU.add))
            link(dve.tensor_scalar(tie[:, :], w_t[:, :], thr[:, :].bitcast(F32), None, ALU.is_equal))
            link(dve.tensor_tensor_scan(rank[:, :], tie[:, :], tie[:, :], 0.0, ALU.add, ALU.max))
            dve.tensor_copy(count[:, 0:1], rank[:, 127:128]).then_inc(counted, 1)
            dve.wait_ge(totalled, ROUNDS + 2)
            link(dve.tensor_tensor(need[:, :], need[:, :], total_ps[:, 0:1], ALU.subtract))
            link(dve.tensor_scalar(rank[:, :], rank[:, :], need[:, :], None, ALU.is_le))
            link(dve.tensor_tensor(tie[:, :], tie[:, :], rank[:, :], ALU.mult))
            link(dve.tensor_tensor(hit[:, :], hit[:, :], tie[:, :], ALU.add))
            link(dve.tensor_tensor_scan(rank[:, :], hit[:, :], hit[:, :], 0.0, ALU.add, ALU.max))
            dve.tensor_copy(count[:, 0:1], rank[:, 127:128]).then_inc(counted, 1)
            dve.wait_ge(totalled, ROUNDS + 3)
            link(dve.tensor_tensor(need[:, :], slot_base, total_ps[:, 0:1], ALU.add))
            dve.scalar_tensor_tensor(rank[:, :], rank[:, :], need[:, :], hit[:, :], ALU.add, ALU.mult).then_inc(slots_ready, 1)
            dve.wait_ge(slots_turned, 1)
            for k, hot in enumerate((R.rest, R.hot)):
                link(dve.tensor_tensor(R.p[:, :, :], hot[:, :, :], slot_ps.rearrange("p (e c) -> p c e", e=E), ALU.mult))
                link(dve.tensor_reduce(slot_f[:, k, :], R.p[:, :, :], AX.X, ALU.add))
                dve.tensor_scalar(slot[:, k, :], slot_f[:, k, :], float(NO_SLOT), None, ALU.add).then_inc(slot_ready, 1)

            def gate(i, k):
                for f in range(FC):
                    n = FC * k + f
                    dve.wait_ge(silu_done, i * (2 * FC) + (n + 1))
                    dve.tensor_tensor(gated[:, n % (2 * FC), :], act_g[:, f % 2, :], u_ps[f % 2][:, 0:CAP],
                                      ALU.mult).then_inc(gate_done, 1)

            def scale(i, p, first):
                dve.wait_ge(y_ready, i * 2 + (p + 1))
                if not first:
                    dve.wait_ge(added, i * (2 * ST * 16) + ST * 16 * (p - 1))
                at = i * (2 * ST) + p * ST
                dve.tensor_copy(ids[p][:, :], slot_rows[:, bass.ds(at, ST), D + 1].bitcast(I32)).then_inc(scaled, 1)
                for c in range(ST):
                    n = min(128, CAP - 128 * c)
                    ins = dve.tensor_scalar(y_rows[p][0:n, c, :], y_ps[p][0:n, blk(c, D)],
                                            slot_rows[0:n, bass.ds(at + c, 1), D], None, ALU.mult)
                    ins.then_inc(y_scaled if c == ST - 1 else scaled, 1)

            gate(0, 0)
            gate(0, 1)
            scale(0, 0, True)
            gate(0, 2)
            scale(0, 1, True)
            with dve.Fori(1, E // 2 - 1) as i:
                gate(i, 1)
                scale(i, 0, False)
                gate(i, 2)
                scale(i, 1, False)
            gate(E // 2 - 1, 1)
            scale(E // 2 - 1, 0, False)
            scale(E // 2 - 1, 1, False)
            for b in range(NB):
                dve.wait_ge(y_turned, b + 1)
                dve.scalar_tensor_tensor(S.xT[:, blk(b)], four_ps[b][:, :], S.mod[:, 6 + GB:7 + GB], S.xT[:, blk(b)],
                                         ALU.mult, ALU.add).then_inc(S.x_ready, 1)

        @block.gpsimd
        def _(pool):
            pool.wait_ge(S.dram_init, 32)
            pool.wait_ge(tags_ready, 4)
            pool.wait_ge(h_first, NB)
            pool.wait_ge(h_rows, NB)
            for k in range(2):
                pool.wait_ge(slot_ready, k + 1)
                for t in range(NTILE):
                    pool.indirect_dma_start(A["slots"], bass.IndirectOffsetOnAxis(slot[:, k, t:t + 1], 0), token_rows[:, t, k, :], None,
                                            bounds_check=E * ST * 128 - 1, oob_is_err=False).then_inc(scattered, 16)

            with pool.Fori(0, E // 2) as i:
                for p in range(2):
                    early(pool, i * 2 + (p + 3))
                    early(pool, i * (2 * ST) + ST * (p + 1))
                    pool.wait_ge(S.dram_init, 32)
                    pool.wait_ge(y_scaled, i * 2 + (p + 3))
                    pool.wait_ge(scaled, i * (2 * ST) + ST * (p + 1))
                    for c in range(ST):
                        n = min(128, CAP - 128 * c)
                        pool.indirect_dma_start(A["y_sum"], bass.IndirectOffsetOnAxis(ids[p][0:n, c:c + 1], 0), y_rows[p][0:n, c, :], None,
                                                compute_op=ALU.add).then_inc(added, 16)
                    pool.wait_ge(added, i * (2 * ST * 16) + ST * 16 * (p + 1))



def stage_store(nc, S, A):
    with ExitStack() as ctx:
        stored = S.sem("stored")
        block = ctx.enter_context(nc.Block())

        @block.sync
        def _(sp):
            sp.wait_ge(S.const_in, 32)
            sp.dma_start(A["out"], S.xT[:, :]).then_inc(stored, 16)
            sp.wait_ge(stored, 16)



def build(nc, A):
    with ExitStack() as ctx:
        S = Shared()
        sb = lambda n, s, d=F32: ctx.enter_context(nc.sbuf_tensor(n, s, d))
        S.sem = lambda n: ctx.enter_context(nc.semaphore(n))
        S.xT = sb("xT_s", [128, NT])
        S.hT = sb("hT_s", [128, NT + 1])
        S.xc = sb("xc_s", [128, NT])
        S.sd = sb("sd_s", [128, NT])
        S.sq = sb("sq_s", [128, 2, TB])
        S.cols = sb("cols_s", [128, 7])
        S.mod = sb("mod_s", [128, 12])
        S.eps_col = sb("eps_col", [128, 1])
        S.mean_w = sb("mean_w", [128, 128])
        S.consts = sb("consts_s", [128, A["consts"].shape[1]])
        S.ident = S.consts[:, 0:128]
        S.same_expert = S.consts[:, 128:256]
        S.earlier_tile = S.consts[:, 256:384]
        S.rev = S.consts[:, 384:392]
        S.bits = sb("bits", [128, (ROUNDS + 1) * NCAND], I32)
        S.cols_in, S.const_in, S.ones_in, S.eps_set = S.sem("cols_in"), S.sem("const_in"), S.sem("ones_in"), S.sem("eps_set")
        S.dram_init = S.sem("dram_init")
        S.x_ready, S.h_ready = S.sem("x_ready"), S.sem("h_ready")
        S.ln_mean, S.ln_centered, S.ln_squared = S.sem("ln_mean"), S.sem("ln_centered"), S.sem("ln_squared")
        S.ln_var, S.ln_sd = S.sem("ln_var"), S.sem("ln_sd")
        S.x_in = [S.sem(f"x_in{b}") for b in range(NB)]
        stage_mix(nc, S, A)
        if STAGE >= 2:
            stage_gelu_moe(nc, S, A)
        if STAGE >= 4:
            with ExitStack() as ctx34:
                sb34 = lambda n, s, d=F32: ctx34.enter_context(nc.sbuf_tensor(n, s, d))
                S.qop = sb34("qop", [128, H, NT], BF16)
                S.kop = sb34("kop", [128, H, NT], BF16)
                S.v_all = sb34("v_all", [128, NTILE, H, VW])
                S.ops_in, S.split = [S.sem("ops_in0"), S.sem("ops_in1")], S.sem("max_split")
                stage_qkv(nc, S, A)
                stage_attention(nc, S, A)
            stage_attention_out(nc, S, A)
        if STAGE >= 6:
            stage_swiglu_moe(nc, S, A)
            return
        stage_store(nc, S, A)


def kernel(**inputs):
    import numpy as np
    import ml_dtypes
    import concourse.bacc as _bacc
    from concourse.bass_utils import run_bass_kernel_spmd as _run

    g = {k: np.asarray(v) for k, v in inputs.items()}
    f32 = np.float32
    col = lambda n: g[n].reshape(D)
    cc = np.ascontiguousarray
    part = np.arange(128)
    causal = np.zeros((128, TB), f32)
    causal[:, TB - 128:] = np.where(part[None, :] > part[:, None], -BIG, 0.0)
    consts = np.concatenate([
        np.eye(128, dtype=f32),
        (part[:, None] // 16 == part[None, :] // 16).astype(f32),
        ((part[:, None] // 16 == part[None, :] // 16) & (part[:, None] % 16 < part[None, :] % 16)).astype(f32),
        np.broadcast_to(np.arange(E, 0, -1).astype(f32), (128, E)),
        np.broadcast_to(2.0 ** np.arange(NBITS - ROUND_BITS, -1, -ROUND_BITS, dtype=f32), (128, ROUNDS)),
        (part[:, None] // 16 * ST * 128 - 1 - NO_SLOT).astype(f32),
    ], axis=1)
    arrays = {
        "xT": cc(g["L0_attn_x"][0].T),
        "cols": cc(np.stack([col("L0_attn_time_decay"), col("L0_attn_time_first"), col("L0_attn_time_mix"),
                             col("L0_c"), col("L1_c"), col("L1_attn_bq"), col("L1_attn_bk")], axis=1)),
        "wmod": cc(np.stack([g["L0_wmod"], g["L1_wmod"]], axis=1)),
        "wmix": cc(np.stack([g[f"L0_attn_W{n}"].T for n in "kvro"], axis=1)),
        "consts": consts,
        "causal": causal,
        "wqkv": cc(np.stack([g[f"L1_attn_W{n}"].T for n in "qkv"], axis=1)),
        "bv": g["L1_attn_bv"].reshape(1, D),
        "wg0": g["L0_ffn_Wg"],
        "bg0": g["L0_ffn_bg"].reshape(1, E),
        "w1_0": np.concatenate([g["L0_ffn_W1"], g["L0_ffn_Ws1"]], axis=0),
        "w2_0": cc(np.concatenate([g["L0_ffn_W2"], g["L0_ffn_Ws2"]], axis=0).reshape(E + 1, FC, 128, D)
                   .transpose(0, 2, 1, 3).reshape(E + 1, 128, FC * D)),
        "b1_0": cc(np.concatenate([g["L0_ffn_b1"], g["L0_ffn_bs1"]], axis=0).reshape(E + 1, FC, 128).transpose(0, 2, 1)),
        "wr1": cc(g["L1_ffn_router_w"].T),
        "wg_1": g["L1_ffn_wg"],
        "wu_1": g["L1_ffn_wu"],
        "wd_1": cc(g["L1_ffn_wd"].reshape(E, FC, 128, D).transpose(0, 2, 1, 3).reshape(E, 128, FC * D)),
        "b2_0": np.concatenate([g["L0_ffn_b2"], g["L0_ffn_bs2"]], axis=0),
    }
    nc = _bacc.Bacc("TRN2", target_bir_lowering=False, num_devices=1)
    A = {n: nc.dram_tensor(f"in_{n}", a.shape, F32, kind="ExternalInput").ap() for n, a in arrays.items()}
    one_rows = np.ones((3, H, NT), ml_dtypes.bfloat16)
    arrays["one_rows"] = one_rows
    round_bits = np.arange(1, NCAND + 1)[None, :] << np.arange(NBITS - ROUND_BITS, -1, -ROUND_BITS)[:, None]
    int_arrays = {
        "bits": np.broadcast_to(np.append(round_bits.reshape(-1), [0] * NCAND).astype(np.int32), (128, (ROUNDS + 1) * NCAND)),
        "token_id": part[:, None] + 128 * np.arange(NTILE)[None, :],
        "empty_slot": np.where(np.arange(ROW)[None, :] == ROW - 1, NT + part[:, None], 0),
    }
    for n, a in int_arrays.items():
        arrays[n] = cc(a.astype(np.int32))
        A[n] = nc.dram_tensor(f"in_{n}", a.shape, I32, kind="ExternalInput").ap()
    arrays["causal_t"] = cc(np.stack([np.eye(128), np.where(part[None, :] < part[:, None], -BIG, 0.0)], axis=1)
                            .astype(ml_dtypes.bfloat16))
    A["causal_t"] = nc.dram_tensor("in_causal_t", (128, 2, 128), BF16, kind="ExternalInput").ap()
    A["one_rows"] = nc.dram_tensor("in_one_rows", one_rows.shape, BF16, kind="ExternalInput").ap()
    A["gates0"] = nc.dram_tensor("gates0", (E + 1, NT), F32, kind="Internal").ap()
    A["qk_parts"] = nc.dram_tensor("qk_parts", (2, 3, D, NT), BF16, kind="Internal").ap()
    A["max_rows"] = nc.dram_tensor("max_rows", (NB, 3, H, TB), BF16, kind="Internal").ap()
    A["attn_sums"] = nc.dram_tensor("attn_sums", (H, VW, NT), F32, kind="Internal").ap()
    A["slots"] = nc.dram_tensor("slots", (E * ST * 128, ROW), F32, kind="Internal").ap()
    A["y_sum"] = nc.dram_tensor("y_sum", (NT + 128, D), F32, kind="Internal").ap()
    A["out"] = nc.dram_tensor("out", (D, NT), F32, kind="ExternalOutput").ap()
    build(nc, A)
    r = _run(nc, [{f"in_{n}": a for n, a in arrays.items()}], core_ids=[0])
    return cc(r.results[0]["out"].T).reshape(1, NT, D)
```

```python
from contextlib import ExitStack, contextmanager

import concourse.bass as bass
from concourse import mybir

F32 = mybir.dt.float32
BF16 = mybir.dt.bfloat16
I32 = mybir.dt.int32
ALU = mybir.AluOpType
ACT = mybir.ActivationFunctionType
AX = mybir.AxisListType

D = 128
NT = 2048
TB = 512
NB = NT // TB
NTILE = NT // 128
E = 8
F = 512
FC = F // 128
H = 16
DK = D // H
CAP = int(1.25 * NT / E)
LN_EPS = 1e-5
BIG = 3.0e38
QUAD = 4
NQ = H // QUAD
NBITS = 30
ROUND_BITS = 3
ROUNDS = NBITS // ROUND_BITS
NCAND = 2 ** ROUND_BITS - 1
ST = -(-CAP // 128)
NO_SLOT = 2 * E * ST * 128
ROW = D + 2
XW = 256
XT = 2 * NT // XW + E - 1
XB = 4
WX = F + FC * D + FC + D

TD, TF, TM, C0, C1, BQ, BK = range(7)
SA, CA, GA, SB, CB, GB = range(6)


class Shared:
    pass


def blk(b, n=TB):
    return slice(b * n, (b + 1) * n)



def ln_tensor(pe, S, k, mean_ps, var_ps):
    def mean(b):
        pe.wait_ge(S.x_ready, 4 * k + b + 1)
        if b >= 2:
            pe.wait_ge(S.ln_centered, 4 * k + b - 1)
        pe.matmul(mean_ps[b % 2][:, :], S.mean_w[:, :], S.xT[:, blk(b)], start=True, stop=True).then_inc(S.ln_mean, 1)

    def variance(b):
        pe.wait_ge(S.ln_squared, 4 * k + b + 1)
        if b >= 2:
            pe.wait_ge(S.h_ready, 4 * k + b - 1)
        for u in range(4):
            last = pe.matmul(var_ps[b % 2][:, u:u + 1], S.sq[:, b % 2, blk(u, 128)], S.mean_w[:, 0:1], start=True, stop=True)
        last.then_inc(S.ln_var, 1)

    def spread(b):
        pe.wait_ge(S.ln_inverse, 4 * k + b + 1)
        for u in range(4):
            last = pe.matmul(var_ps[b % 2][:, blk(u, 128)], S.inv_sd[:, 4 * b + u:4 * b + u + 1].to_broadcast([128, 128]),
                             S.ident, start=True, stop=True)
        last.then_inc(S.ln_spread, 1)

    if k == 0:
        pe.wait_ge(S.const_in, 32)
    mean(0)
    mean(1)
    for b in range(NB):
        variance(b)
        if b + 2 < NB:
            mean(b + 2)
        if b:
            spread(b - 1)
    spread(NB - 1)


def ln_scalar(act, S, k, var_ps):
    def root(b):
        act.wait_ge(S.ln_var, 4 * k + b + 1)
        act.activation(S.inv_sd[:, blk(b, 4)], var_ps[b % 2][:, 0:4], ACT.Sqrt, bias=S.eps_col[:, :]).then_inc(S.ln_sd, 1)

    for b in range(NB):
        act.wait_ge(S.ln_centered, 4 * k + b + 1)
        if b >= 2:
            act.wait_ge(S.ln_var, 4 * k + b - 1)
        act.activation(S.sq[:, b % 2, :], S.xc[:, blk(b)], ACT.Square).then_inc(S.ln_squared, 1)
        if b:
            root(b - 1)
    root(NB - 1)


def ln_vector(dve, S, link, k, mean_ps, var_ps, scale, shift):
    def center(b):
        dve.wait_ge(S.ln_mean, 4 * k + b + 1)
        dve.tensor_tensor(S.xc[:, blk(b)], S.xT[:, blk(b)], mean_ps[b % 2][:, :], ALU.subtract).then_inc(S.ln_centered, 1)

    def inverse(b):
        dve.wait_ge(S.ln_sd, 4 * k + b + 1)
        dve.reciprocal(S.inv_sd[:, blk(b, 4)], S.inv_sd[:, blk(b, 4)]).then_inc(S.ln_inverse, 1)

    center(0)
    center(1)
    inverse(0)
    for b in range(NB):
        if b + 2 < NB:
            center(b + 2)
        if b + 1 < NB:
            inverse(b + 1)
        dve.wait_ge(S.ln_centered, 4 * k + b + 1)
        dve.wait_ge(S.ln_spread, 4 * k + b + 1)
        link(dve.scalar_tensor_tensor(S.sd[:, blk(b)], S.xc[:, blk(b)], scale, var_ps[b % 2][:, :], ALU.mult, ALU.mult))
        dve.tensor_scalar(S.hT[:, 1 + b * TB:1 + (b + 1) * TB], S.sd[:, blk(b)], shift, None, ALU.add).then_inc(S.h_ready, 1)


def h_block(S, b):
    return S.hT[:, 1 + b * TB:1 + (b + 1) * TB]


def h_tile(S, t):
    return S.hT[:, 1 + t * 128:1 + (t + 1) * 128]


def make_link(eng, S):
    def link(ins):
        S.linked += 1
        ins.then_inc(S.link_sem, 1)
        eng.wait_ge(S.link_sem, S.linked)

    return link



def stage_mix(nc, S, A):
    with ExitStack() as ctx:
        sb = lambda n, s, d=F32: ctx.enter_context(nc.sbuf_tensor(n, s, d))
        ps = lambda n: ctx.enter_context(nc.psum_tensor(n, [128, TB], F32))
        wmod = sb("wmod", [128, 2, 6 * D])
        wmix = sb("wmix", [128, 4, D])
        small = sb("small", [128, 16])
        kf = sb("kf", [128, TB])
        k_exp = sb("k_exp", [128, 2, TB])
        r_exp = sb("r_exp", [128, 2, TB])
        kv = sb("kv", [128, TB])
        xm = sb("xm", [128, 2, TB])
        mix_t = sb("mix_t", [128, 2, TB])
        r_plus_1 = sb("r_plus_1", [128, 2, TB])
        sum_kv = sb("sum_kv", [128, NT + 1])
        sum_k = sb("sum_k", [128, NT + 1])
        decay_row = sb("decay_row", [128, TB])
        wkv = sb("wkv", [128, TB])
        wk = sb("wk", [128, TB])
        rwkv = sb("rwkv", [128, 2, TB])
        mean_ps = [ps("mean0"), ps("mean1")]
        var_ps = [ps("var0"), ps("var1")]
        k_ps, v_ps, r_ps, o_ps = ps("k_ps"), ps("v_ps"), ps("r_ps"), ps("o_ps")
        decay, first, one_m_tm = small[:, 0:1], small[:, 1:2], small[:, 2:3]
        silu_c, c_exp = small[:, 4:6], small[:, 6:8]

        sem = S.sem
        w_in, c_exped, silu_done, mod_mm = sem("w_in"), sem("c_exped"), sem("silu_done"), sem("mod_mm")
        coef, xm_ready, kvr_ready, kmin_done = sem("coef"), sem("xm_ready"), sem("kvr_ready"), sem("kmin_done")
        kr_exped, kvr_read, rwkv_ready, o_ready = sem("kr_exped"), sem("kvr_read"), sem("rwkv_ready"), sem("o_ready")
        mixed, r_plus = sem("mixed"), sem("r_plus")
        block = ctx.enter_context(nc.Block())

        @block.gpsimd
        def _(pool):
            pool.wait_ge(S.x_ready, NB)
            for b in range(NB + 1):
                if b < NB:
                    pool.wait_ge(S.h_ready, b + 1)
                    if b >= 2:
                        pool.wait_ge(xm_ready, b - 1)
                    pool.tensor_scalar(mix_t[:, b % 2, :], S.hT[:, blk(b)], one_m_tm, None, ALU.mult).then_inc(mixed, 1)
                if b >= 1:
                    pool.wait_ge(kvr_read, 3 * b)
                    if b >= 3:
                        pool.wait_ge(rwkv_ready, b - 2)
                    pool.tensor_scalar(r_plus_1[:, (b - 1) % 2, :], r_exp[:, (b - 1) % 2, :], 1.0, None, ALU.add).then_inc(r_plus, 1)

        @block.sync
        def _(sp):
            sp.dma_start(S.cols[:, :], A["cols"]).then_inc(S.cols_in, 16)
            for b in range(NB):
                sp.dma_start(S.xT[:, blk(b)], A["xT"][:, blk(b)]).then_inc(S.x_in[b], 16)
            sp.dma_start(wmod[:, :, :], A["wmod"]).then_inc(w_in, 16)
            sp.dma_start(S.consts[:, :], A["consts"]).then_inc(S.const_in, 16)
            sp.dma_start(S.bits[:, :], A["bits"]).then_inc(S.const_in, 16)
            sp.dma_start(wmix[:, :, :], A["wmix"]).then_inc(w_in, 16)
            sp.dma_start(A["slots"].bitcast(I32).rearrange("(e r) w -> r e w", e=E),
                         A["empty_slots"].unsqueeze(1).to_broadcast([ST * 128, E, ROW])).then_inc(S.dram_init, 16)
            sp.dma_start(A["slots0"].bitcast(I32).rearrange("(e r) w -> r e w", r=XW),
                         A["empty_slots"][0:XW, :].unsqueeze(1).to_broadcast([XW, XT, ROW])).then_inc(S.dram_init, 16)
            sp.dma_start(A["y_sum0"].bitcast(I32).rearrange("(c p) w -> p c w", p=128),
                         A["empty_slots"][0:128, 0:D].unsqueeze(1).to_broadcast([128, NTILE + ST, D])).then_inc(S.dram_init, 16)
            sp.dma_start(A["y_sum"].bitcast(I32).rearrange("(c p) w -> p c w", p=128),
                         A["empty_slots"][0:128, 0:D].unsqueeze(1).to_broadcast([128, NTILE + ST, D])).then_inc(S.dram_init, 16)

        @block.tensor
        def _(pe):
            pe.wait_ge(w_in, 32)
            pe.wait_ge(silu_done, 1)
            for layer in range(2):
                for j in range(6):
                    last = pe.matmul(o_ps[:, 6 * layer + j:6 * layer + j + 1], wmod[:, layer, blk(j, 128)],
                                     silu_c[:, layer:layer + 1], start=True, stop=True)
            last.then_inc(mod_mm, 1)
            ln_tensor(pe, S, 0, mean_ps, var_ps)
            for b in range(NB + 1):
                if b < NB:
                    pe.wait_ge(xm_ready, b + 1)
                    if b >= 1:
                        pe.wait_ge(kvr_read, 3 * b)
                    for j, bank in enumerate((k_ps, v_ps, r_ps)):
                        pe.matmul(bank[:, :], wmix[:, j, :], xm[:, b % 2, :], start=True, stop=True).then_inc(kvr_ready, 1)
                if b >= 1:
                    pe.wait_ge(rwkv_ready, b)
                    if b >= 2:
                        pe.wait_ge(S.x_ready, NB + b - 1)
                    pe.matmul(o_ps[:, :], wmix[:, 3, :], rwkv[:, (b - 1) % 2, :], start=True, stop=True).then_inc(o_ready, 1)

        @block.scalar
        def _(act):
            act.wait_ge(S.cols_in, 16)
            act.activation(c_exp, S.cols[:, C0:C1 + 1], ACT.Exp, scale=-1.0).then_inc(c_exped, 1)
            act.activation(first, S.cols[:, TF:TF + 1], ACT.Exp).then_inc(coef, 1)
            act.activation(decay, S.cols[:, TD:TD + 1], ACT.Exp).then_inc(coef, 1)
            act.wait_ge(coef, 2)
            act.activation(decay, decay, ACT.Exp, scale=-1.0).then_inc(coef, 1)
            act.wait_ge(S.eps_set, 1)
            ln_scalar(act, S, 0, var_ps)
            for b in range(NB):
                if b >= 2:
                    act.wait_ge(rwkv_ready, b - 1)
                    act.wait_ge(r_plus, b - 1)
                act.wait_ge(kmin_done, b + 1)
                act.activation(k_exp[:, b % 2, :], kf[:, :], ACT.Exp).then_inc(kr_exped, 1)
                act.wait_ge(kvr_ready, 3 * b + 3)
                act.activation(r_exp[:, b % 2, :], r_ps[:, :], ACT.Exp, scale=-1.0).then_inc(kvr_read, 1)

        @block.vector
        def _(dve):
            link = make_link(dve, S)
            link(dve.memset(S.mean_w[:, :], 1.0 / D))
            dve.memset(S.eps_col[:, :], LN_EPS).then_inc(S.eps_set, 1)
            link(dve.memset(S.hT[:, 0:1], 0.0))
            link(dve.memset(sum_kv[:, 0:1], 0.0))
            link(dve.memset(sum_k[:, 0:1], 0.0))
            link(dve.memset(decay_row[:, :], 0.0))
            for b in range(NB):
                dve.wait_ge(S.x_in[b], 16)
            dve.wait_ge(c_exped, 1)
            link(dve.tensor_scalar(c_exp, c_exp, 1.0, None, ALU.add))
            link(dve.reciprocal(c_exp, c_exp))
            dve.tensor_tensor(silu_c, S.cols[:, C0:C1 + 1], c_exp, ALU.mult).then_inc(silu_done, 1)
            dve.tensor_scalar(one_m_tm, S.cols[:, TM:TM + 1], -1.0, 1.0, ALU.mult, ALU.add).then_inc(S.x_ready, NB)
            dve.wait_ge(S.x_ready, NB)
            dve.wait_ge(coef, 3)
            link(dve.tensor_scalar(decay_row[:, :], decay_row[:, :], decay, None, ALU.add))
            dve.wait_ge(mod_mm, 1)
            link(dve.tensor_copy(S.mod[:, :], o_ps[:, 0:12]))
            mods = S.mod[:, :].rearrange("p (l m) -> p l m", l=2)
            for c in (CA, CB):
                link(dve.tensor_scalar(mods[:, :, c], mods[:, :, c], 1.0, None, ALU.add))
            for g in (GA, GB):
                sign, size = small[:, 8:10], small[:, 10:12]
                link(dve.tensor_scalar(sign, mods[:, :, g], 0.0, 2.0, ALU.is_ge, ALU.mult))
                link(dve.tensor_scalar(sign, sign, -1.0, None, ALU.add))
                link(dve.scalar_tensor_tensor(size, mods[:, :, g], -1.0, mods[:, :, g], ALU.mult, ALU.max))
                link(dve.tensor_scalar(size, size, 0.25, None, ALU.max))
                link(dve.tensor_tensor(mods[:, :, g], sign, size, ALU.mult))
            ln_vector(dve, S, link, 0, mean_ps, var_ps, S.mod[:, CA:CA + 1], S.mod[:, SA:SA + 1])
            dve.wait_ge(S.h_ready, NB)

            def add_to_x(b):
                dve.wait_ge(o_ready, b + 1)
                dve.scalar_tensor_tensor(S.xT[:, blk(b)], o_ps[:, :], S.mod[:, GA:GA + 1], S.xT[:, blk(b)],
                                         ALU.mult, ALU.add).then_inc(S.x_ready, 1)

            def mix(b):
                dve.wait_ge(mixed, b + 1)
                if b >= 2:
                    dve.wait_ge(kvr_ready, 3 * b - 3)
                dve.scalar_tensor_tensor(xm[:, b % 2, :], h_block(S, b), S.cols[:, TM:TM + 1], mix_t[:, b % 2, :],
                                         ALU.mult, ALU.add).then_inc(xm_ready, 1)

            def bound_k(b):
                dve.wait_ge(kvr_ready, 3 * b + 1)
                dve.tensor_scalar(kf[:, :], k_ps[:, :], 60.0, None, ALU.min).then_inc(kmin_done, 1)

            mix(0)
            mix(1)
            bound_k(0)
            for b in range(NB):
                dve.wait_ge(kr_exped, b + 1)
                dve.wait_ge(kvr_ready, 3 * b + 2)
                ke = k_exp[:, b % 2, :]
                dve.wait_ge(kmin_done, b + 1)
                dve.tensor_tensor(kv[:, :], ke, v_ps[:, :], ALU.mult).then_inc(kvr_read, 2)
                dve.wait_ge(kvr_read, 3 * b + 3)
                new = slice(1 + b * TB, 1 + (b + 1) * TB)
                old = slice(b * TB, (b + 1) * TB)
                link(dve.tensor_tensor_scan(sum_k[:, new], decay_row[:, :], ke, sum_k[:, b * TB:b * TB + 1],
                                            ALU.mult, ALU.add))
                link(dve.tensor_tensor_scan(sum_kv[:, new], decay_row[:, :], kv[:, :], sum_kv[:, b * TB:b * TB + 1],
                                            ALU.mult, ALU.add))
                if b + 1 < NB:
                    bound_k(b + 1)
                link(dve.scalar_tensor_tensor(wk[:, :], ke, first, sum_k[:, old], ALU.mult, ALU.add))
                link(dve.scalar_tensor_tensor(wkv[:, :], kv[:, :], first, sum_kv[:, old], ALU.mult, ALU.add))
                dve.wait_ge(r_plus, b + 1)
                link(dve.scalar_tensor_tensor(wk[:, :], wk[:, :], 1e-9, r_plus_1[:, b % 2, :], ALU.add, ALU.mult))
                link(dve.reciprocal(wk[:, :], wk[:, :]))
                if b >= 2:
                    dve.wait_ge(o_ready, b - 1)
                dve.tensor_tensor(rwkv[:, b % 2, :], wkv[:, :], wk[:, :], ALU.mult).then_inc(rwkv_ready, 1)
                dve.wait_ge(rwkv_ready, b + 1)
                if b + 2 < NB:
                    mix(b + 2)
                if b >= 1:
                    add_to_x(b - 1)
            add_to_x(NB - 1)
            dve.wait_ge(S.x_ready, 2 * NB)



def router_tensor(pe, S, logits_ps, router_w, h_done, done):
    for t in range(NTILE):
        pe.wait_ge(S.h_ready, h_done + t // (NTILE // NB) + 1)
        last = pe.matmul(logits_ps[:, blk(t, E)], h_tile(S, t), router_w, start=True, stop=True)
    last.then_inc(done, 1)


def top2_vector(dve, S, link, R, to_exp, exped):
    wide = lambda a: a.unsqueeze(2).to_broadcast([128, NTILE, E])
    rev = S.rev.unsqueeze(1).to_broadcast([128, NTILE, E])
    link(dve.tensor_reduce(R.m[:, :], R.p[:, :, :], AX.X, ALU.max))
    dve.tensor_tensor(R.p[:, :, :], R.p[:, :, :], wide(R.m[:, :]), ALU.subtract).then_inc(to_exp, 1)
    dve.wait_ge(exped, 1)
    link(dve.tensor_reduce(R.m[:, :], R.p[:, :, :], AX.X, ALU.add))
    link(dve.reciprocal(R.m[:, :], R.m[:, :]))
    link(dve.tensor_tensor(R.p[:, :, :], R.p[:, :, :], wide(R.m[:, :]), ALU.mult))

    def pick(src, top, hot):
        link(dve.tensor_reduce(top, src, AX.X, ALU.max))
        link(dve.tensor_tensor(hot, src, wide(top), ALU.is_equal))
        link(dve.tensor_tensor(hot, hot, rev, ALU.mult))
        link(dve.tensor_reduce(R.m[:, :], hot, AX.X, ALU.max))
        link(dve.tensor_tensor(hot, hot, wide(R.m[:, :]), ALU.is_equal))

    pick(R.p[:, :, :], R.top1[:, :], R.sel[:, :, :])
    link(dve.scalar_tensor_tensor(R.rest[:, :, :], R.sel[:, :, :], -2.0, R.p[:, :, :], ALU.mult, ALU.add))
    pick(R.rest[:, :, :], R.top2[:, :], R.hot[:, :, :])
    link(dve.tensor_tensor(R.sel[:, :, :], R.sel[:, :, :], R.hot[:, :, :], ALU.add))


class Routing:
    def __init__(self, sb, k):
        self.p = sb(f"rt{k}_p", [128, NTILE, E])
        self.sel = sb(f"rt{k}_sel", [128, NTILE, E])
        self.hot = sb(f"rt{k}_hot", [128, NTILE, E])
        self.rest = sb(f"rt{k}_rest", [128, NTILE, E])
        self.gate = sb(f"rt{k}_gate", [128, E, NTILE])
        self.m = sb(f"rt{k}_m", [128, NTILE])
        self.top1 = sb(f"rt{k}_top1", [128, NTILE])
        self.top2 = sb(f"rt{k}_top2", [128, NTILE])



def stage_gelu_moe(nc, S, A):
    with ExitStack() as ctx:
        sb = lambda n, s, d=F32: ctx.enter_context(nc.sbuf_tensor(n, s, d))
        ps = lambda n: ctx.enter_context(nc.psum_tensor(n, [128, TB], F32))
        R = Routing(sb, 0)
        wr = sb("wg0", [128, E])
        bgB = sb("bgB", [128, E])
        token_id = sb("token_id0", [128, NTILE], I32)
        b2s = sb("b2s", [1, D])
        one_row = sb("one_row", [1, TB])
        hit = sb("hit0", [128, 128])
        rank = sb("rank0", [128, 128])
        count = sb("count0", [128, 1])
        tiles = sb("tiles0", [128, 1])
        base = sb("base0", [128, 1])
        fits = sb("fits0", [128, E])
        passed = sb("passed0", [128, XT + XB])
        w_row = sb("w_row", [128, XT + XB], I32)
        slot_f = sb("slot_f0", [128, 2, NTILE])
        slot = sb("slot0", [128, 2, NTILE], I32)
        token_rows = sb("token_rows0", [128, NTILE, 2, ROW])
        slot_rows = sb("slot_rows0", [128, 2 * XT, ROW])
        x_slots = sb("x_slots0", [128, XT * XW])
        ws = sb("w_shared", [128, WX])
        wx = [sb(f"wx_{p}", [128, WX]) for p in range(XB)]
        w_next = [sb(f"w_next_{p}", [128, 1], I32) for p in range(XB)]
        ids = [sb(f"ids0_{p}", [128, 2], I32) for p in range(2)]
        y_tmp = sb("y_tmp", [128, 2, D])
        y_rows = [sb(f"y_rows0_{p}", [128, 2, D]) for p in range(2)]
        hid_sb = sb("hid_sb", [128, FC, TB])
        hid = [S.sd[:, blk(f)] for f in range(FC)] + [hid_sb[:, f, :] for f in range(FC)]
        y_tok = S.xc[:, :].rearrange("p (t d) -> p t d", d=D)
        y_ps = [ps(f"y{b}") for b in range(NB)]
        hid_ps = [ps(f"hid{n}") for n in range(4)]
        mean_ps, var_ps = hid_ps[0:2], hid_ps[2:4]
        aside = y_ps[NB - 1]
        logits_ps, turn_ps, slot_ps = aside[:, 0:128], aside[:, 128:256], aside[:, 256:384]
        offset_ps, total_ps, start_ps, passed_ps = aside[:, 384:385], aside[:, 385:386], aside[:, 386:387], aside[:, 388:388 + XT + XB]

        sem = S.sem
        rw_in, ws_in, logits_done, to_exp, exped = sem("rw_in"), sem("ws_in"), sem("logits0"), sem("to_exp0"), sem("exped0")
        h_turned, h_first, h_rows = sem("h_turned0"), sem("h_first0"), sem("h_rows0")
        sel_ready, sel_turned, tags_ready = sem("sel0"), sem("sel_turned0"), sem("tags0")
        counted, totalled = sem("counted0"), sem("totalled0")
        slots_ready, slots_turned, slot_ready, w_row_ready = sem("slots0"), sem("slots_turned0"), sem("slot_ready0"), sem("w_row")
        scattered, wx_in = sem("scattered0"), [sem(f"wx_in{p}") for p in range(XB)]
        rows_in = [sem(f"slot_rows_in0_{i}") for i in range(4)]
        x_turned, x_copied = sem("x_turned0"), sem("x_copied0")
        hid_ready, shared_used, y_read = sem("hid_ready0"), sem("shared_used"), sem("shared_read")
        gelu_done = sem("gelu0")
        y_ready = sem("y_ready0")
        y_scaled = sem("y_scaled0")
        scaled, added = sem("scaled0"), sem("added0")
        y_turned = sem("y_turned0")
        block = ctx.enter_context(nc.Block())
        groups = [range(6 * i, min(6 * i + 6, XT)) for i in range(4)]

        @block.sync
        def _(sp):
            sp.dma_start(wr[:, :], A["wg0"]).then_inc(rw_in, 16)
            sp.dma_start(bgB[:, :], A["bg0"].to_broadcast([128, E])).then_inc(rw_in, 16)
            sp.dma_start(token_id[:, :], A["token_id"]).then_inc(rw_in, 16)
            sp.dma_start(ws[:, :], A["wx0"][E * 128:(E + 1) * 128, :]).then_inc(ws_in, 16)
            sp.dma_start(b2s[:, :], A["bs2"]).then_inc(ws_in, 16)
            sp.wait_ge(scattered, 2 * NTILE * 16)
            for i, g in enumerate(groups):
                sp.dma_start(slot_rows[:, 2 * g.start:2 * g.stop, :],
                             A["slots0"][g.start * XW:g.stop * XW, :].rearrange("(c p) w -> p c w", p=128)).then_inc(rows_in[i], 16)
            sp.wait_ge(added, 32 * XT)
            for b in range(NB):
                sp.dma_start(y_tok[:, blk(b, 4), :],
                             A["y_sum0"][blk(b), :].rearrange("(c p) d -> p c d", p=128)).then_inc(S.y_in[b], 16)

        @block.tensor
        def _(pe):
            ln_tensor(pe, S, 1, mean_ps, var_ps)
            pe.wait_ge(rw_in, 48)
            router_tensor(pe, S, logits_ps, wr[:, :], NB, logits_done)
            for b in range(NB):
                for u in range(4):
                    last = pe.transpose(hid_ps[b][:, blk(u, 128)], h_tile(S, 4 * b + u), S.ident)
                last.then_inc(h_turned, 1)

            def turn_sel():
                pe.wait_ge(sel_ready, 1)
                pe.transpose(turn_ps, R.gate[:, :, :].rearrange("p e c -> p (e c)"), S.ident).then_inc(sel_turned, 1)

            def totals():
                pe.wait_ge(counted, 1)
                pe.matmul(offset_ps, S.earlier_tile, count[:, :], start=True, stop=True)
                pe.matmul(total_ps, S.same_expert, count[:, :], start=True, stop=True).then_inc(totalled, 1)

            def starts():
                pe.wait_ge(counted, 2)
                pe.matmul(start_ps, S.earlier_expert, tiles[:, :], start=True, stop=True).then_inc(totalled, 1)

            def numbers():
                pe.wait_ge(counted, 3)
                pe.matmul(passed_ps, S.mean_w[:, :], passed[:, :], start=True, stop=True).then_inc(totalled, 1)

            def turn_slots():
                pe.wait_ge(slots_ready, 1)
                pe.wait_ge(w_row_ready, 1)
                pe.transpose(slot_ps, rank[:, :], S.ident).then_inc(slots_turned, 1)

            asides = {6: turn_sel, 7: totals, 8: starts, 9: numbers, 10: turn_slots}
            at = [0]

            def between():
                if at[0] in asides:
                    asides[at[0]]()
                at[0] += 1

            def hidden_shared(b):
                for f in range(FC):
                    n = FC * b + f
                    pe.wait_ge(gelu_done, n + 1)
                    pe.matmul(hid_ps[n % 4][:, :], ws[:, blk(f, 128)], h_block(S, b), start=True, stop=True).then_inc(hid_ready, 1)
                    between()

            def back_shared(b):
                pe.matmul(y_ps[b][:, :], b2s[:, :], one_row[:, :], start=True, stop=False)
                for f in range(FC):
                    n = FC * b + f
                    pe.wait_ge(gelu_done, n + 5)
                    pe.matmul(y_ps[b][:, :], ws[:, F + f * D:F + (f + 1) * D], hid[n % (2 * FC)],
                              start=False, stop=(f == FC - 1)).then_inc(shared_used, 1)
                    between()

            pe.wait_ge(ws_in, 32)
            pe.wait_ge(h_first, NB)
            pe.wait_ge(h_rows, NB)
            hidden_shared(0)
            for b in range(NB):
                if b + 1 < NB:
                    hidden_shared(b + 1)
                if b == NB - 1:
                    pe.wait_ge(slot_ready, 2)
                    pe.wait_ge(w_row_ready, 1)
                back_shared(b)
            pe.wait_ge(y_read, NB)

            for t in range(XT):
                if t % 6 == 0:
                    pe.wait_ge(rows_in[t // 6], 16)
                if t >= 2:
                    pe.wait_ge(x_copied, t - 1)
                for c in range(2):
                    last = pe.transpose(y_ps[2 + t % 2][:, blk(c, 128)], slot_rows[:, 2 * t + c, 0:D], S.ident)
                last.then_inc(x_turned, 1)
            pe.wait_ge(x_copied, XT)

            def hidden(i, k):
                w = wx[k % XB]
                pe.wait_ge(wx_in[k % XB], i * 16 + 16 * (k // XB + 1))
                for f in range(FC):
                    pe.wait_ge(gelu_done, i * (XB * FC) + (FC * k + f + 17))
                    pe.matmul(hid_ps[f][:, 0:XW], w[:, blk(f, 128)], x_slots[:, bass.ds(i * (XB * XW) + k * XW, XW)],
                              start=True, stop=True).then_inc(hid_ready, 1)

            def back(i, k):
                p = k % 2
                pe.wait_ge(y_scaled, i * XB + (k + 1))
                pe.wait_ge(gelu_done, i * (XB * FC) + (FC * k + 24))
                for c in range(2):
                    for f in range(FC):
                        last = pe.matmul(y_ps[p][:, blk(c, D)], hid[FC * p + f][:, blk(c, 128)],
                                         wx[k][:, F + f * D:F + (f + 1) * D], start=(f == 0), stop=(f == FC - 1))
                last.then_inc(y_ready, 1)

            hidden(0, 0)
            with pe.Fori(0, XT // XB) as i:
                for k in range(XB):
                    hidden(i, k + 1)
                    back(i, k)
            for k in range(XT % XB):
                if k + 1 < XT % XB:
                    hidden(XT // XB, k + 1)
                back(XT // XB, k)
            for b in range(NB):
                pe.wait_ge(S.y_in[b], 16)
                for u in range(4):
                    last = pe.transpose(hid_ps[b][:, blk(u, 128)], y_tok[:, 4 * b + u, :], S.ident)
                last.then_inc(y_turned, 1)

        @block.scalar
        def _(act):
            ln_scalar(act, S, 1, var_ps)
            act.wait_ge(to_exp, 1)
            act.activation(R.p[:, :, :], R.p[:, :, :], ACT.Exp).then_inc(exped, 1)
            for b in range(NB):
                act.wait_ge(h_turned, b + 1)
                for k, done in enumerate((h_first, h_rows)):
                    act.activation(token_rows[:, blk(b, 4), k, 0:D],
                                   hid_ps[b][:, :].rearrange("p (c d) -> p c d", d=D), ACT.Copy).then_inc(done, 1)
            act.wait_ge(ws_in, 32)
            for n in range(4 * FC):
                act.wait_ge(hid_ready, n + 1)
                if n >= 2 * FC:
                    act.wait_ge(shared_used, n - 2 * FC + 1)
                act.activation(hid[n % (2 * FC)], hid_ps[n % 4][:, :], ACT.Gelu,
                               bias=ws[:, F + FC * D + n % FC:F + FC * D + n % FC + 1]).then_inc(gelu_done, 1)
            for t in range(XT):
                act.wait_ge(x_turned, t + 1)
                act.activation(x_slots[:, blk(t, XW)], y_ps[2 + t % 2][:, 0:XW], ACT.Copy).then_inc(x_copied, 1)
            act.wait_ge(shared_used, 4 * FC)

            def tile(i, k):
                w, p = wx[k], k % 2
                for f in range(FC):
                    act.wait_ge(y_ready, i * XB + (k + 1))
                    act.wait_ge(hid_ready, i * (XB * FC) + (FC * k + f + 17))
                    act.activation(hid[FC * p + f][:, 0:XW], hid_ps[f][:, 0:XW], ACT.Gelu,
                                   bias=w[:, F + FC * D + f:F + FC * D + f + 1]).then_inc(gelu_done, 1)

            with act.Fori(0, XT // XB) as i:
                for k in range(XB):
                    tile(i, k)
            for k in range(XT % XB):
                tile(XT // XB, k)

        @block.vector
        def _(dve):
            link = make_link(dve, S)
            link(dve.memset(one_row[:, :], 1.0))
            dve.memset(R.m[:, 0:1], 0.0).then_inc(gelu_done, 4)
            dve.memset(R.m[:, 1:2], 0.0).then_inc(y_ready, 2)
            dve.memset(R.m[:, 2:3], 0.0).then_inc(y_scaled, 2)
            dve.wait_ge(y_scaled, 2)
            ln_vector(dve, S, link, 1, mean_ps, var_ps, S.mod[:, CB:CB + 1], S.mod[:, SB:SB + 1])
            dve.wait_ge(rw_in, 48)
            dve.wait_ge(logits_done, 1)
            link(dve.tensor_tensor(R.p[:, :, :], logits_ps.rearrange("p (t e) -> p t e", e=E),
                                   bgB[:, :].unsqueeze(1).to_broadcast([128, NTILE, E]), ALU.add))
            top2_vector(dve, S, link, R, to_exp, exped)
            dve.tensor_copy(R.gate[:, :, :].rearrange("p e c -> p c e"), R.sel[:, :, :]).then_inc(sel_ready, 1)
            link(dve.tensor_tensor(R.rest[:, :, :], R.sel[:, :, :], R.hot[:, :, :], ALU.subtract))
            for k, top in enumerate((R.top1, R.top2)):
                dve.tensor_copy(token_rows[:, :, k, D], top[:, :]).then_inc(tags_ready, 1)
                dve.tensor_copy(token_rows[:, :, k, D + 1].bitcast(I32), token_id[:, :]).then_inc(tags_ready, 1)
            dve.wait_ge(sel_turned, 1)
            link(dve.tensor_copy(hit[:, :], turn_ps))
            link(dve.tensor_tensor_scan(rank[:, :], hit[:, :], hit[:, :], 0.0, ALU.add, ALU.max))
            dve.tensor_copy(count[:, :], rank[:, 127:128]).then_inc(counted, 1)
            dve.wait_ge(totalled, 1)
            link(dve.tensor_scalar(base[:, :], offset_ps, -1.0, None, ALU.add))
            dve.tensor_scalar(fits[:, :], S.tile_sizes, total_ps, None, ALU.is_lt, ALU.add,
                              accum_out=tiles[:, :]).then_inc(counted, 1)
            dve.wait_ge(totalled, 2)
            link(dve.tensor_tensor(tiles[:, :], tiles[:, :], start_ps, ALU.add))
            link(dve.scalar_tensor_tensor(base[:, :], start_ps, float(XW), base[:, :], ALU.mult, ALU.add))
            dve.tensor_scalar(passed[:, :], S.tile_numbers, tiles[:, :], None, ALU.is_ge).then_inc(counted, 1)
            dve.scalar_tensor_tensor(rank[:, :], rank[:, :], base[:, :], hit[:, :], ALU.add, ALU.mult).then_inc(slots_ready, 1)
            dve.wait_ge(totalled, 3)
            link(dve.tensor_scalar(passed[:, :], passed_ps, float(E * 128), S.row_number, ALU.mult, ALU.add))
            dve.tensor_scalar(w_row[:, :], passed[:, :], S.last_expert_row, None, ALU.min).then_inc(w_row_ready, 1)
            dve.wait_ge(slots_turned, 1)
            for k, hot in enumerate((R.rest, R.hot)):
                link(dve.tensor_tensor(R.p[:, :, :], hot[:, :, :], slot_ps.rearrange("p (e c) -> p c e", e=E), ALU.mult))
                link(dve.tensor_reduce(slot_f[:, k, :], R.p[:, :, :], AX.X, ALU.add))
                dve.tensor_copy(slot[:, k, :], slot_f[:, k, :]).then_inc(slot_ready, 1)
            dve.wait_ge(shared_used, 4 * FC)
            for b in range(NB):
                dve.scalar_tensor_tensor(S.xT[:, blk(b)], y_ps[b][:, :], S.mod[:, GB:GB + 1], S.xT[:, blk(b)],
                                         ALU.mult, ALU.add).then_inc(y_read, 1)

            def scale(i, k, first):
                p = k % 2
                dve.wait_ge(y_ready, i * XB + (k + 3))
                if not (first and k < 2):
                    dve.wait_ge(added, i * (32 * XB) + 32 * (k - 1))
                at = i * (2 * XB) + 2 * k
                dve.tensor_copy(ids[p][:, :], slot_rows[:, bass.ds(at, 2), D + 1].bitcast(I32)).then_inc(scaled, 1)
                dve.tensor_copy(w_next[k][:, :], w_row[:, bass.ds(i * XB + (k + XB), 1)]).then_inc(scaled, 1)
                dve.tensor_tensor(y_tmp[:, :, :], y_ps[p][:, 0:2 * D].rearrange("p (c d) -> p c d", d=D),
                                  wx[k][:, WX - D:WX].unsqueeze(1).to_broadcast([128, 2, D]), ALU.add).then_inc(scaled, 1)
                dve.wait_ge(scaled, i * (4 * XB) + (4 * k + 3))
                dve.tensor_scalar(y_rows[p][:, 0, :], y_tmp[:, 0, :], slot_rows[:, bass.ds(at, 1), D], None,
                                  ALU.mult).then_inc(scaled, 1)
                dve.tensor_scalar(y_rows[p][:, 1, :], y_tmp[:, 1, :], slot_rows[:, bass.ds(at + 1, 1), D], None,
                                  ALU.mult).then_inc(y_scaled, 1)
                dve.wait_ge(y_scaled, i * XB + (k + 3))
                dve.wait_ge(scaled, i * (4 * XB) + (4 * k + 4))

            for k in range(XB):
                scale(0, k, True)
            with dve.Fori(1, XT // XB) as i:
                for k in range(XB):
                    scale(i, k, False)
            for k in range(XT % XB):
                scale(XT // XB, k, False)
            for b in range(NB):
                dve.wait_ge(y_turned, b + 1)
                dve.wait_ge(y_read, NB)
                dve.scalar_tensor_tensor(S.xT[:, blk(b)], hid_ps[b][:, :], S.mod[:, GB:GB + 1], S.xT[:, blk(b)],
                                         ALU.mult, ALU.add).then_inc(S.x_ready, 1)
            dve.wait_ge(S.x_ready, 3 * NB)

        @block.gpsimd
        def _(pool):
            for i in range(NQ):
                pool.memset(S.kop[:, QUAD * i:QUAD * (i + 1), :].bitcast(I32), 0).then_inc(S.k_zeroed, 1)
            pool.wait_ge(S.k_zeroed, NQ)

            def gather_weights(p, rows):
                pool.indirect_dma_start(wx[p][:, :], None, A["wx0"], bass.IndirectOffsetOnAxis(rows, 0)).then_inc(wx_in[p], 16)

            pool.wait_ge(w_row_ready, 1)
            for p in range(XB):
                gather_weights(p, w_row[:, p:p + 1])
            pool.wait_ge(S.dram_init, 64)
            pool.wait_ge(tags_ready, 4)
            pool.wait_ge(h_first, NB)
            pool.wait_ge(h_rows, NB)
            for k in range(2):
                pool.wait_ge(slot_ready, k + 1)
                for t in range(NTILE):
                    pool.indirect_dma_start(A["slots0"], bass.IndirectOffsetOnAxis(slot[:, k, t:t + 1], 0), token_rows[:, t, k, :],
                                            None).then_inc(scattered, 16)

            def tile(i, k, more):
                p = k % 2
                early(pool, i * XB + (k + 3))
                early(pool, i * (4 * XB) + (4 * k + 4))
                pool.wait_ge(S.dram_init, 64)
                pool.wait_ge(y_scaled, i * XB + (k + 3))
                pool.wait_ge(scaled, i * (4 * XB) + (4 * k + 4))
                for c in range(2):
                    pool.indirect_dma_start(A["y_sum0"], bass.IndirectOffsetOnAxis(ids[p][:, c:c + 1], 0), y_rows[p][:, c, :], None,
                                            compute_op=ALU.add).then_inc(added, 16)
                if more:
                    gather_weights(k, w_next[k][:, :])
                pool.wait_ge(added, i * (32 * XB) + 32 * (k + 1))

            with pool.Fori(0, XT // XB) as i:
                for k in range(XB):
                    tile(i, k, True)
            for k in range(XT % XB):
                tile(XT // XB, k, False)
            pool.wait_ge(wx_in[XB - 1], 16 * (XT // XB + 1))



Q_PARTS = (0, 0, 0, 1, 1, 2)
K_PARTS = (0, 1, 2, 0, 1, 0)
KP = DK * len(Q_PARTS)
KM = KP + 3
VW = DK + 1


def stage_qkv(nc, S, A):
    with ExitStack() as ctx:
        sb = lambda n, s, d=F32: ctx.enter_context(nc.sbuf_tensor(n, s, d))
        ps = lambda n: ctx.enter_context(nc.psum_tensor(n, [128, TB], F32))
        wqkv = sb("wqkv", [128, 3, D])
        bvB = sb("bvB", [128, D])
        full = sb("qk_full", [128, 2, TB])
        parts = sb("parts_sb", [128, 2, 2, 3, TB], BF16)
        mean_ps = [ps("mean3a"), ps("mean3b")]
        var_ps = [ps("var3a"), ps("var3b")]
        qk_ps = [ps("qk0"), ps("qk1")]
        v_ps = [ps("v0"), ps("v1")]

        sem = S.sem
        w_in, qk_mm, full_done, part1, rest_done, part2, part3 = (
            sem("w_in3"), sem("qk_mm"), sem("full_done"), sem("part1"), sem("rest_done"), sem("part2"), sem("part3"))
        parts_out = [sem("parts_out0"), sem("parts_out1")]
        v_mm, v_done = sem("v_mm"), sem("v_done")
        zeroed = sem("zeroed")
        block = ctx.enter_context(nc.Block())

        def q_rows(eng, b, first, end, done):
            for r in range(first, end):
                eng.dma_start(S.qop[DK * r:DK * (r + 1), :, blk(b)],
                              A["qk_parts"][0, Q_PARTS[r], :, :, blk(b)]).then_inc(done, 16)

        @block.gpsimd
        def _(pool):
            for i in range(NQ):
                pool.memset(S.qop[:, QUAD * i:QUAD * (i + 1), :].bitcast(I32), 0).then_inc(zeroed, 1)
            pool.wait_ge(zeroed, NQ)
            for b in range(NB):
                pool.wait_ge(parts_out[b % 2], 32 * (b // 2 + 1))
                q_rows(pool, b, 0, 3, S.ops_in_sw[b])

        @block.sync
        def _(sp):
            sp.dma_start(wqkv[:, :, :], A["wqkv"]).then_inc(w_in, 16)
            sp.dma_start(bvB[:, :], A["bv"].to_broadcast([128, D])).then_inc(w_in, 16)
            def store_parts(b):
                for j in range(2):
                    sp.wait_ge(part3, 2 * b + j + 1)
                    sp.dma_start(A["qk_parts"][j].rearrange("s d h t -> (d h) s t")[:, :, blk(b)],
                                 parts[:, b % 2, j, :, :]).then_inc(parts_out[b % 2], 16)

            store_parts(0)
            sp.wait_ge(zeroed, NQ)
            sp.wait_ge(S.k_zeroed, NQ)
            sp.dma_start(S.kop[KP:KM, :, :], A["one_rows"]).then_inc(S.ones_in, 16)
            for b in range(NB):
                if b + 1 < NB:
                    store_parts(b + 1)
                sp.wait_ge(parts_out[b % 2], 32 * (b // 2 + 1))
                q_rows(sp, b, 3, 6, S.ops_in[b])
                row = 0
                for n in (3, 2, 1):
                    rows = A["qk_parts"][1, 0:n, :, :, blk(b)].rearrange("s d h t -> (s d) h t")
                    sp.dma_start(S.kop[row:row + n * DK, :, blk(b)], rows).then_inc(S.ops_in[b], 16)
                    row += n * DK

        @block.tensor
        def _(pe):
            ln_tensor(pe, S, 2, mean_ps, var_ps)
            pe.wait_ge(w_in, 32)
            for b in range(NB):
                pe.wait_ge(S.h_ready, 2 * NB + b + 1)
                for j in range(2):
                    n = 2 * b + j
                    if n >= 2:
                        pe.wait_ge(full_done, n - 1)
                    pe.matmul(qk_ps[j][:, :], wqkv[:, j, :], h_block(S, b), start=True, stop=True).then_inc(qk_mm, 1)
                if b >= 2:
                    pe.wait_ge(v_done, b - 1)
                for u in range(TB // 128):
                    last = pe.matmul(v_ps[b % 2][:, blk(u, 128)], h_tile(S, 4 * b + u), wqkv[:, 2, :], start=True, stop=True)
                last.then_inc(v_mm, 1)

        @block.scalar
        def _(act):
            ln_scalar(act, S, 2, var_ps)
            for n in range(2 * NB):
                act.wait_ge(full_done, n + 1)
                if n >= 4:
                    act.wait_ge(parts_out[n // 2 % 2], 32 * (n // 4))
                act.activation(parts[:, n // 2 % 2, n % 2, 0, :], full[:, n % 2, :], ACT.Copy).then_inc(part1, 1)
                act.wait_ge(rest_done, n + 1)
                act.activation(parts[:, n // 2 % 2, n % 2, 1, :], full[:, n % 2, :], ACT.Copy).then_inc(part2, 1)

        @block.vector
        def _(dve):
            link = make_link(dve, S)
            link(dve.memset(S.v_all[:, :, :, DK:VW], 1.0))
            ln_vector(dve, S, link, 2, mean_ps, var_ps, S.mod[:, 6 + CA:7 + CA], S.mod[:, 6 + SA:7 + SA])
            dve.wait_ge(w_in, 32)
            for b in range(NB):
                for j in range(2):
                    n = 2 * b + j
                    dve.wait_ge(qk_mm, n + 1)
                    if n >= 2:
                        dve.wait_ge(part3, n - 1)
                    x = full[:, n % 2, :]
                    dve.tensor_scalar(x, qk_ps[j][:, :], S.cols[:, BQ + j:BQ + j + 1], None, ALU.add).then_inc(full_done, 1)
                dve.wait_ge(v_mm, b + 1)
                dve.tensor_tensor(S.v_all[:, 4 * b:4 * b + 4, :, 0:DK],
                                  v_ps[b % 2][:, :].rearrange("p (t h d) -> p t h d", t=4, d=DK),
                                  bvB[:, :].rearrange("p (h d) -> p h d", d=DK).unsqueeze(1).to_broadcast([128, 4, H, DK]),
                                  ALU.add).then_inc(v_done, 1)
                for j in range(2):
                    n = 2 * b + j
                    x = full[:, n % 2, :]
                    dve.wait_ge(part1, n + 1)
                    dve.tensor_tensor(x, x, parts[:, n // 2 % 2, n % 2, 0, :], ALU.subtract).then_inc(rest_done, 1)
                for j in range(2):
                    n = 2 * b + j
                    dve.wait_ge(part2, n + 1)
                    dve.tensor_tensor(parts[:, n // 2 % 2, n % 2, 2, :], full[:, n % 2, :], parts[:, n // 2 % 2, n % 2, 1, :],
                                      ALU.subtract).then_inc(part3, 1)



LEAD_16THS = 8.5
RING = 4
STEPS = [(g, kt, max(0, kt - 4 * g) * 128) for g in range(NB) for kt in range(4 * g + 4)]
TURN_DELAY = 3
CHUNKS = []
for _g in range(NB):
    _block = [("chunk", _t, _j, _c, 128 * (_c * (_t + 1) // (_g + 1)), 128 * ((_c + 1) * (_t + 1) // (_g + 1)))
              for _t in range(4 * _g, 4 * _g + 4) for _j in range(QUAD) for _c in range(_g + 1)]
    CHUNKS += _block if _g == 0 else _block[:TURN_DELAY] + [("turn", _g - 1)] + _block[TURN_DELAY:]
CHUNKS.append(("turn", NB - 1))
BLOCK_FIRST = [min(n for n, c in enumerate(CHUNKS) if c[0] == "chunk" and c[1] // 4 == g) for g in range(NB)]
BLOCK_LAST = [max(n for n, c in enumerate(CHUNKS) if c[0] == "chunk" and c[1] // 4 == g) for g in range(NB)]
NS, NCH = len(STEPS), len(CHUNKS)
CHUNK_COST = [c[5] - c[4] + 64 if c[0] == "chunk" else 64 for c in CHUNKS]
CHUNK_COST[-1] = 2048
LEAD = next(n for n in range(NCH) if 16 * sum(CHUNK_COST[:n]) >= LEAD_16THS * sum(CHUNK_COST))


def chunks_by_step():
    order = [(n, 0) for n in range(LEAD, NCH)] + [(n, 1) for n in range(LEAD)]
    step_cost = [TB - off for _, _, off in STEPS]
    total = sum(CHUNK_COST)
    done, at, spent, out = 0, 0, 0, []
    for cost in step_cost:
        done += cost
        first = at
        while at < NCH and (spent + CHUNK_COST[order[at][0]] // 2) * sum(step_cost) <= done * total:
            spent += CHUNK_COST[order[at][0]]
            at += 1
        out.append(order[first:at])
    out[-1] += order[at:]
    return out


V_FIRST = 12


def early(eng, value):
    if not isinstance(value, int):
        eng.compute_val(value)


def stage_attention(nc, S, A):
    with ExitStack() as ctx:
        sb = lambda n, s, d=F32: ctx.enter_context(nc.sbuf_tensor(n, s, d))
        ps = lambda n, w=TB: ctx.enter_context(nc.psum_tensor(n, [128, w], F32))
        num, den = S.sd, S.hT
        mask, masked = S.sd[:, blk(0)], (S.sd[:, blk(1)], S.sd[:, blk(2)], S.sd[:, blk(3)], S.xc[:, blk(2)])
        o_sb = S.xc[:, 0:2 * TB].rearrange("p (a t) -> p a t", a=2)
        chunk_max = sb("chunk_max", [128, QUAD, NTILE, NB])
        causal_t = sb("causal_t", [128, 2, 128], BF16)
        neg_max = sb("neg_max", [128, QUAD, 4])
        max_rest = sb("max_rest", [QUAD * 4, 128])
        max_parts = sb("max_parts", [QUAD * 4, 2, 3, 128], BF16)
        probs = sb("probs", [128, 2, QUAD, TB])
        v_quad = sb("v_quad", [128, NTILE, QUAD, VW])
        max_ps = [ps(f"max{n}") for n in range(RING)]
        st_ps = [ps(f"st{n}") for n in range(3)]
        o_ps = ps("o_acc")
        qop = S.qop[:, :, :].rearrange("p h t -> p (h t)")
        kop = S.kop[:, :, :].rearrange("p h t -> p (h t)")

        sem = S.sem
        mask_in, causal_in = sem("mask_in"), sem("causal_in")
        scores_ready = sem("scores_ready")
        max_bank_free = sem("max_bank_free")
        max_stored, neg_max_ready, max_parts_ready = sem("max_stored"), sem("neg_max"), sem("max_parts")
        max_rows_in = [sem("max_rows_in0"), sem("max_rows_in1")]
        st_ready = sem("st_ready")
        st_free = sem("st_free")
        probs_free = sem("probs_free")
        v_ready, o_out = sem("v_ready"), [sem("o_out0"), sem("o_out1")]
        o_free = sem("o_free")
        sums_in = [sem(f"sums_in{g}") for g in range(NB)]
        block = ctx.enter_context(nc.Block())

        last_step = [max(s for s, x in enumerate(STEPS) if x[0] == g) for g in range(NB)]
        plan = chunks_by_step()

        @block.sync
        def _(sp):
            sp.dma_start(mask, A["causal"]).then_inc(mask_in, 16)
            sp.dma_start(causal_t[:, :, :], A["causal_t"]).then_inc(causal_in, 16)

            def max_rows(i, g):
                sp.wait_ge(max_parts_ready, NB * i + g + 1)
                rows = A["max_rows"][g, :, bass.ds(QUAD * i, QUAD), :]
                sp.dma_start(rows.rearrange("s j (t q) -> (j t) s q", q=128),
                             max_parts[:, g % 2, :, :]).then_inc(max_stored, 16)
                sp.wait_ge(max_stored, i * (16 * NB) + 16 * (g + 1))
                sp.dma_start(S.qop[KP:KM, bass.ds(QUAD * i, QUAD), blk(g)], rows).then_inc(max_rows_in[g % 2], 16)

            def store(i, g):
                sp.wait_ge(o_free, NB * i + g + 2)
                for j in range(QUAD):
                    sp.dma_start(A["attn_sums"][bass.ds(QUAD * i + j, 1), :, blk(g)].rearrange("o v t -> (o v) t"),
                                 o_sb[32 * j:32 * j + VW, g % 2, :]).then_inc(o_out[g % 2], 16)

            max_rows(0, 0)
            max_rows(0, 1)
            with sp.Fori(0, NQ - 1) as i:
                max_rows(i, 2)
                store(i, 0)
                store(i, 1)
                max_rows(i, 3)
                max_rows(i + 1, 0)
                store(i, 2)
                max_rows(i + 1, 1)
                store(i, 3)
            def sums(g):
                sp.wait_ge(o_out[g % 2], (NQ - 1) * (32 * NB) + 64 * (g // 2 + 1))
                sp.dma_start(num[:, blk(g)], A["attn_sums"][:, 0:DK, blk(g)]).then_inc(sums_in[g], 16)
                sp.dma_start(den[:, blk(g)], A["attn_sums"][:, DK:VW, blk(g)].to_broadcast([H, DK, TB])).then_inc(sums_in[g], 16)

            max_rows(NQ - 1, 2)
            store(NQ - 1, 0)
            store(NQ - 1, 1)
            max_rows(NQ - 1, 3)
            sp.wait_ge(max_bank_free, NQ * NCH + RING)
            sums(0)
            store(NQ - 1, 2)
            sums(1)
            sums(2)
            store(NQ - 1, 3)
            sums(3)

        @block.tensor
        def _(pe):
            pe.wait_ge(S.ones_in, 16)
            pe.wait_ge(causal_in, 16)
            pe.wait_ge(S.const_in, 32)

            @contextmanager
            def quad_offset(i, s):
                if isinstance(i, int):
                    yield i * (QUAD * NT)
                    return
                reg = pe.alloc_register(f"quad_offset{s}")
                pe.reg_mov(reg, i * (QUAD * NT))
                yield pe.snap(reg, min_val=0, max_val=(NQ - 2) * QUAD * NT)
                pe.free_register(reg)

            def chunk(at, i, ahead, n):
                pe.wait_ge(max_bank_free, i * NCH + (ahead * NCH + n + 1))
                bank = max_ps[n % RING]
                if CHUNKS[n][0] == "turn":
                    g = CHUNKS[n][1]
                    pe.wait_ge(neg_max_ready, i * NB + (ahead * NB + g + 1))
                    pe.transpose(bank[0:4 * QUAD, 0:128], neg_max[:, :, :].rearrange("p j t -> p (j t)"),
                                 S.ident).then_inc(scores_ready, 1)
                    return
                _, t, j, _, key, end = CHUNKS[n]
                head = (ahead * QUAD + j) * NT
                pe.matmul(bank[:, 0:end - key], qop[:, bass.ds(at + (head + 128 * t), 128)],
                          kop[:, bass.ds(at + (head + key), end - key)], start=True, stop=True).then_inc(scores_ready, 1)

            def scores(at, i, s, j):
                g, kt, off = STEPS[s]
                if kt == 0 and j == 0:
                    pe.wait_ge(max_rows_in[g % 2], i * (8 * NB) + 16 * (g // 2 + 1))
                n = QUAD * s + j
                pe.wait_ge(st_free, i * (QUAD * NS) + max(n + 1, 3))
                own = kt >= 4 * g
                last = pe.matmul(st_ps[n % 3][:, off:TB], kop[:, bass.ds(at + (j * NT + 128 * kt), 128)],
                                 qop[:, bass.ds(at + (j * NT + TB * g + off), TB - off)],
                                 start=True, stop=not own)
                if own:
                    last = pe.matmul(st_ps[n % 3][:, off:off + 128], causal_t[:, 0, :], causal_t[:, 1, :],
                                     start=False, stop=True)
                last.then_inc(st_ready, 1)

            def products(i, s):
                g, kt, off = STEPS[s]
                if s == 0:
                    pe.wait_ge(v_ready, 2 * i + 1)
                if kt == V_FIRST and g == NB - 1:
                    pe.wait_ge(v_ready, 2 * i + 2)
                if kt == 0:
                    pe.wait_ge(o_free, NB * i + g + 1)
                pe.wait_ge(st_free, i * (QUAD * NS) + QUAD * (s + 1) + 3)
                for j in range(QUAD):
                    last = pe.matmul(o_ps[32 * j:32 * j + VW, off:TB], v_quad[:, kt, j, :], probs[:, s % 2, j, off:TB],
                                     start=(kt == 0), stop=(kt == 4 * g + 3))
                last.then_inc(probs_free, 1)

            def rows_of(g):
                pe.wait_ge(S.ops_in[g], 6 * 16)
                pe.wait_ge(S.ops_in_sw[g], 3 * 16)

            for n in range(LEAD):
                if n in BLOCK_FIRST:
                    rows_of(BLOCK_FIRST.index(n))
                chunk(0, 0, 0, n)
            for g in range(NB):
                if BLOCK_FIRST[g] >= LEAD:
                    rows_of(g)

            def quad(i, next_too):
                for s in range(NS):
                    beside = [c for c in plan[s] if next_too or not c[1]]
                    with quad_offset(i, s) as at:
                        for j in range(QUAD):
                            scores(at, i, s, j)
                            for n, ahead in beside[j * len(beside) // QUAD:(j + 1) * len(beside) // QUAD]:
                                chunk(at, i, ahead, n)
                            if j == 2 and s:
                                products(i, s - 1)
                products(i, NS - 1)

            with pe.Fori(0, NQ - 1) as i:
                quad(i, True)
            quad(NQ - 1, False)

        @block.vector
        def _(dve):
            dve.memset(chunk_max[:, :, :, :], -BIG).then_inc(max_bank_free, RING)
            dve.memset(neg_max[:, 0, 0:1], 0.0).then_inc(st_free, 3)
            dve.memset(o_ps[:, :], 0.0).then_inc(o_free, 1)
            dve.memset(neg_max[:, 0, 1:2], 0.0).then_inc(probs_free, 2)
            dve.wait_ge(max_bank_free, RING)

            def maxima(i, first):
                for n, c in enumerate(CHUNKS):
                    if c[0] == "turn":
                        split_maxima(i, first, n, c[1])
                        continue
                    early(dve, NCH * i + n + 1)
                    dve.wait_ge(mask_in, 16)
                    dve.wait_ge(scores_ready, NCH * i + n + 1)
                    bank = max_ps[n % RING]
                    _, t, j, k, key, end = c
                    width = end - key
                    out = chunk_max[:, j, t, k:k + 1]
                    if end == 128 * (t + 1):
                        dve.tensor_tensor_reduce(masked[n % RING][:, 0:width], bank[:, 0:width], mask[:, TB - width:TB], 1.0,
                                                 -BIG, ALU.add, ALU.max, out).then_inc(max_bank_free, 1)
                    else:
                        dve.tensor_reduce(out, bank[:, 0:width], AX.X, ALU.max).then_inc(max_bank_free, 1)
                    if n in BLOCK_LAST:
                        g = BLOCK_LAST.index(n)
                        dve.wait_ge(max_bank_free, NCH * i + n + 1 + RING)
                        dve.tensor_reduce(neg_max[:, :, :], chunk_max[:, :, 4 * g:4 * g + 4, :], AX.X, ALU.max,
                                          negate=True).then_inc(neg_max_ready, 1)

            def split_maxima(i, first, n, g):
                dve.wait_ge(scores_ready, NCH * i + n + 1)
                if not (first and g < 2):
                    dve.wait_ge(max_rows_in[g % 2], i * (8 * NB) + 16 * (g // 2))
                parts = max_parts[:, g % 2, :, :]
                turned = max_ps[n % RING][0:4 * QUAD, 0:128]
                dve.tensor_copy(parts[:, 0, :], turned).then_inc(S.split, 1)
                dve.wait_ge(S.split, i * (2 * NB) + 2 * g + 1)
                dve.tensor_tensor(max_rest[:, :], turned, parts[:, 0, :], ALU.subtract).then_inc(max_bank_free, 1)
                dve.wait_ge(max_bank_free, NCH * i + n + 1 + RING)
                dve.tensor_copy(parts[:, 1, :], max_rest[:, :]).then_inc(S.split, 1)
                dve.wait_ge(S.split, i * (2 * NB) + 2 * g + 2)
                dve.tensor_tensor(parts[:, 2, :], max_rest[:, :], parts[:, 1, :], ALU.subtract).then_inc(max_parts_ready, 1)
                early(dve, NB * i + g + 1)
                dve.wait_ge(mask_in, 16)
                dve.wait_ge(max_parts_ready, NB * i + g + 1)

            maxima(0, True)
            with dve.Fori(1, NQ) as i:
                maxima(i, False)
            link = make_link(dve, S)
            for g in range(NB):
                dve.wait_ge(sums_in[g], 32)
                link(dve.reciprocal(den[:, blk(g)], den[:, blk(g)]))
                link(dve.scalar_tensor_tensor(num[:, blk(g)], num[:, blk(g)], S.mod[:, 6 + GA:7 + GA], den[:, blk(g)],
                                              ALU.mult, ALU.mult))
                dve.tensor_tensor(S.xT[:, blk(g)], S.xT[:, blk(g)], num[:, blk(g)], ALU.add).then_inc(S.x_ready, 1)
            dve.wait_ge(S.x_ready, 4 * NB)

        @block.scalar
        def _(act):
            def quad(i, first):
                for s, (g, kt, off) in enumerate(STEPS):
                    act.wait_ge(probs_free, NS * i + s + 1)
                    for j in range(QUAD):
                        n = QUAD * s + j
                        act.wait_ge(st_ready, i * (QUAD * NS) + n + 1)
                        act.activation(probs[:, s % 2, j, off:TB], st_ps[n % 3][:, off:TB], ACT.Exp,
                                       scale=DK ** -0.5).then_inc(st_free, 1)
                    if kt == 0 and g:
                        copy_sums(i, g - 1, first)
                copy_sums(i, NB - 1, first)

            def copy_sums(i, g, first):
                act.wait_ge(probs_free, NS * i + last_step[g] + 3)
                if not (first and g < 2):
                    act.wait_ge(o_out[g % 2], i * (32 * NB) + 64 * (g // 2))
                act.activation(o_sb[:, g % 2, :], o_ps[:, :], ACT.Copy).then_inc(o_free, 1)

            quad(0, True)
            with act.Fori(1, NQ) as i:
                quad(i, False)

        @block.gpsimd
        def _(pool):
            def gather(i, tiles):
                pool.tensor_copy(v_quad[:, tiles, :, :], S.v_all[:, tiles, bass.ds(QUAD * i, QUAD), :]).then_inc(v_ready, 1)

            first, rest = slice(0, V_FIRST), slice(V_FIRST, NTILE)
            gather(0, first)
            gather(0, rest)
            with pool.Fori(1, NQ) as i:
                pool.wait_ge(probs_free, NS * i + (V_FIRST - NTILE + 2))
                gather(i, first)
                pool.wait_ge(probs_free, NS * i + 2)
                gather(i, rest)



def stage_swiglu_moe(nc, S, A):
    with ExitStack() as ctx:
        sb = lambda n, s, d=F32: ctx.enter_context(nc.sbuf_tensor(n, s, d))
        ps = lambda n: ctx.enter_context(nc.psum_tensor(n, [128, TB], F32))
        R = Routing(sb, 1)
        wr = sb("wr1", [128, E])
        token_id = sb("token_id", [128, NTILE], I32)
        w_t = sb("w_t", [128, 128])
        reach = sb("reach", [128, NCAND, 128])
        reached = sb("reached", [128, NCAND])
        hit = sb("hit", [128, 128])
        tie = sb("tie", [128, 128])
        rank = sb("rank", [128, 128])
        count = sb("count", [128, NCAND])
        need = sb("need", [128, 1])
        step = sb("step", [128, 1])
        bits = sb("found_bits", [128, 1], I32)
        thr = sb("thr", [128, 1], I32)
        cand = sb("cand", [128, NCAND], I32)
        next_cand = sb("next_cand", [128, NCAND], I32)
        slot_f = sb("slot_f", [128, 2, NTILE])
        slot = sb("slot", [128, 2, NTILE], I32)
        token_rows = sb("token_rows", [128, NTILE, 2, ROW])
        slot_rows = sb("slot_rows", [128, E * ST, ROW])
        x_slots = sb("x_slots", [128, E, ST * 128])
        ids = [sb(f"ids_{p}", [128, ST], I32) for p in range(2)]
        y_rows = [sb(f"y_rows_{p}", [128, ST, D]) for p in range(2)]
        y_tok = sb("y_tok", [128, NTILE, D])
        wg = [sb(f"wgt_{p}", [128, F]) for p in range(2)]
        wu = [sb(f"wup_{p}", [128, F]) for p in range(2)]
        wd = [sb(f"wdn_{p}", [128, FC, D]) for p in range(2)]
        act_g = sb("act_g", [128, 2, CAP])
        gated = sb("gated1", [128, 2 * FC, CAP])
        g_ps = [ps("g_ps0"), ps("g_ps1")]
        u_ps = [ps("u_ps0"), ps("u_ps1")]
        y_ps = [ps("y_ps0"), ps("y_ps1")]
        t_ps = [ps("t_ps0"), ps("t_ps1")]
        mean_ps, var_ps = g_ps, u_ps
        four_ps = g_ps + u_ps
        logits_ps = y_ps[0][:, 0:NTILE * E]
        turn_ps = y_ps[1][:, 0:128]
        total_ps = t_ps[0]
        slot_ps = t_ps[1][:, 0:128]
        slot_base = S.consts[:, 392 + ROUNDS:393 + ROUNDS]

        sem = S.sem
        rw_in, logits_done, to_exp, exped = sem("rw_in1"), sem("logits1"), sem("to_exp1"), sem("exped1")
        h_turned, h_first, h_rows = sem("h_turned"), sem("h_first"), sem("h_rows")
        weights_ready, turned, slots_ready, slots_turned = sem("weights1"), sem("turned1"), sem("slots1"), sem("slots_turned")
        tags_ready, slot_ready, scattered = sem("tags_ready"), sem("slot_ready"), sem("scattered")
        counted, totalled = sem("counted"), sem("totalled")
        rows_in = [sem(f"slot_rows_in{i}") for i in range(E // 2)]
        x_turned, x_copied = sem("x_turned"), sem("x_copied")
        gu_in = [sem(f"gu_in{p}") for p in range(2)]
        d_in = [sem(f"d_in{p}") for p in range(2)]
        up_ready, silu_done = sem("up_ready"), sem("silu_done1")
        gate_done = sem("gated1_done")
        y_ready = sem("y_ready")
        y_scaled = sem("y_scaled")
        scaled, added = sem("scaled"), sem("added")
        y_turned = sem("y_turned")
        tloop = sem("bit_steps")
        stored = sem("stored")
        block = ctx.enter_context(nc.Block())

        @block.sync
        def _(sp):
            sp.dma_start(wr[:, :], A["wr1"]).then_inc(rw_in, 16)
            sp.dma_start(token_id[:, :], A["token_id"]).then_inc(rw_in, 16)

            def load_gu(e, p):
                sp.dma_start(wg[p][:, :], A["wg_1"][bass.ds(e, 1), :, :].rearrange("e p f -> (e p) f")).then_inc(gu_in[p], 16)
                sp.dma_start(wu[p][:, :], A["wu_1"][bass.ds(e, 1), :, :].rearrange("e p f -> (e p) f")).then_inc(gu_in[p], 16)

            def load_d(e, p):
                sp.dma_start(wd[p][:, :, :], A["wd_1"][bass.ds(e, 1), :, :].rearrange("e p (c d) -> (e p) c d", c=FC)).then_inc(d_in[p], 16)

            for p in range(2):
                load_gu(p, p)
                load_d(p, p)
            sp.wait_ge(scattered, 2 * NTILE * 16)
            for i in range(E // 2):
                sp.dma_start(slot_rows[:, blk(i, 2 * ST), :],
                             A["slots"][blk(i, 2 * ST * 128), :].rearrange("(c p) w -> p c w", p=128)).then_inc(rows_in[i], 16)
            with sp.Fori(0, E // 2 - 1) as i:
                for p in range(2):
                    sp.wait_ge(up_ready, i * (2 * FC) + FC * (p + 1))
                    load_gu(2 * i + (2 + p), p)
                    sp.wait_ge(y_ready, i * 2 + (p + 1))
                    load_d(2 * i + (2 + p), p)
            sp.wait_ge(added, ST * 16 * E)
            for b in range(NB):
                sp.dma_start(y_tok[:, blk(b, NTILE // NB), :],
                             A["y_sum"][blk(b), :].rearrange("(c p) d -> p c d", p=128)).then_inc(S.y_in[b], 16)
            for b in range(NB):
                sp.wait_ge(S.x_ready, 4 * NB + b + 1)
                sp.dma_start(A["out"][:, blk(b)], S.xT[:, blk(b)]).then_inc(stored, 16)
            sp.wait_ge(stored, 16 * NB)

        @block.tensor
        def _(pe):
            ln_tensor(pe, S, 3, mean_ps, var_ps)
            pe.wait_ge(rw_in, 32)
            router_tensor(pe, S, logits_ps, wr[:, :], 3 * NB, logits_done)
            for b in range(NB):
                for u in range(4):
                    last = pe.transpose(four_ps[b][:, blk(u, 128)], h_tile(S, 4 * b + u), S.ident)
                last.then_inc(h_turned, 1)
            pe.wait_ge(weights_ready, 1)
            pe.transpose(turn_ps, R.gate[:, :, :].rearrange("p e c -> p (e c)"), S.ident).then_inc(turned, 1)

            def total(n, weights, width):
                pe.wait_ge(counted, n)
                pe.matmul(total_ps[:, 0:width], weights, count[:, 0:width], start=True, stop=True).then_inc(totalled, 1)

            total(NCAND, S.same_expert, NCAND)
            with pe.Fori(1, ROUNDS) as r:
                total(r * NCAND + NCAND, S.same_expert, NCAND)
            total(ROUNDS * NCAND + 1, S.same_expert, 1)
            total(ROUNDS * NCAND + 2, S.earlier_tile, 1)
            total(ROUNDS * NCAND + 3, S.earlier_tile, 1)
            pe.wait_ge(slots_ready, 1)
            pe.transpose(slot_ps, rank[:, :], S.ident).then_inc(slots_turned, 1)
            pe.wait_ge(slot_ready, 2)

            for e in range(E):
                if e % 2 == 0:
                    pe.wait_ge(rows_in[e // 2], 16)
                if e >= 2:
                    pe.wait_ge(x_copied, e - 1)
                for c in range(ST):
                    last = pe.transpose(t_ps[e % 2][:, blk(c, 128)], slot_rows[:, ST * e + c, 0:D], S.ident)
                last.then_inc(x_turned, 1)
            pe.wait_ge(x_copied, E)
            pe.wait_ge(h_rows, NB)

            def hidden(i, k):
                p = k % 2
                x = x_slots[:, :, :].rearrange("p e s -> p (e s)")[:, bass.ds(i * (2 * ST * 128) + k * (ST * 128), CAP)]
                pe.wait_ge(gu_in[p], i * 32 + 32 * (k // 2 + 1))
                for f in range(FC):
                    pe.wait_ge(gate_done, i * (2 * FC) + (FC * k + f + 1))
                    pe.matmul(g_ps[f % 2][:, 0:CAP], wg[p][:, blk(f, 128)], x, start=True, stop=True)
                    pe.matmul(u_ps[f % 2][:, 0:CAP], wu[p][:, blk(f, 128)], x, start=True, stop=True).then_inc(up_ready, 1)

            def back(i, p):
                pe.wait_ge(d_in[p], i * 16 + 16)
                pe.wait_ge(y_scaled, i * 2 + (p + 1))
                pe.wait_ge(gate_done, i * (2 * FC) + (FC * p + FC + 2))
                for c in range(ST):
                    n = min(128, CAP - 128 * c)
                    for f in range(FC):
                        last = pe.matmul(y_ps[p][0:n, blk(c, D)], gated[:, FC * p + f, 128 * c:128 * c + n], wd[p][:, f, :],
                                         start=(f == 0), stop=(f == FC - 1))
                last.then_inc(y_ready, 1)

            hidden(0, 0)
            with pe.Fori(0, E // 2 - 1) as i:
                hidden(i, 1)
                back(i, 0)
                hidden(i, 2)
                back(i, 1)
            last_pair = E // 2 - 1
            hidden(last_pair, 1)
            back(last_pair, 0)
            back(last_pair, 1)

            for b in range(NB):
                pe.wait_ge(S.y_in[b], 32)
                for u in range(4):
                    last = pe.transpose(four_ps[b][:, blk(u, 128)], y_tok[:, 4 * b + u, :], S.ident)
                last.then_inc(y_turned, 1)

        @block.scalar
        def _(act):
            ln_scalar(act, S, 3, var_ps)
            act.wait_ge(to_exp, 1)
            act.activation(R.p[:, :, :], R.p[:, :, :], ACT.Exp).then_inc(exped, 1)
            for b in range(NB):
                act.wait_ge(h_turned, b + 1)
                for k in range(2):
                    ins = act.activation(token_rows[:, blk(b, 4), k, 0:D],
                                         four_ps[b][:, :].rearrange("p (c d) -> p c d", d=D), ACT.Copy)
                    if k == 0:
                        ins.then_inc(h_first, 1)
                    else:
                        ins.then_inc(h_rows, 1)
            for e in range(E):
                act.wait_ge(x_turned, e + 1)
                act.activation(x_slots[:, e, :], t_ps[e % 2][:, 0:ST * 128], ACT.Copy).then_inc(x_copied, 1)
            with act.Fori(0, E // 2) as i:
                for n in range(2 * FC):
                    act.wait_ge(gate_done, i * (2 * FC) + (n + 1))
                    act.wait_ge(up_ready, i * (2 * FC) + (n + 1))
                    act.activation(act_g[:, n % 2, :], g_ps[n % 2][:, 0:CAP], ACT.Silu).then_inc(silu_done, 1)

        @block.vector
        def _(dve):
            link = make_link(dve, S)
            dve.memset(R.m[:, 0:1], 0.0).then_inc(gate_done, 2)
            dve.memset(R.m[:, 1:2], 0.0).then_inc(y_scaled, 2)
            dve.wait_ge(gate_done, 2)
            dve.wait_ge(y_scaled, 2)
            ln_vector(dve, S, link, 3, mean_ps, var_ps, S.mod[:, 6 + CB:7 + CB], S.mod[:, 6 + SB:7 + SB])
            dve.wait_ge(logits_done, 1)
            link(dve.tensor_copy(R.p[:, :, :], logits_ps.rearrange("p (t e) -> p t e", e=E)))
            top2_vector(dve, S, link, R, to_exp, exped)
            link(dve.tensor_tensor(R.rest[:, :, :], R.sel[:, :, :], R.hot[:, :, :], ALU.subtract))
            link(dve.tensor_tensor(R.m[:, :], R.top1[:, :], R.top2[:, :], ALU.add))
            link(dve.tensor_scalar(R.m[:, :], R.m[:, :], 1e-6, None, ALU.add))
            link(dve.reciprocal(R.m[:, :], R.m[:, :]))
            link(dve.tensor_tensor(R.p[:, :, :], R.p[:, :, :], R.m[:, :].unsqueeze(2).to_broadcast([128, NTILE, E]), ALU.mult))
            link(dve.tensor_tensor(R.p[:, :, :], R.p[:, :, :], R.sel[:, :, :], ALU.mult))
            link(dve.tensor_scalar(R.sel[:, :, :], R.sel[:, :, :], -1.0, None, ALU.add))
            dve.tensor_tensor(R.gate[:, :, :].rearrange("p e c -> p c e"), R.p[:, :, :], R.sel[:, :, :],
                              ALU.add).then_inc(weights_ready, 1)
            for k, top in enumerate((R.top1, R.top2)):
                dve.tensor_tensor(token_rows[:, :, k, D], top[:, :], R.m[:, :], ALU.mult).then_inc(tags_ready, 1)
                dve.wait_ge(rw_in, 32)
                dve.tensor_copy(token_rows[:, :, k, D + 1].bitcast(I32), token_id[:, :]).then_inc(tags_ready, 1)
            dve.wait_ge(turned, 1)
            link(dve.tensor_copy(w_t[:, :], turn_ps))
            link(dve.memset(thr[:, :], 0))
            link(dve.tensor_copy(cand[:, :], S.bits[:, 0:NCAND]))

            with dve.Fori(0, ROUNDS) as r:
                for j in range(NCAND):
                    dve.tensor_scalar(reach[:, j, :], w_t[:, :], cand[:, j:j + 1].bitcast(F32), None, ALU.is_ge, ALU.add,
                                      accum_out=count[:, j:j + 1]).then_inc(counted, 1)
                dve.tensor_tensor(next_cand[:, :], S.bits[:, bass.ds(r * NCAND + NCAND, NCAND)],
                                  thr[:, :].to_broadcast([128, NCAND]), ALU.bitwise_or).then_inc(tloop, 1)
                dve.wait_ge(totalled, r + 1)
                dve.tensor_scalar(reached[:, :], total_ps[:, 0:NCAND], float(CAP), None, ALU.is_ge, ALU.add,
                                  accum_out=step[:, :]).then_inc(tloop, 1)
                dve.wait_ge(tloop, r * 5 + 2)
                dve.tensor_scalar(bits[:, :], step[:, :], S.consts[:, bass.ds(r + 392, 1)], None, ALU.mult).then_inc(tloop, 1)
                dve.wait_ge(tloop, r * 5 + 3)
                dve.tensor_tensor(cand[:, :], next_cand[:, :], bits[:, :].to_broadcast([128, NCAND]), ALU.bitwise_or).then_inc(tloop, 1)
                dve.tensor_tensor(thr[:, :], thr[:, :], bits[:, :], ALU.bitwise_or).then_inc(tloop, 1)
                dve.wait_ge(tloop, r * 5 + 5)
            link(dve.tensor_scalar(hit[:, :], w_t[:, :], thr[:, :].bitcast(F32), None, ALU.is_gt))
            dve.tensor_scalar(tie[:, :], hit[:, :], 1.0, None, ALU.mult, ALU.add, accum_out=count[:, 0:1]).then_inc(counted, 1)
            dve.wait_ge(totalled, ROUNDS + 1)
            link(dve.tensor_scalar(need[:, :], total_ps[:, 0:1], -1.0, float(CAP), ALU.mult, ALU.add))
            link(dve.tensor_scalar(tie[:, :], w_t[:, :], thr[:, :].bitcast(F32), None, ALU.is_equal))
            link(dve.tensor_tensor_scan(rank[:, :], tie[:, :], tie[:, :], 0.0, ALU.add, ALU.max))
            dve.tensor_copy(count[:, 0:1], rank[:, 127:128]).then_inc(counted, 1)
            dve.wait_ge(totalled, ROUNDS + 2)
            link(dve.tensor_tensor(need[:, :], need[:, :], total_ps[:, 0:1], ALU.subtract))
            link(dve.tensor_scalar(rank[:, :], rank[:, :], need[:, :], None, ALU.is_le))
            link(dve.tensor_tensor(tie[:, :], tie[:, :], rank[:, :], ALU.mult))
            link(dve.tensor_tensor(hit[:, :], hit[:, :], tie[:, :], ALU.add))
            link(dve.tensor_tensor_scan(rank[:, :], hit[:, :], hit[:, :], 0.0, ALU.add, ALU.max))
            dve.tensor_copy(count[:, 0:1], rank[:, 127:128]).then_inc(counted, 1)
            dve.wait_ge(totalled, ROUNDS + 3)
            link(dve.tensor_tensor(need[:, :], slot_base, total_ps[:, 0:1], ALU.add))
            dve.scalar_tensor_tensor(rank[:, :], rank[:, :], need[:, :], hit[:, :], ALU.add, ALU.mult).then_inc(slots_ready, 1)
            dve.wait_ge(slots_turned, 1)
            for k, hot in enumerate((R.rest, R.hot)):
                link(dve.tensor_tensor(R.p[:, :, :], hot[:, :, :], slot_ps.rearrange("p (e c) -> p c e", e=E), ALU.mult))
                link(dve.tensor_reduce(slot_f[:, k, :], R.p[:, :, :], AX.X, ALU.add))
                dve.tensor_scalar(slot[:, k, :], slot_f[:, k, :], float(NO_SLOT), None, ALU.add).then_inc(slot_ready, 1)

            def gate(i, k):
                for f in range(FC):
                    n = FC * k + f
                    dve.wait_ge(silu_done, i * (2 * FC) + (n + 1))
                    dve.tensor_tensor(gated[:, n % (2 * FC), :], act_g[:, f % 2, :], u_ps[f % 2][:, 0:CAP],
                                      ALU.mult).then_inc(gate_done, 1)

            def scale(i, p, first):
                dve.wait_ge(y_ready, i * 2 + (p + 1))
                if not first:
                    dve.wait_ge(added, i * (2 * ST * 16) + ST * 16 * (p - 1))
                at = i * (2 * ST) + p * ST
                dve.tensor_copy(ids[p][:, :], slot_rows[:, bass.ds(at, ST), D + 1].bitcast(I32)).then_inc(scaled, 1)
                for c in range(ST):
                    n = min(128, CAP - 128 * c)
                    ins = dve.tensor_scalar(y_rows[p][0:n, c, :], y_ps[p][0:n, blk(c, D)],
                                            slot_rows[0:n, bass.ds(at + c, 1), D], None, ALU.mult)
                    ins.then_inc(y_scaled if c == ST - 1 else scaled, 1)

            gate(0, 0)
            gate(0, 1)
            scale(0, 0, True)
            gate(0, 2)
            scale(0, 1, True)
            with dve.Fori(1, E // 2 - 1) as i:
                gate(i, 1)
                scale(i, 0, False)
                gate(i, 2)
                scale(i, 1, False)
            gate(E // 2 - 1, 1)
            scale(E // 2 - 1, 0, False)
            scale(E // 2 - 1, 1, False)
            for b in range(NB):
                dve.wait_ge(y_turned, b + 1)
                dve.scalar_tensor_tensor(S.xT[:, blk(b)], four_ps[b][:, :], S.mod[:, 6 + GB:7 + GB], S.xT[:, blk(b)],
                                         ALU.mult, ALU.add).then_inc(S.x_ready, 1)

        @block.gpsimd
        def _(pool):
            pool.wait_ge(S.dram_init, 64)
            pool.wait_ge(tags_ready, 4)
            pool.wait_ge(h_first, NB)
            pool.wait_ge(h_rows, NB)
            for k in range(2):
                pool.wait_ge(slot_ready, k + 1)
                for t in range(NTILE):
                    pool.indirect_dma_start(A["slots"], bass.IndirectOffsetOnAxis(slot[:, k, t:t + 1], 0), token_rows[:, t, k, :], None,
                                            bounds_check=E * ST * 128 - 1, oob_is_err=False).then_inc(scattered, 16)

            with pool.Fori(0, E // 2) as i:
                for p in range(2):
                    early(pool, i * 2 + (p + 3))
                    early(pool, i * (2 * ST) + ST * (p + 1))
                    pool.wait_ge(S.dram_init, 64)
                    pool.wait_ge(y_scaled, i * 2 + (p + 3))
                    pool.wait_ge(scaled, i * (2 * ST) + ST * (p + 1))
                    for c in range(ST):
                        n = min(128, CAP - 128 * c)
                        pool.indirect_dma_start(A["y_sum"], bass.IndirectOffsetOnAxis(ids[p][0:n, c:c + 1], 0), y_rows[p][0:n, c, :], None,
                                                compute_op=ALU.add).then_inc(added, 16)
                    pool.wait_ge(added, i * (2 * ST * 16) + ST * 16 * (p + 1))



def build(nc, A):
    with ExitStack() as ctx:
        S = Shared()
        sb = lambda n, s, d=F32: ctx.enter_context(nc.sbuf_tensor(n, s, d))
        S.sem = lambda n: ctx.enter_context(nc.semaphore(n))
        S.xT = sb("xT_s", [128, NT])
        S.hT = sb("hT_s", [128, NT + 1])
        S.xc = sb("xc_s", [128, NT])
        S.sd = sb("sd_s", [128, NT])
        S.sq = sb("sq_s", [128, 2, TB])
        S.inv_sd = sb("inv_sd", [128, NTILE])
        S.cols = sb("cols_s", [128, 7])
        S.mod = sb("mod_s", [128, 12])
        S.eps_col = sb("eps_col", [128, 1])
        S.mean_w = sb("mean_w", [128, 128])
        S.consts = sb("consts_s", [128, A["consts"].shape[1]])
        S.ident = S.consts[:, 0:128]
        S.same_expert = S.consts[:, 128:256]
        S.earlier_tile = S.consts[:, 256:384]
        S.rev = S.consts[:, 384:392]
        at = 393 + ROUNDS
        S.earlier_expert, S.tile_sizes = S.consts[:, at:at + 128], S.consts[:, at + 128:at + 128 + E]
        at += 128 + E
        S.tile_numbers, S.row_number = S.consts[:, at:at + XT + XB], S.consts[:, at + XT + XB:at + XT + XB + 1]
        S.last_expert_row = S.consts[:, at + XT + XB + 1:at + XT + XB + 2]
        S.bits = sb("bits", [128, (ROUNDS + 1) * NCAND], I32)
        S.cols_in, S.const_in, S.ones_in, S.eps_set = S.sem("cols_in"), S.sem("const_in"), S.sem("ones_in"), S.sem("eps_set")
        S.dram_init = S.sem("dram_init")
        S.link_sem, S.linked = S.sem("link"), 0
        S.y_in = [S.sem(f"y_in{b}") for b in range(NB)]
        S.x_ready, S.h_ready = S.sem("x_ready"), S.sem("h_ready")
        S.ln_mean, S.ln_centered, S.ln_squared = S.sem("ln_mean"), S.sem("ln_centered"), S.sem("ln_squared")
        S.ln_var, S.ln_sd = S.sem("ln_var"), S.sem("ln_sd")
        S.ln_inverse, S.ln_spread = S.sem("ln_inverse"), S.sem("ln_spread")
        S.x_in = [S.sem(f"x_in{b}") for b in range(NB)]
        stage_mix(nc, S, A)
        S.kop = sb("kop", [128, H, NT], BF16)
        S.k_zeroed = S.sem("k_zeroed")
        stage_gelu_moe(nc, S, A)
        with ExitStack() as ctx34:
            sb34 = lambda n, s, d=F32: ctx34.enter_context(nc.sbuf_tensor(n, s, d))
            S.qop = sb34("qop", [128, H, NT], BF16)
            S.v_all = sb34("v_all", [128, NTILE, H, VW])
            S.ops_in_sw = [S.sem(f"ops_in_sw{b}") for b in range(NB)]
            S.ops_in, S.split = [S.sem(f"ops_in{b}") for b in range(NB)], S.sem("max_split")
            stage_qkv(nc, S, A)
            stage_attention(nc, S, A)
        stage_swiglu_moe(nc, S, A)


def kernel(**inputs):
    import numpy as np
    import ml_dtypes
    import concourse.bacc as _bacc
    from concourse.bass_utils import run_bass_kernel_spmd as _run

    g = {k: np.asarray(v) for k, v in inputs.items()}
    f32 = np.float32
    col = lambda n: g[n].reshape(D)
    cc = np.ascontiguousarray
    by_dim = lambda a: a.reshape(H, DK, *a.shape[1:]).swapaxes(0, 1).reshape(a.shape)
    part = np.arange(128)
    causal = np.zeros((128, TB), f32)
    causal[:, TB - 128:] = np.where(part[None, :] > part[:, None], -BIG, 0.0)
    consts = np.concatenate([
        np.eye(128, dtype=f32),
        (part[:, None] // 16 == part[None, :] // 16).astype(f32),
        ((part[:, None] // 16 == part[None, :] // 16) & (part[:, None] % 16 < part[None, :] % 16)).astype(f32),
        np.broadcast_to(np.arange(E, 0, -1).astype(f32), (128, E)),
        np.broadcast_to(2.0 ** np.arange(NBITS - ROUND_BITS, -1, -ROUND_BITS, dtype=f32), (128, ROUNDS)),
        (part[:, None] // 16 * ST * 128 - 1 - NO_SLOT).astype(f32),
        (part[:, None] // 16 < part[None, :] // 16).astype(f32) / 16,
        np.broadcast_to(XW * np.arange(E, dtype=f32), (128, E)),
        np.broadcast_to(np.arange(XT + XB, dtype=f32), (128, XT + XB)),
        part[:, None].astype(f32),
        (part[:, None] + (E - 1) * 128).astype(f32),
    ], axis=1)
    both = lambda n, m: np.concatenate([g[f"L0_ffn_{n}"], g[f"L0_ffn_{m}"]], axis=0)
    rows_of_experts = cc(np.concatenate([
        both("W1", "Ws1"),
        both("W2", "Ws2").reshape(E + 1, FC, 128, D).transpose(0, 2, 1, 3).reshape(E + 1, 128, FC * D),
        both("b1", "bs1").reshape(E + 1, FC, 128).transpose(0, 2, 1),
        np.broadcast_to(both("b2", "bs2")[:, None, :], (E + 1, 128, D)),
    ], axis=2).reshape((E + 1) * 128, WX))
    arrays = {
        "xT": cc(g["L0_attn_x"][0].T),
        "cols": cc(np.stack([col("L0_attn_time_decay"), col("L0_attn_time_first"), col("L0_attn_time_mix"),
                             col("L0_c"), col("L1_c"), by_dim(col("L1_attn_bq")), by_dim(col("L1_attn_bk"))], axis=1)),
        "wmod": cc(np.stack([g["L0_wmod"], g["L1_wmod"]], axis=1)),
        "wmix": cc(np.stack([g[f"L0_attn_W{n}"].T for n in "kvro"], axis=1)),
        "consts": consts,
        "causal": causal,
        "wqkv": cc(np.stack([by_dim(g["L1_attn_Wq"]).T, by_dim(g["L1_attn_Wk"]).T, g["L1_attn_Wv"].T], axis=1)),
        "bv": g["L1_attn_bv"].reshape(1, D),
        "wg0": g["L0_ffn_Wg"],
        "bg0": g["L0_ffn_bg"].reshape(1, E),
        "wx0": rows_of_experts,
        "bs2": g["L0_ffn_bs2"],
        "wr1": cc(g["L1_ffn_router_w"].T),
        "wg_1": g["L1_ffn_wg"],
        "wu_1": g["L1_ffn_wu"],
        "wd_1": cc(g["L1_ffn_wd"].reshape(E, FC, 128, D).transpose(0, 2, 1, 3).reshape(E, 128, FC * D)),
    }
    nc = _bacc.Bacc("TRN2", target_bir_lowering=False, num_devices=1)
    A = {n: nc.dram_tensor(f"in_{n}", a.shape, F32, kind="ExternalInput").ap() for n, a in arrays.items()}
    one_rows = np.ones((3, H, NT), ml_dtypes.bfloat16)
    arrays["one_rows"] = one_rows
    round_bits = np.arange(1, NCAND + 1)[None, :] << np.arange(NBITS - ROUND_BITS, -1, -ROUND_BITS)[:, None]
    int_arrays = {
        "bits": np.broadcast_to(np.append(round_bits.reshape(-1), [0] * NCAND).astype(np.int32), (128, (ROUNDS + 1) * NCAND)),
        "token_id": part[:, None] + 128 * np.arange(NTILE)[None, :],
        "empty_slots": np.where(np.arange(ROW)[None, :] == ROW - 1, NT + np.arange(ST * 128)[:, None], 0),
    }
    for n, a in int_arrays.items():
        arrays[n] = cc(a.astype(np.int32))
        A[n] = nc.dram_tensor(f"in_{n}", a.shape, I32, kind="ExternalInput").ap()
    arrays["causal_t"] = cc(np.stack([np.eye(128), np.where(part[None, :] < part[:, None], -BIG, 0.0)], axis=1)
                            .astype(ml_dtypes.bfloat16))
    A["causal_t"] = nc.dram_tensor("in_causal_t", (128, 2, 128), BF16, kind="ExternalInput").ap()
    A["one_rows"] = nc.dram_tensor("in_one_rows", one_rows.shape, BF16, kind="ExternalInput").ap()
    A["slots0"] = nc.dram_tensor("slots0", (XT * XW, ROW), F32, kind="Internal").ap()
    A["y_sum0"] = nc.dram_tensor("y_sum0", (NT + ST * 128, D), F32, kind="Internal").ap()
    A["qk_parts"] = nc.dram_tensor("qk_parts", (2, 3, DK, H, NT), BF16, kind="Internal").ap()
    A["max_rows"] = nc.dram_tensor("max_rows", (NB, 3, H, TB), BF16, kind="Internal").ap()
    A["attn_sums"] = nc.dram_tensor("attn_sums", (H, VW, NT), F32, kind="Internal").ap()
    A["slots"] = nc.dram_tensor("slots", (E * ST * 128, ROW), F32, kind="Internal").ap()
    A["y_sum"] = nc.dram_tensor("y_sum", (NT + ST * 128, D), F32, kind="Internal").ap()
    A["out"] = nc.dram_tensor("out", (D, NT), F32, kind="ExternalOutput").ap()
    build(nc, A)
    r = _run(nc, [{f"in_{n}": a for n, a in arrays.items()}], core_ids=[0])
    return cc(r.results[0]["out"].T).reshape(1, NT, D)
```
